# Optimizing a Trainium2 kernel written in Bass

```python
import numpy as np
import jax
import jax.numpy as jnp

def _softmax(x, axis=-1):
    return jax.nn.softmax(x, axis=axis)

def _gelu(x):
    return jax.nn.gelu(x, approximate=True)

def _silu(x):
    return jax.nn.silu(x)

def _sigmoid(x):
    return jax.nn.sigmoid(x)

def _layernorm(x, axis=-1, eps=1e-05):
    m = jnp.mean(x, axis=axis, keepdims=True)
    v = jnp.var(x, axis=axis, keepdims=True)
    return (x - m) / jnp.sqrt(v + eps)

def _scatter_add(tgt, idx, src, axis=0):
    return tgt.at[idx].add(src)

def _segment_sum(src, seg, n):
    return jax.ops.segment_sum(src, seg, n)
kernel_name = 'mk_gnn_resnorm_d4_gnn_r64_809bf7'

def setup_inputs(seed: int=0):
    np.random.seed(seed)
    _w = jnp.asarray

    def _rec_inputs():
        import jax
        import jax.numpy as jnp
        _gk = jax.random.key(seed)
        x = -0.000202 + 1 * jax.random.normal(jax.random.fold_in(_gk, 1), (100000, 64), jnp.float32)
        src = jax.random.randint(jax.random.fold_in(_gk, 2), (25000,), 0, 100000, jnp.int32)
        dst = jax.random.randint(jax.random.fold_in(_gk, 3), (25000,), 0, 100000, jnp.int32)
        _o = jnp.argsort(dst, stable=True)
        src = src[_o]
        dst = dst[_o]
        edge_attr_32 = 0.000189758 + 1.00013 * jax.random.normal(jax.random.fold_in(_gk, 12), (25000, 32), jnp.float32)
        node_vec = jax.random.uniform(jax.random.fold_in(_gk, 14), (100000,), jnp.float32, 0.0, 0.999994)
        return (x, src, dst, edge_attr_32, node_vec)
    x, src, dst, edge_attr_32, node_vec = _rec_inputs()

    def _L0_gnn_setup():
        import jax, jax.numpy as jnp
        import numpy as np
        N = 100000
        E = 25000
        H = 64
        ED = 32
        LN_EPS = 1e-05

        def _mlp(h, w1, b1, w2, b2):
            return jax.nn.relu(h @ w1 + b1) @ w2 + b2
        key = jax.random.key(seed)
        ks = jax.random.split(key, 12)
        block_in = 2 * H + ED
        inp = {'x': jax.random.normal(ks[0], (N, H), dtype=jnp.float32), 'edge_index': jax.random.randint(ks[1], (2, E), 0, N, dtype=jnp.int64), 'edge_attr': jax.random.normal(ks[2], (E, ED), dtype=jnp.float32), 'msg_w1': jax.random.normal(ks[3], (block_in, H), dtype=jnp.float32) / np.sqrt(block_in), 'msg_b1': jnp.zeros((H,), dtype=jnp.float32), 'msg_w2': jax.random.normal(ks[4], (H, H), dtype=jnp.float32) / np.sqrt(H), 'msg_b2': jnp.zeros((H,), dtype=jnp.float32), 'upd_w1': jax.random.normal(ks[5], (2 * H, H), dtype=jnp.float32) / np.sqrt(2 * H), 'upd_b1': jnp.zeros((H,), dtype=jnp.float32), 'upd_w2': jax.random.normal(ks[6], (H, H), dtype=jnp.float32) / np.sqrt(H), 'upd_b2': jnp.zeros((H,), dtype=jnp.float32), 'ln_g': jnp.ones((H,), dtype=jnp.float32), 'ln_b': jnp.zeros((H,), dtype=jnp.float32)}
        return inp
    _L0_gnn_all = _L0_gnn_setup()
    _L0_gnn_in = {k: v for k, v in _L0_gnn_all.items() if k in ('msg_w1', 'msg_b1', 'msg_w2', 'msg_b2', 'upd_w1', 'upd_b1', 'upd_w2', 'upd_b2', 'ln_g', 'ln_b')}
    del _L0_gnn_all

    def _L1_gnn_setup():
        import jax, jax.numpy as jnp
        import numpy as np
        N = 50000
        E = 12500
        IN = 64
        H = 4
        D = 16
        OH = H * D
        SCALE = float(np.sqrt(IN))
        LN_EPS = 1e-05
        key = jax.random.key(seed)
        ks = jax.random.split(key, 16)
        w = 0.05
        return {'feats': jax.random.normal(ks[0], (N, IN), jnp.float32), 'Wq': jax.random.normal(ks[1], (IN, OH), jnp.float32) * w, 'bq': jnp.zeros((OH,), jnp.float32), 'Wk': jax.random.normal(ks[2], (IN, OH), jnp.float32) * w, 'bk': jnp.zeros((OH,), jnp.float32), 'Wv': jax.random.normal(ks[3], (IN, OH), jnp.float32) * w, 'bv': jnp.zeros((OH,), jnp.float32), 'Wo': jax.random.normal(ks[4], (OH, OH), jnp.float32) * w, 'bo': jnp.zeros((OH,), jnp.float32), 'Wf': jax.random.normal(ks[5], (IN, OH), jnp.float32) * w, 'bf': jnp.zeros((OH,), jnp.float32), 'gamma': jnp.ones((OH,), jnp.float32), 'beta': jnp.zeros((OH,), jnp.float32), 'src': jax.random.randint(ks[6], (E,), 0, N, jnp.int32), 'dst': jax.random.randint(ks[7], (E,), 0, N, jnp.int32)}
    _L1_gnn_all = _L1_gnn_setup()
    _L1_gnn_in = {k: v for k, v in _L1_gnn_all.items() if k in ('Wq', 'bq', 'Wk', 'bk', 'Wv', 'bv', 'Wo', 'bo', 'Wf', 'bf', 'gamma', 'beta')}
    del _L1_gnn_all

    def _L2_gnn_setup():
        import jax, jax.numpy as jnp
        import numpy as np
        N_NODES = 50000
        key = jax.random.key(seed)
        k1, k2 = jax.random.split(key)
        edge_index = jax.random.randint(k1, (2, 12500), 0, N_NODES, dtype=jnp.int64)
        x = jax.random.normal(k2, (N_NODES, 64), dtype=jnp.float32)
        return {'edge_index': edge_index, 'x': x}
    _L2_gnn_all = _L2_gnn_setup()
    _L2_gnn_in = {k: v for k, v in _L2_gnn_all.items() if k in ()}
    del _L2_gnn_all

    def _L3_gnn_setup():
        import jax, jax.numpy as jnp
        import numpy as np
        N_NODES = 100000
        N_EDGES = 25000
        IN_FEATS = 64
        N_HIDDEN = 64
        OUT_FEATS = 64

        def _graph_conv(h, norm, src, dst, W, b, activation):
            h = h * norm[:, None]
            h = h @ W
            msgs = jnp.take(h, src, axis=0)
            agg = jax.ops.segment_sum(msgs, dst, num_segments=N_NODES)
            h = agg * norm[:, None] + b
            return jax.nn.relu(h) if activation else h
        key = jax.random.key(seed)
        ks = jax.random.split(key, 12)
        feat = jax.random.normal(ks[0], (N_NODES, IN_FEATS), dtype=jnp.float32)
        norm_data = jax.random.uniform(ks[1], (N_NODES,), dtype=jnp.float32, minval=0.1, maxval=1.0)
        src = jax.random.randint(ks[2], (N_EDGES,), 0, N_NODES)
        dst = jax.random.randint(ks[3], (N_EDGES,), 0, N_NODES)
        s = 0.05
        return {'feat': feat, 'norm_data': norm_data, 'src': src, 'dst': dst, 'W0': jax.random.normal(ks[4], (IN_FEATS, N_HIDDEN), dtype=jnp.float32) * s, 'b0': jnp.zeros((N_HIDDEN,), dtype=jnp.float32), 'W1': jax.random.normal(ks[5], (N_HIDDEN, N_HIDDEN), dtype=jnp.float32) * s, 'b1': jnp.zeros((N_HIDDEN,), dtype=jnp.float32), 'W2': jax.random.normal(ks[6], (N_HIDDEN, OUT_FEATS), dtype=jnp.float32) * s, 'b2': jnp.zeros((OUT_FEATS,), dtype=jnp.float32)}
    _L3_gnn_all = _L3_gnn_setup()
    _L3_gnn_in = {k: v for k, v in _L3_gnn_all.items() if k in ('W0', 'b0', 'W1', 'b1', 'W2', 'b2')}
    del _L3_gnn_all
    return {'x': x, 'src': src, 'dst': dst, 'edge_attr_32': edge_attr_32, 'node_vec': node_vec, 'L0_gnn_msg_w1': _L0_gnn_in['msg_w1'], 'L0_gnn_msg_b1': _L0_gnn_in['msg_b1'], 'L0_gnn_msg_w2': _L0_gnn_in['msg_w2'], 'L0_gnn_msg_b2': _L0_gnn_in['msg_b2'], 'L0_gnn_upd_w1': _L0_gnn_in['upd_w1'], 'L0_gnn_upd_b1': _L0_gnn_in['upd_b1'], 'L0_gnn_upd_w2': _L0_gnn_in['upd_w2'], 'L0_gnn_upd_b2': _L0_gnn_in['upd_b2'], 'L0_gnn_ln_g': _L0_gnn_in['ln_g'], 'L0_gnn_ln_b': _L0_gnn_in['ln_b'], 'L1_gnn_Wq': _L1_gnn_in['Wq'], 'L1_gnn_bq': _L1_gnn_in['bq'], 'L1_gnn_Wk': _L1_gnn_in['Wk'], 'L1_gnn_bk': _L1_gnn_in['bk'], 'L1_gnn_Wv': _L1_gnn_in['Wv'], 'L1_gnn_bv': _L1_gnn_in['bv'], 'L1_gnn_Wo': _L1_gnn_in['Wo'], 'L1_gnn_bo': _L1_gnn_in['bo'], 'L1_gnn_Wf': _L1_gnn_in['Wf'], 'L1_gnn_bf': _L1_gnn_in['bf'], 'L1_gnn_gamma': _L1_gnn_in['gamma'], 'L1_gnn_beta': _L1_gnn_in['beta'], 'L3_gnn_W0': _L3_gnn_in['W0'], 'L3_gnn_b0': _L3_gnn_in['b0'], 'L3_gnn_W1': _L3_gnn_in['W1'], 'L3_gnn_b1': _L3_gnn_in['b1'], 'L3_gnn_W2': _L3_gnn_in['W2'], 'L3_gnn_b2': _L3_gnn_in['b2']}

def reference(x, src, dst, edge_attr_32, node_vec, L0_gnn_msg_w1, L0_gnn_msg_b1, L0_gnn_msg_w2, L0_gnn_msg_b2, L0_gnn_upd_w1, L0_gnn_upd_b1, L0_gnn_upd_w2, L0_gnn_upd_b2, L0_gnn_ln_g, L0_gnn_ln_b, L1_gnn_Wq, L1_gnn_bq, L1_gnn_Wk, L1_gnn_bk, L1_gnn_Wv, L1_gnn_bv, L1_gnn_Wo, L1_gnn_bo, L1_gnn_Wf, L1_gnn_bf, L1_gnn_gamma, L1_gnn_beta, L3_gnn_W0, L3_gnn_b0, L3_gnn_W1, L3_gnn_b1, L3_gnn_W2, L3_gnn_b2):
    import jax
    import jax.numpy as jnp

    def _L0_gnn_ref(x, edge_index, edge_attr, msg_w1, msg_b1, msg_w2, msg_b2, upd_w1, upd_b1, upd_w2, upd_b2, ln_g, ln_b):
        import jax, jax.numpy as jnp
        import numpy as np
        N = 100000
        E = 25000
        H = 64
        ED = 32
        LN_EPS = 1e-05

        def _mlp(h, w1, b1, w2, b2):
            return jax.nn.relu(h @ w1 + b1) @ w2 + b2
        src, dst = (edge_index[0], edge_index[1])
        msg_in = jnp.concatenate([x[src], x[dst], edge_attr], axis=-1)
        messages = _mlp(msg_in, msg_w1, msg_b1, msg_w2, msg_b2)
        agg = jax.ops.segment_sum(messages, dst, num_segments=N)
        out = _mlp(jnp.concatenate([x, agg], axis=-1), upd_w1, upd_b1, upd_w2, upd_b2)
        h = x + jax.nn.silu(out)
        mu = jnp.mean(h, axis=-1, keepdims=True)
        var = jnp.var(h, axis=-1, keepdims=True)
        return (h - mu) * jax.lax.rsqrt(var + LN_EPS) * ln_g + ln_b

    def _L1_gnn_ref(feats, Wq, bq, Wk, bk, Wv, bv, Wo, bo, Wf, bf, gamma, beta, src, dst):
        import jax, jax.numpy as jnp
        import numpy as np
        N = 50000
        E = 12500
        IN = 64
        H = 4
        D = 16
        OH = H * D
        SCALE = float(np.sqrt(IN))
        LN_EPS = 1e-05
        n = feats.shape[0]
        q = (feats @ Wq + bq).reshape(n, H, D)
        k = (feats @ Wk + bk).reshape(n, H, D)
        v = (feats @ Wv + bv).reshape(n, H, D)
        score = jnp.sum(k[src] * q[dst], axis=-1)
        score = jnp.exp(jnp.clip(score / SCALE, -5.0, 5.0))
        wv = jax.ops.segment_sum(v[src] * score[..., None], dst, num_segments=n)
        z = jax.ops.segment_sum(score, dst, num_segments=n)
        wv = wv / (z[..., None] + 1.0)
        o = wv.reshape(n, OH) @ Wo + bo
        h = feats @ Wf + bf + o
        mu = jnp.mean(h, axis=-1, keepdims=True)
        var = jnp.var(h, axis=-1, keepdims=True)
        ln = (h - mu) * jax.lax.rsqrt(var + LN_EPS) * gamma + beta
        return h + ln

    def _L2_gnn_ref(edge_index, x):
        import jax, jax.numpy as jnp
        import numpy as np
        N_NODES = 50000
        msgs = x[edge_index[1]]
        out = jax.ops.segment_sum(msgs, edge_index[0], num_segments=x.shape[0])
        return out

    def _L3_gnn_ref(feat, norm_data, src, dst, W0, b0, W1, b1, W2, b2):
        import jax, jax.numpy as jnp
        import numpy as np
        N_NODES = 100000
        N_EDGES = 25000
        IN_FEATS = 64
        N_HIDDEN = 64
        OUT_FEATS = 64

        def _graph_conv(h, norm, src, dst, W, b, activation):
            h = h * norm[:, None]
            h = h @ W
            msgs = jnp.take(h, src, axis=0)
            agg = jax.ops.segment_sum(msgs, dst, num_segments=N_NODES)
            h = agg * norm[:, None] + b
            return jax.nn.relu(h) if activation else h
        h = _graph_conv(feat, norm_data, src, dst, W0, b0, True)
        h = _graph_conv(h, norm_data, src, dst, W1, b1, True)
        h = _graph_conv(h, norm_data, src, dst, W2, b2, False)
        return h
    edge_index = jnp.stack([src, dst])
    x = _layernorm(x + _L0_gnn_ref(x, edge_index, edge_attr_32, L0_gnn_msg_w1, L0_gnn_msg_b1, L0_gnn_msg_w2, L0_gnn_msg_b2, L0_gnn_upd_w1, L0_gnn_upd_b1, L0_gnn_upd_w2, L0_gnn_upd_b2, L0_gnn_ln_g, L0_gnn_ln_b), axis=-1)
    x = _layernorm(x + _L1_gnn_ref(x, L1_gnn_Wq, L1_gnn_bq, L1_gnn_Wk, L1_gnn_bk, L1_gnn_Wv, L1_gnn_bv, L1_gnn_Wo, L1_gnn_bo, L1_gnn_Wf, L1_gnn_bf, L1_gnn_gamma, L1_gnn_beta, src, dst), axis=-1)
    x = _layernorm(x + _L2_gnn_ref(edge_index, x), axis=-1)
    x = _layernorm(x + _L3_gnn_ref(x, node_vec, src, dst, L3_gnn_W0, L3_gnn_b0, L3_gnn_W1, L3_gnn_b1, L3_gnn_W2, L3_gnn_b2), axis=-1)
    return x

_drawn_inputs = setup_inputs


def setup_inputs(seed=0):
    import zlib

    import numpy as np

    out = dict(_drawn_inputs(seed))
    spreads = {'L0_gnn_msg_b1': (0.0, 2.0),
     'L0_gnn_msg_b2': (0.0, 0.8),
     'L0_gnn_upd_b1': (0.0, 0.409),
     'L0_gnn_upd_b2': (0.0, 0.1),
     'L0_gnn_ln_g': (1.0, 0.2),
     'L0_gnn_ln_b': (0.0, 0.1),
     'L1_gnn_bq': (0.0, 2.0),
     'L1_gnn_bk': (0.0, 2.0),
     'L1_gnn_bv': (0.0, 0.338),
     'L1_gnn_bo': (0.0, 0.1),
     'L1_gnn_bf': (0.0, 0.1),
     'L1_gnn_gamma': (1.0, 0.2),
     'L1_gnn_beta': (0.0, 0.1),
     'L3_gnn_b0': (0.0, 0.8),
     'L3_gnn_b1': (0.0, 0.8),
     'L3_gnn_b2': (0.0, 0.1)}
    factors = {'node_vec': 8.0,
     'L1_gnn_Wq': 8.0,
     'L1_gnn_Wk': 8.0,
     'L3_gnn_W0': 8.0,
     'L3_gnn_W1': 8.0,
     'L3_gnn_W2': 8.0,
     'edge_attr_32': 3.98}
    for name, (base, spread) in spreads.items():
        noise = np.random.default_rng([zlib.crc32(name.encode()), seed]).standard_normal(out[name].shape)
        drawn = base * np.exp(spread * noise) if base else spread * noise
        out[name] = jnp.asarray(drawn.astype(out[name].dtype))
    for name, factor in factors.items():
        out[name] = (out[name] * factor).astype(out[name].dtype)
    return out
```

```python
import concourse.bass as bass
from concourse import mybir
from contextlib import ExitStack
import itertools

F32 = mybir.dt.float32
I32 = mybir.dt.int32
ALU = mybir.AluOpType
ACT = mybir.ActivationFunctionType
AX = mybir.AxisListType

N = 100000
E = 25000
H = 64
ED = 32
HEADS = 4
HD = H // HEADS
EPS = 1e-5
P = 128

SW = 256
SLOTS = P * SW
LOGS = 15
LOGW = 8
IDB = 15
HALF = N // 2
PADKEY = 115000
FAR = float(1 << 20)

CT = 4
STEPS = 50
TILES = STEPS * CT
CW = CT * P
ROWS = STEPS * CW

NP = 125
NPP = N // NP
G = NPP // STEPS
DW = G * H
QN = 4
QW = (G // QN) * NP


def steps(eng, peeled=2):
    for it in range(peeled):
        yield it, it % 2, it // 2
    with eng.Fori(0, (STEPS - peeled) // 2) as i:
        yield i * 2 + peeled, 0, i + peeled // 2
        yield i * 2 + (peeled + 1), 1, i + peeled // 2


def wake(eng, sem, value, woke):
    eng.wait_ge(sem, value)
    eng.sem_inc(woke, 1)


class Chain:

    def __init__(self, eng, sem, links=0):
        self.eng, self.sem, self.links, self.step, self.n = eng, sem, links, 0, 0

    def start(self, step):
        assert self.n in (0, self.links), (self.n, self.links)
        self.step, self.n = step, 0

    def __call__(self, ins):
        self.n += 1
        ins.then_inc(self.sem, 1)
        self.eng.wait_ge(self.sem, self.step * self.links + self.n)


SCOPES = itertools.count()


def scope(nc, ctx):
    n = next(SCOPES)
    used = []

    def sem(name):
        used.append(nc.alloc_semaphore(f"{name}_{n}"))
        return used[-1]

    def clear():
        if used:
            nc.clear_and_free_semaphores(used)
            nc.all_engine_barrier()

    ctx.callback(clear)
    sb = lambda name, shape, dt=F32: ctx.enter_context(nc.sbuf_tensor(f"{name}_{n}", shape, dt))
    ps = lambda name, shape: ctx.enter_context(nc.psum_tensor(f"{name}_{n}", shape, F32))
    return sb, ps, sem


def rows_of(table):
    return table.rearrange("(p n) h -> p (n h)", p=NP)


def halves(table):
    return table.rearrange("n (two h) -> (n two) h", two=2)


def over_tiles(col, width, n):
    return col.unsqueeze(2).to_broadcast([col.shape[0], n, width])


def over_rows(vec, parts, n):
    return vec[0:parts, :].unsqueeze(1).to_broadcast([parts, n, H])


def tiled(ap, n):
    return ap.rearrange("p (n h) -> p n h", n=n)


def fill_table(eng, table, tile, sem):
    w = tile.shape[1]
    with eng.Fori(0, NPP * H // w) as i:
        eng.dma_start(rows_of(table)[:, bass.ds(i * w, w)], tile[0:NP, :]).then_inc(sem, 16)


def load_constants(nc, g):
    with ExitStack() as ctx:
        sb, ps, sem = scope(nc, ctx)
        loaded = sem("constants_loaded")
        zeroed = sem("weights_zeroed")
        block = ctx.enter_context(nc.Block())
        a = g["in"]
        plain = [("ident", "eye", P, H * 2), ("signs", "signs", P, LOGS * SW)]

        @block.vector
        def _(dve):
            dve.memset(g["wk"][:, :], 0.0)
            dve.memset(g["wv"][:, :], 0.0)
            dve.memset(g["wq"][:, :], 0.0).then_inc(zeroed, 1)

        @block.sync
        def _(sp):
            n = [0]

            def load(dst, src):
                n[0] += 16
                sp.dma_start(dst, src).then_inc(loaded, 16)

            load(g["ident"][:, :], a["eye"])
            load(g["w_msg1"][:, :], a["L0_gnn_msg_w1"][0:2 * H, :])
            load(g["w_msg1e"][:, :], a["L0_gnn_msg_w1"][2 * H:2 * H + ED, :])
            load(g["w_msg2"][:, :], a["L0_gnn_msg_w2"])
            load(g["w_upd1"][:, :], a["L0_gnn_upd_w1"])
            load(g["w_upd2"][0:H, :], a["L0_gnn_upd_w2"])
            load(g["w_upd2"][H:H + 1, :], a["L0_gnn_upd_b2"].rearrange("(a h) -> a h", a=1))
            load(g["w_out"][0:H, :], a["L1_gnn_Wf"])
            load(g["w_out"][H:2 * H, :], a["L1_gnn_Wo"])
            for k in range(3):
                load(g[f"w_conv{k}"][:, :], a[f"L3_gnn_W{k}"])
            load(g["head_sum"][:, :], a["head_sum"])
            for col, name in (("b_msg1", "L0_gnn_msg_b1"), ("b_msg2", "L0_gnn_msg_b2"), ("b_upd1", "L0_gnn_upd_b1"),
                              ("b_q", "L1_gnn_bq"), ("b_k", "L1_gnn_bk"), ("b_v", "L1_gnn_bv")):
                load(g[col][:, :], a[name].rearrange("(h a) -> h a", a=1))
            for row, name in (("r_g", "L0_gnn_ln_g"), ("r_b", "L0_gnn_ln_b"), ("r_gamma", "L1_gnn_gamma"),
                              ("r_beta", "L1_gnn_beta"), ("r_bf", "L1_gnn_bf"), ("r_bo", "L1_gnn_bo"),
                              ("r_c0", "L3_gnn_b0"), ("r_c1", "L3_gnn_b1"), ("r_c2", "L3_gnn_b2")):
                load(g[row][:, :], a[name].partition_broadcast(P))
            sp.wait_ge(zeroed, 1)
            load(g["wk"][0:H, :], a["L1_gnn_Wk"])
            load(g["wv"][0:H, :], a["L1_gnn_Wv"])
            load(g["wq"][H:2 * H, :], a["L1_gnn_Wq"])
            sp.wait_ge(loaded, n[0])


def sort_edges(nc, g):
    with ExitStack() as ctx:
        sb, ps, sem = scope(nc, ctx)
        keys = sb("keys", [P, 2, SW], I32)
        ids = sb("ids", [P, 2, SW], I32)
        tmp = sb("tmp", [P, 2, SW], I32)
        tmp2 = sb("tmp2", [P, 2, SW], I32)
        tmp3 = sb("tmp3", [P, 2, SW], I32)
        nxt = sb("nxt", [P, 2, SW], I32)
        same = sb("same", [P, 2, SW])
        flt = sb("flt", [P, 2, 3, SW])
        bufs = (sb("bufA", [P, 2 * SW]), sb("bufB", [P, 2 * SW]))
        signs = sb("signs", [P, LOGS, SW])
        zero1 = sb("zero1", [1, 8], I32)
        EPP = E // NP
        record = sb("record", [NP, EPP, ED + 1], I32)
        srcs = sb("srcs", [NP, EPP], I32)
        none = sb("none", [NP, NPP], I32)
        x_in = sb("x_in", [NP, 2, DW])
        pair = sb("pair", [NP, 2, G, 2 * H])
        ident = g["ident"]
        pT = ps("pT", [P, 2 * SW])
        pU = [ps(f"pU{n}", [P, SW]) for n in range(5)]
        s_pad, s_keys, s_ids, s_const = sem("keys_padded"), sem("keys_loaded"), sem("ids_ready"), sem("signs_loaded")
        s_dve, s_turn, s_turned, s_words = sem("dve_step"), sem("turn_ready"), sem("turned"), sem("words_stored")
        s_zero, s_next, s_same, s_keep = sem("zero_ready"), sem("next_loaded"), sem("same_ready"), sem("keep_stored")
        s_flt, s_cols, s_wr, s_out = sem("floats_ready"), sem("columns_turned"), sem("words_ready"), sem("columns_kept")
        w_pool = sem("pool_woke")
        s_rec, s_recs, s_joined, s_fill, s_filled = (sem("record_loaded"), sem("record_stored"), sem("record_joined"),
                                                     sem("fill_ready"), sem("filled"))
        s_nofl, s_xcopy, w_act = sem("none_stored"), sem("x_copied"), sem("act_woke")
        x_loaded = [sem("x_loaded_even"), sem("x_loaded_odd")]
        pair_out = [sem("pair_stored_even"), sem("pair_stored_odd")]
        block = ctx.enter_context(nc.Block())
        OUTS = (("edge_id", 0, 0), ("scat_dst", 0, 1), ("dst_id", 0, 2), ("edge_id2", 1, 0), ("scat_src", 1, 1))

        @block.sync
        def _(sp):
            sp.wait_ge(s_pad, 1)
            full = E // SW
            for q, name in enumerate(("dst", "src")):
                k = g["in"][name]
                sp.dma_start(keys[0:full, q, :], k[0:full * SW, :].rearrange("(p f) a -> p (f a)", f=SW)).then_inc(s_keys, 16)
                sp.dma_start(keys[full:full + 1, q, 0:E - full * SW],
                             k[full * SW:E, :].rearrange("(p f) a -> p (f a)", p=1)).then_inc(s_keys, 16)
            sp.dma_start(signs[:, :, :], g["in"]["signs"].rearrange("p (k f) -> p k f", k=LOGS)).then_inc(s_const, 16)
            sp.dma_start(record[:, :, 0:ED], g["in"]["edge_attr_32"].bitcast(I32).rearrange("(p e) f -> p e f", p=NP)).then_inc(s_rec, 16)
            sp.dma_start(srcs[:, :], g["in"]["src"].rearrange("(p e) a -> p (e a)", p=NP)).then_inc(s_rec, 16)
            sp.wait_ge(s_zero, 1)
            for q in range(2):
                sp.dma_start(g["words"][q:q + 1, SLOTS:SLOTS + 8], zero1[0:1, :]).then_inc(s_words, 16)
                sp.dma_start(g["keep"][q:q + 1, 0:1], zero1[0:1, 0:1].bitcast(F32)).then_inc(s_keep, 16)
            sp.wait_ge(s_joined, 1)
            sp.dma_start(g["records"].rearrange("(p e) f -> p (e f)", p=NP), record[:, :, :].rearrange("p e f -> p (e f)")).then_inc(s_recs, 16)
            sp.wait_ge(s_wr, 1)
            for q in range(2):
                sp.dma_start(g["words"][q, 0:SLOTS].rearrange("(p f) -> p f", f=SW),
                             bufs[0][:, q * SW:(q + 1) * SW].bitcast(I32)).then_inc(s_words, 16)
            sp.wait_ge(s_words, 64)
            for q in range(2):
                sp.dma_start(nxt[:, q, :], g["words"][q, 1:SLOTS + 1].rearrange("(p f) -> p f", f=SW)).then_inc(s_next, 16)
            sp.wait_ge(s_same, 1)
            for q in range(2):
                sp.dma_start(g["keep"][q, 1:SLOTS + 1].rearrange("(p f) -> p f", f=SW), same[:, q, :]).then_inc(s_keep, 16)
            sp.wait_ge(s_recs, 16)
            sp.wait_ge(s_keep, 64)

        @block.scalar
        def _(act):
            act.wait_ge(s_fill, 1)
            act.dma_start(g["edge_row"].rearrange("(p n) a -> p (n a)", p=NP), none[:, :]).then_inc(s_nofl, 16)
            for it, b, k in steps(act):
                wake(act, x_loaded[b], (k + 1) * 16, w_act)
                if not first(it, 2):
                    wake(act, pair_out[b], k * 16, w_act)
                act.activation(pair[:, b, :, 0:H], tiled(x_in[:, b, :], G), ACT.Copy).then_inc(s_xcopy, 1)
                act.wait_ge(s_xcopy, it + 1)
                act.dma_start(rows_of(g["XA0"])[:, bass.ds(it * (2 * DW), 2 * DW)], pair[:, b, :, :].rearrange("p n h -> p (n h)")).then_inc(pair_out[b], 16)
            for b in range(2):
                act.wait_ge(pair_out[b], 16 * STEPS // 2)
            act.wait_ge(s_nofl, 16)

        @block.gpsimd
        def _(pool):
            pool.memset(pair[:, :, :, H:2 * H], 0.0)
            pool.memset(none[:, :], ROWS).then_inc(s_fill, 1)
            for q in range(2):
                pool.iota(ids[:, q, :], pattern=[[1, SW]], base=0, channel_multiplier=SW).then_inc(s_ids, 1)
            pool.iota(g["slot_row"][:, :].rearrange("p (c t) -> p c t", t=CT), pattern=[[CW, STEPS], [1, CT]], base=0, channel_multiplier=CT)
            pool.wait_ge(s_rec, 32)
            pool.tensor_copy(record[:, :, ED:ED + 1], srcs[:, :].unsqueeze(2)).then_inc(s_joined, 1)
            for it, b, k in steps(pool):
                if not first(it, 2):
                    wake(pool, s_xcopy, it - 1, w_pool)
                pool.dma_start(x_in[:, b, :], rows_of(g["in"]["x"])[:, bass.ds(it * DW, DW)]).then_inc(x_loaded[b], 16)

        TURNS, at = [], 0
        for k in range(1, LOGS + 1):
            at += 1
            if k > LOGW:
                TURNS.append(at % 2)
                at += 1 + k - LOGW
                TURNS.append(at % 2)
                at += 1
            at += min(k, LOGW)

        @block.tensor
        def _(pe):
            for n in range(2 * (LOGS - LOGW)):
                pe.wait_ge(s_turn, n + 1)
                src = bufs[TURNS[n]]
                for b in range(4):
                    last = pe.transpose(pT[:, b * P:(b + 1) * P], src[:, b * P:(b + 1) * P], ident[:, :])
                last.then_inc(s_turned, 1)
            pe.wait_ge(s_flt, 1)
            for n, (_, q, a) in enumerate(OUTS):
                for b in range(2):
                    last = pe.transpose(pU[n][:, b * P:(b + 1) * P], flt[:, q, a, b * P:(b + 1) * P], ident[:, :])
            last.then_inc(s_cols, 1)

        @block.vector
        def _(dve):
            link = Chain(dve, s_dve)
            dve.memset(keys[:, :, :], PADKEY).then_inc(s_pad, 1)
            dve.memset(zero1[:, :], 0).then_inc(s_zero, 1)
            dve.wait_ge(s_keys, 64)
            link(dve.tensor_scalar(tmp[:, :, :], keys[:, :, :], HALF, None, ALU.is_lt))
            link(dve.tensor_scalar(tmp2[:, :, :], tmp[:, :, :], HALF, 256 - HALF, ALU.mult, ALU.add))
            link(dve.tensor_tensor(tmp3[:, :, :], keys[:, :, :], tmp2[:, :, :], ALU.add))
            link(dve.tensor_scalar(tmp3[:, :, :], tmp3[:, :, :], IDB, None, ALU.logical_shift_left))
            link(dve.tensor_scalar(tmp[:, :, :], tmp[:, :, :], 31, None, ALU.logical_shift_left))
            link(dve.tensor_tensor(tmp[:, :, :], tmp[:, :, :], tmp3[:, :, :], ALU.bitwise_or))
            dve.wait_ge(s_ids, 2)
            link(dve.tensor_tensor(bufs[0][:, :].bitcast(I32).rearrange("p (q f) -> p q f", q=2), tmp[:, :, :], ids[:, :, :], ALU.bitwise_or))
            dve.wait_ge(s_const, 16)
            at = turns = 0

            def exchange(src, dst, stride):
                v = src[:, :].rearrange("p (b two s) -> p b two s", two=2, s=stride)
                o = dst[:, :].rearrange("p (b two s) -> p b two s", two=2, s=stride)
                dve.tensor_tensor(o[:, :, 0, :], v[:, :, 0, :], v[:, :, 1, :], ALU.min)
                link(dve.tensor_tensor(o[:, :, 1, :], v[:, :, 0, :], v[:, :, 1, :], ALU.max))

            for k in range(1, LOGS + 1):
                s = signs[:, k - 1, :].unsqueeze(1).to_broadcast([P, 2, SW])
                link(dve.tensor_tensor(bufs[1 - at][:, :].rearrange("p (q f) -> p q f", q=2),
                                       bufs[at][:, :].rearrange("p (q f) -> p q f", q=2), s, ALU.mult))
                at = 1 - at
                if k > LOGW:
                    dve.sem_inc(s_turn, 1)
                    turns += 1
                    dve.wait_ge(s_turned, turns)
                    link(dve.tensor_copy(bufs[1 - at][:, :], pT[:, :]))
                    at = 1 - at
                    for b in range(k - 1, LOGW - 1, -1):
                        exchange(bufs[at], bufs[1 - at], 1 << (b - LOGW))
                        at = 1 - at
                    dve.sem_inc(s_turn, 1)
                    turns += 1
                    dve.wait_ge(s_turned, turns)
                    link(dve.tensor_copy(bufs[1 - at][:, :], pT[:, :]))
                    at = 1 - at
                for b in range(min(k, LOGW) - 1, -1, -1):
                    exchange(bufs[at], bufs[1 - at], 1 << b)
                    at = 1 - at
            if at:
                link(dve.tensor_copy(bufs[0][:, :], bufs[1][:, :]))
            dve.sem_inc(s_wr, 1)
            w = bufs[0][:, :].bitcast(I32).rearrange("p (q f) -> p q f", q=2)
            link(dve.tensor_scalar(tmp[:, :, :], w, 31, None, ALU.logical_shift_right))
            link(dve.tensor_scalar(tmp2[:, :, :], tmp[:, :, :], -HALF, HALF - 256, ALU.mult, ALU.add))
            link(dve.tensor_scalar(tmp3[:, :, :], w, IDB, 0xFFFF, ALU.logical_shift_right, ALU.bitwise_and))
            link(dve.tensor_tensor(keys[:, :, :], tmp2[:, :, :], tmp3[:, :, :], ALU.add))
            link(dve.tensor_scalar(tmp[:, :, :], w, (1 << IDB) - 1, None, ALU.bitwise_and))
            link(dve.tensor_scalar(flt[:, :, 0, :], tmp[:, :, :], E - 1, None, ALU.min))
            link(dve.tensor_scalar(flt[:, :, 2, :], keys[:, :, :], N - 1, None, ALU.min))
            link(dve.tensor_scalar(tmp3[:, :, :], w, IDB, 0x1FFFF, ALU.logical_shift_right, ALU.bitwise_and))
            dve.wait_ge(s_next, 32)
            link(dve.tensor_scalar(nxt[:, :, :], nxt[:, :, :], IDB, 0x1FFFF, ALU.logical_shift_right, ALU.bitwise_and))
            link(dve.tensor_tensor(same[:, :, :], nxt[:, :, :], tmp3[:, :, :], ALU.is_equal))
            dve.sem_inc(s_same, 1)
            link(dve.scalar_tensor_tensor(flt[:, :, 1, :], same[:, :, :], FAR, keys[:, :, :], ALU.mult, ALU.add))
            dve.sem_inc(s_flt, 1)
            dve.wait_ge(s_cols, 1)
            for n, (name, _, _) in enumerate(OUTS):
                dve.tensor_copy(g[name][:, :].rearrange("p (t b) -> p t b", b=2),
                                pU[n][:, :].rearrange("p (b t) -> p t b", b=2)[:, 0:TILES // 2, :]).then_inc(s_out, 1)
            dve.wait_ge(s_out, len(OUTS))
            dve.tensor_scalar(g["scat_dst_agg"][:, :], g["scat_dst"][:, :], 2.0, 1.0, ALU.mult, ALU.add)
            dve.tensor_scalar(g["dst_x"][:, :], g["dst_id"][:, :], 2.0, None, ALU.mult)


def stage(pool, ix, slot, index, it, ready, woke):
    pool.tensor_copy(ix[:, slot, :], index[:, bass.ds(it * CT, CT)]).then_inc(ready, 1)


def gather_rows(pool, dst, table, ix, slot, sem):
    for t in range(CT):
        pool.indirect_dma_start(dst(t), None, table, bass.IndirectOffsetOnAxis(ix[:, slot, t:t + 1], 0)).then_inc(sem, 16)


def scatter_rows(pool, table, src, ix, slot, sem):
    for t in range(CT):
        pool.indirect_dma_start(table, bass.IndirectOffsetOnAxis(ix[:, slot, t:t + 1], 0), src(t), None,
                                bounds_check=table.shape[0] - 1, oob_is_err=False).then_inc(sem, 16)


def gather_pass(nc, g, table, width, index, keep_in, dt, fill=None):
    with ExitStack() as ctx:
        sb, ps, sem = scope(nc, ctx)
        buf = sb("gathered", [P, 2, CT, width], dt)
        ix = sb("index", [P, 2, CT], I32)
        tiles = [sb(f"fill_tile{n}", [P, 3200]) for n in range(len(fill or ()))]
        got = [sem("rows_gathered_even"), sem("rows_gathered_odd")]
        ix_ready, woke, kept = sem("index_staged"), sem("pool_woke"), sem("rows_kept")
        s_fill, s_filled = sem("fill_ready"), sem("filled")
        block = ctx.enter_context(nc.Block())

        @block.gpsimd
        def _(pool):
            for it, b, k in steps(pool):
                if not (isinstance(it, int) and it < 2):
                    wake(pool, kept, it - 1, woke)
                stage(pool, ix, b, index, it, ix_ready, woke)
                wake(pool, ix_ready, it + 1, woke)
                gather_rows(pool, lambda t: buf[:, b, t, :], table, ix, b, got[b])

        @block.vector
        def _(dve):
            for tile, (_, vec) in zip(tiles, fill or ()):
                if vec:
                    dve.tensor_copy(tiled(tile[:, :], 3200 // H), over_rows(g[vec], P, 3200 // H)).then_inc(s_fill, 1)
                else:
                    dve.memset(tile[:, :], 0.0).then_inc(s_fill, 1)
            for it, b, k in steps(dve):
                wake(dve, got[b], (k + 1) * (16 * CT), woke)
                dve.tensor_copy(keep_in[:, bass.ds(it * CT, CT), :], buf[:, b, :, :]).then_inc(kept, 1)

        @block.scalar
        def _(act):
            if fill:
                act.wait_ge(s_fill, len(fill))
                for tile, (name, _) in zip(tiles, fill):
                    fill_table(act, g[name], tile, s_filled)
                act.wait_ge(s_filled, 16 * len(fill) * (NPP * H // 3200))


def first(it, n):
    return isinstance(it, int) and it < n


def scatter_steps(pool, gather, scatter):
    for it, b, k in steps(pool, 4):
        gather(it, b, k)
        if not first(it, 2):
            scatter(it - 2, b, k - 1)
    for it in (STEPS - 2, STEPS - 1):
        scatter(it, it % 2, it // 2)


def load_keep(sp, g, row, parts, keep, loaded, used, dma=None):
    for it, b, k in steps(sp):
        if not first(it, 2):
            sp.wait_ge(used, it - 1)
        sp.dma_start(keep[:, b, :], g["keep"][row, bass.ds(it * CW, CW)].partition_broadcast(parts)).then_inc(loaded[b], 16)
        if dma:
            dma(it, b, k)


def messages(nc, g):
    with ExitStack() as ctx:
        sb, ps, sem = scope(nc, ctx)
        ends = sb("ends", [P, 2, CT, 2, H + 1])
        pair = sb("pair", [P, CT, 2 * H])
        ea = sb("edge_features", [P, 2, CT, ED], I32)
        ix = sb("ix", [P, 3, 2, CT], I32)
        catT = sb("catT", [P, CW])
        eaT = sb("eaT", [ED, CW])
        hT = sb("hT", [H, CW])
        mT = sb("mT", [H, CW])
        keep = sb("keep_row", [H, 2, CW])
        run = sb("running", [H, 2, CW])
        rows = sb("sum_rows", [P, 2, CT, H])
        pT = [ps("pT0", [P, CW]), ps("pT1", [P, CW])]
        pE = ps("pE", [ED, CW])
        pH = ps("pH", [H, CW])
        pM = ps("pM", [H, CW])
        pB = ps("pB", [P, CT * H])
        got = [sem("ends_gathered_even"), sem("ends_gathered_odd")]
        sent = [sem("sums_scattered_even"), sem("sums_scattered_odd")]
        loaded = [sem("keep_loaded_even"), sem("keep_loaded_odd")]
        ix_ready, turned, cat, eat, hid, act_h, msg, act_m = (sem(n) for n in (
            "index_staged", "ends_turned", "cat_copied", "features_copied", "hidden_summed", "hidden_ready", "message_summed", "message_ready"))
        scanned, back, rows_ready, norms, ea_ready = (sem(n) for n in (
            "scanned", "sums_turned_back", "sum_rows_ready", "norms_kept", "features_staged"))
        w_pool, w_pe, w_dve = sem("pool_woke"), sem("pe_woke"), sem("dve_woke")
        paired = sem("ends_paired")
        block = ctx.enter_context(nc.Block())
        src_ix = g["record"][:, :, ED:ED + 1]

        @block.gpsimd
        def _(pool):
            def gather(it, b, k):
                if not first(it, 2):
                    wake(pool, paired, it - 1, w_pool)
                    wake(pool, norms, it - 1, w_pool)
                pool.tensor_copy(ix[:, 0, b, :].unsqueeze(2), src_ix[:, bass.ds(it * CT, CT), :]).then_inc(ix_ready, 1)
                pool.tensor_copy(ix[:, 1, b, :], g["dst_id"][:, bass.ds(it * CT, CT)]).then_inc(ix_ready, 1)
                wake(pool, ix_ready, staged(it, 0), w_pool)
                gather_rows(pool, lambda t: ends[:, b, t, 0, :], g["in"]["x_norm"], ix[:, 0], b, got[b])
                gather_rows(pool, lambda t: ends[:, b, t, 1, :], g["in"]["x_norm"], ix[:, 1], b, got[b])

            def staged(it, scatter):
                if scatter:
                    return 2 * STEPS + it + 1 if isinstance(it, int) and it >= STEPS - 2 else it * 3 + 7
                return 2 * it + 2 if first(it, 2) else it * 3

            def scatter(it, b, k):
                if not first(it, 2):
                    wake(pool, sent[b], k * (16 * CT), w_pool)
                pool.tensor_copy(ix[:, 2, b, :], g["scat_dst_agg"][:, bass.ds(it * CT, CT)]).then_inc(ix_ready, 1)
                wake(pool, ix_ready, staged(it, 1), w_pool)
                wake(pool, rows_ready, it + 1, w_pool)
                scatter_rows(pool, halves(g["XA0"]), lambda t: rows[:, b, t, :], ix[:, 2], b, sent[b])

            scatter_steps(pool, gather, scatter)
            for b in range(2):
                pool.wait_ge(sent[b], 16 * CT * STEPS // 2)

        @block.sync
        def _(sp):
            load_keep(sp, g, 0, H, keep, loaded, scanned)
            for b in range(2):
                sp.wait_ge(loaded[b], 16 * STEPS // 2)

        @block.tensor
        def _(pe):
            for it, b, k in steps(pe):
                wake(pe, paired, it + 1, w_pe)
                wake(pe, ea_ready, it + 1, w_pe)
                for t in range(CT):
                    pe.transpose(pT[b][:, t * P:(t + 1) * P], pair[:, t, :], g["ident"][:, :])
                for t in range(CT):
                    last = pe.transpose(pE[:, t * P:(t + 1) * P], ea[:, b, t, :].bitcast(F32), g["ident"][:, :])
                last.then_inc(turned, 1)
                wake(pe, cat, it + 1, w_pe)
                pe.matmul(pH[:, :], g["w_msg1"][:, :], catT[:, :], start=True, stop=False)
                wake(pe, eat, it + 1, w_pe)
                pe.matmul(pH[:, :], g["w_msg1e"][:, :], eaT[:, :], start=False, stop=True).then_inc(hid, 1)
                wake(pe, act_h, it + 1, w_pe)
                pe.matmul(pM[:, :], g["w_msg2"][:, :], hT[:, :], start=True, stop=True).then_inc(msg, 1)
                wake(pe, scanned, it + 1, w_pe)
                if not first(it, 1):
                    wake(pe, rows_ready, it, w_pe)
                for t in range(CT):
                    last = pe.transpose(pB[:, t * H:(t + 1) * H], run[:, b, t * P:(t + 1) * P], g["ident"][0:H, 0:H])
                last.then_inc(back, 1)

        @block.scalar
        def _(act):
            for it, b, k in steps(act):
                act.wait_ge(got[b], (k + 1) * (16 * 2 * CT))
                if not first(it, 1):
                    act.wait_ge(turned, it)
                act.activation(pair[:, :, :].rearrange("p t (e h) -> p t e h", e=2), ends[:, b, :, :, 0:H], ACT.Copy).then_inc(paired, 1)
                act.wait_ge(turned, it + 1)
                if not first(it, 1):
                    act.wait_ge(hid, it)
                act.activation(catT[:, :], pT[b][:, :], ACT.Copy).then_inc(cat, 1)
                act.wait_ge(hid, it + 1)
                if not first(it, 1):
                    act.wait_ge(msg, it)
                act.activation(hT[:, :], pH[:, :], ACT.Relu, bias=g["b_msg1"][:, 0:1]).then_inc(act_h, 1)
                act.wait_ge(msg, it + 1)
                if not first(it, 1):
                    act.wait_ge(scanned, it)
                act.activation(mT[:, :], pM[:, :], ACT.Identity, bias=g["b_msg2"][:, 0:1]).then_inc(act_m, 1)

        @block.vector
        def _(dve):
            dve.tensor_scalar(g["src_x"][:, :], g["record"][:, :, ED], 2.0, None, ALU.mult)
            for it, b, k in steps(dve):
                if not first(it, 2):
                    wake(dve, turned, it - 1, w_dve)
                dve.tensor_copy(ea[:, b, :, :], g["record"][:, bass.ds(it * CT, CT), 0:ED]).then_inc(ea_ready, 1)
                wake(dve, got[b], (k + 1) * (16 * 2 * CT), w_dve)
                dve.tensor_copy(g["norm_src"][:, bass.ds(it * CT, CT)], ends[:, b, :, 0, H])
                dve.tensor_copy(g["norm_dst"][:, bass.ds(it * CT, CT)], ends[:, b, :, 1, H]).then_inc(norms, 1)
                wake(dve, turned, it + 1, w_dve)
                if not first(it, 1):
                    wake(dve, hid, it, w_dve)
                dve.tensor_copy(eaT[:, :], pE[:, :]).then_inc(eat, 1)
                wake(dve, act_m, it + 1, w_dve)
                wake(dve, loaded[b], (k + 1) * 16, w_dve)
                if not first(it, 1):
                    wake(dve, scanned, it, w_dve)
                if not first(it, 2):
                    wake(dve, back, it - 1, w_dve)
                dve.tensor_tensor_scan(run[:, b, :], keep[:, b, :], mT[:, :],
                                       0.0 if first(it, 1) else run[:, 1 - b, CW - 1:CW], ALU.mult, ALU.add).then_inc(scanned, 1)
                wake(dve, back, it + 1, w_dve)
                if not first(it, 2):
                    wake(dve, sent[b], k * (16 * CT), w_dve)
                dve.tensor_copy(rows[:, b, :, :].rearrange("p t h -> p (t h)"), pB[:, :]).then_inc(rows_ready, 1)


def attention(nc, g):
    with ExitStack() as ctx:
        sb, ps, sem = scope(nc, ctx)
        ends = sb("ends", [P, 2, CT, 2, H])
        ix = sb("ix", [P, 3, 2, CT], I32)
        catT = sb("catT", [P, CW])
        qT = sb("qT", [H, CW])
        prod = sb("prod", [H, CW])
        clip = sb("clip", [P, CW])
        e_low = sb("e_low", [H, CW])
        mz = sb("mz", [P, CW])
        keep = sb("keep_row", [P, 2, CW])
        run = sb("running", [P, 2, CW])
        z1 = sb("z1", [P, CT, H])
        rz = sb("rz", [P, CT, H])
        rows = sb("sum_rows", [P, 2, CT, H])
        pT = [ps("pT0", [P, CW]), ps("pT1", [P, CW])]
        pQ, pK, pV = ps("pQ", [H, CW]), ps("pK", [H, CW]), ps("pV", [H, CW])
        pS = ps("pS", [P, CW])
        pB = ps("pB", [P, CT * P])
        got = [sem("ends_gathered_even"), sem("ends_gathered_odd")]
        sent = [sem("sums_scattered_even"), sem("sums_scattered_odd")]
        loaded = [sem("keep_loaded_even"), sem("keep_loaded_odd")]
        ix_ready, turned, cat, qkv, q_ready, prod_ready, score, clipped, exped, weighed = (sem(n) for n in (
            "index_staged", "ends_turned", "cat_copied", "qkv_ready", "q_biased", "prod_ready", "score_summed", "score_clipped",
            "exp_ready", "values_weighed"))
        scanned, back, rows_ready, s_dve = (sem(n) for n in ("scanned", "sums_turned_back", "sum_rows_ready", "dve_step"))
        w_pool, w_pe, w_dve = sem("pool_woke"), sem("pe_woke"), sem("dve_woke")
        block = ctx.enter_context(nc.Block())

        @block.gpsimd
        def _(pool):
            def staged(it, scatter):
                if scatter:
                    return 2 * STEPS + it + 1 if isinstance(it, int) and it >= STEPS - 2 else it * 3 + 7
                return 2 * it + 2 if first(it, 2) else it * 3

            def gather(it, b, k):
                if not first(it, 2):
                    wake(pool, turned, it - 1, w_pool)
                pool.tensor_copy(ix[:, 0, b, :], g["src_x"][:, bass.ds(it * CT, CT)]).then_inc(ix_ready, 1)
                pool.tensor_copy(ix[:, 1, b, :], g["dst_x"][:, bass.ds(it * CT, CT)]).then_inc(ix_ready, 1)
                wake(pool, ix_ready, staged(it, 0), w_pool)
                gather_rows(pool, lambda t: ends[:, b, t, 0, :], halves(g["XA1"]), ix[:, 0], b, got[b])
                gather_rows(pool, lambda t: ends[:, b, t, 1, :], halves(g["XA1"]), ix[:, 1], b, got[b])

            def scatter(it, b, k):
                if not first(it, 2):
                    wake(pool, sent[b], k * (16 * CT), w_pool)
                pool.tensor_copy(ix[:, 2, b, :], g["scat_dst_agg"][:, bass.ds(it * CT, CT)]).then_inc(ix_ready, 1)
                wake(pool, ix_ready, staged(it, 1), w_pool)
                wake(pool, rows_ready, it + 1, w_pool)
                scatter_rows(pool, halves(g["XA1"]), lambda t: rows[:, b, t, :], ix[:, 2], b, sent[b])

            scatter_steps(pool, gather, scatter)
            for b in range(2):
                pool.wait_ge(sent[b], 16 * CT * STEPS // 2)

        @block.sync
        def _(sp):
            load_keep(sp, g, 0, P, keep, loaded, scanned)
            for b in range(2):
                sp.wait_ge(loaded[b], 16 * STEPS // 2)

        @block.tensor
        def _(pe):
            for it, b, k in steps(pe):
                wake(pe, got[b], (k + 1) * (16 * 2 * CT), w_pe)
                for t in range(CT):
                    last = pe.transpose(pT[b][:, t * P:(t + 1) * P], ends[:, b, t, :, :].rearrange("p e h -> p (e h)"), g["ident"][:, :])
                last.then_inc(turned, 1)
                wake(pe, cat, it + 1, w_pe)
                if not first(it, 1):
                    wake(pe, weighed, it, w_pe)
                pe.matmul(pQ[:, :], g["wq"][:, :], catT[:, :], start=True, stop=True).then_inc(qkv, 1)
                pe.matmul(pK[:, :], g["wk"][:, :], catT[:, :], start=True, stop=True).then_inc(qkv, 1)
                pe.matmul(pV[:, :], g["wv"][:, :], catT[:, :], start=True, stop=True).then_inc(qkv, 1)
                wake(pe, prod_ready, it + 1, w_pe)
                pe.matmul(pS[:, :], g["head_sum"][:, :], prod[:, :], start=True, stop=True).then_inc(score, 1)
                wake(pe, scanned, it + 1, w_pe)
                if not first(it, 1):
                    wake(pe, rows_ready, it, w_pe)
                for t in range(CT):
                    last = pe.transpose(pB[:, t * P:(t + 1) * P], run[:, b, t * P:(t + 1) * P], g["ident"][:, :])
                last.then_inc(back, 1)

        @block.scalar
        def _(act):
            for it, b, k in steps(act):
                act.wait_ge(turned, it + 1)
                if not first(it, 1):
                    act.wait_ge(qkv, it * 3)
                act.activation(catT[:, :], pT[b][:, :], ACT.Copy).then_inc(cat, 1)
                act.wait_ge(qkv, it * 3 + 1)
                if not first(it, 1):
                    act.wait_ge(prod_ready, it)
                act.activation(qT[:, :], pQ[:, :], ACT.Identity, bias=g["b_q"][:, 0:1]).then_inc(q_ready, 1)
                act.wait_ge(clipped, it + 1)
                if not first(it, 1):
                    act.wait_ge(scanned, it)
                act.activation(e_low[:, :], clip[0:H, :], ACT.Exp)
                act.activation(mz[H:P, :], clip[H:P, :], ACT.Exp).then_inc(exped, 1)

        @block.vector
        def _(dve):
            link = Chain(dve, s_dve, 2)
            for it, b, k in steps(dve):
                link.start(it)
                wake(dve, q_ready, it + 1, w_dve)
                wake(dve, qkv, it * 3 + 2, w_dve)
                if not first(it, 1):
                    wake(dve, score, it, w_dve)
                dve.scalar_tensor_tensor(prod[:, :], pK[:, :], g["b_k"][:, 0:1], qT[:, :], ALU.add, ALU.mult).then_inc(prod_ready, 1)
                wake(dve, score, it + 1, w_dve)
                if not first(it, 1):
                    wake(dve, exped, it, w_dve)
                dve.tensor_scalar(clip[:, :], pS[:, :], 5.0, -5.0, ALU.min, ALU.max).then_inc(clipped, 1)
                wake(dve, exped, it + 1, w_dve)
                wake(dve, qkv, it * 3 + 3, w_dve)
                dve.scalar_tensor_tensor(mz[0:H, :], pV[:, :], g["b_v"][:, 0:1], e_low[:, :], ALU.add, ALU.mult).then_inc(weighed, 1)
                wake(dve, weighed, it + 1, w_dve)
                wake(dve, loaded[b], (k + 1) * 16, w_dve)
                if not first(it, 1):
                    wake(dve, scanned, it, w_dve)
                if not first(it, 2):
                    wake(dve, back, it - 1, w_dve)
                dve.tensor_tensor_scan(run[:, b, :], keep[:, b, :], mz[:, :],
                                       0.0 if first(it, 1) else run[:, 1 - b, CW - 1:CW], ALU.mult, ALU.add).then_inc(scanned, 1)
                wake(dve, back, it + 1, w_dve)
                sums = pB[:, :].rearrange("p (t c) -> p t c", t=CT)
                link(dve.tensor_scalar(z1[:, :, :], sums[:, :, H:P], 1.0, None, ALU.add))
                link(dve.reciprocal(rz[:, :, :], z1[:, :, :]))
                if not first(it, 2):
                    wake(dve, sent[b], k * (16 * CT), w_dve)
                dve.tensor_tensor(rows[:, b, :, :], sums[:, :, 0:H], rz[:, :, :], ALU.mult).then_inc(rows_ready, 1)


def spread(nc, g, table, index, keep_row, weight=None, bias=None, relu=False, scatter_to=None, scatter_ix=None, rows_to=None):
    with ExitStack() as ctx:
        sb, ps, sem = scope(nc, ctx)
        got_rows = sb("got_rows", [P, 2, CT, H])
        scaled = sb("scaled", [P, 2, CT, H])
        ix = sb("ix", [P, 2, 2, CT], I32)
        xT = sb("xT", [H, CW])
        keep = sb("keep_row", [H, 2, CW])
        run = sb("running", [H, 2, CW])
        normed = sb("normed", [P, CT, H])
        biased = sb("biased", [P, CT, H])
        lone = sb("lone_row", [1, H])
        rows = sb("sum_rows", [P, 2, CT, H])
        pT = [ps("pT0", [H, CW]), ps("pT1", [H, CW])]
        pM = ps("pM", [H, CW])
        pB = ps("pB", [P, CT * H])
        got = [sem("rows_gathered_even"), sem("rows_gathered_odd")]
        sent = [sem("sums_out_even"), sem("sums_out_odd")]
        loaded = [sem("keep_loaded_even"), sem("keep_loaded_odd")]
        ix_ready, turned, copied, prod, scaled_up = (sem(n) for n in ("index_staged", "rows_turned", "turned_copied", "product_ready", "rows_scaled"))
        scanned, back, rows_ready, s_dve = (sem(n) for n in ("scanned", "sums_turned_back", "sum_rows_ready", "dve_step"))
        w_pool, w_pe, w_dve = sem("pool_woke"), sem("pe_woke"), sem("dve_woke")
        lone_ready, lone_sent = sem("lone_row_ready"), sem("lone_row_stored")
        block = ctx.enter_context(nc.Block())
        per_row = 16 * CT if scatter_to is not None else 16

        @block.gpsimd
        def _(pool):
            both = 2 if scatter_to is not None else 1

            def gather(it, b, k):
                if not first(it, 2):
                    wake(pool, scaled_up if weight is not None else turned, it - 1, w_pool)
                pool.tensor_copy(ix[:, 0, b, :], index[:, bass.ds(it * CT, CT)]).then_inc(ix_ready, 1)
                wake(pool, ix_ready, it * 2 - 1 if both == 2 and not first(it, 2) else it + 1, w_pool)
                gather_rows(pool, lambda t: got_rows[:, b, t, :], table, ix[:, 0], b, got[b])

            def scatter(it, b, k):
                if not first(it, 2):
                    wake(pool, sent[b], k * (16 * CT), w_pool)
                pool.tensor_copy(ix[:, 1, b, :], scatter_ix[:, bass.ds(it * CT, CT)]).then_inc(ix_ready, 1)
                wake(pool, ix_ready, STEPS + it + 1 if isinstance(it, int) and it >= STEPS - 2 else it * 2 + 4, w_pool)
                wake(pool, rows_ready, it + 1, w_pool)
                scatter_rows(pool, scatter_to, lambda t: rows[:, b, t, :], ix[:, 1], b, sent[b])

            if scatter_to is not None:
                scatter_steps(pool, gather, scatter)
                for b in range(2):
                    pool.wait_ge(sent[b], per_row * STEPS // 2)
            else:
                for it, b, k in steps(pool):
                    gather(it, b, k)

        @block.sync
        def _(sp):
            load_keep(sp, g, keep_row, H, keep, loaded, scanned)
            for b in range(2):
                sp.wait_ge(loaded[b], 16 * STEPS // 2)

        @block.tensor
        def _(pe):
            src = scaled if weight is not None else got_rows
            for it, b, k in steps(pe):
                if weight is not None:
                    wake(pe, scaled_up, it + 1, w_pe)
                else:
                    wake(pe, got[b], (k + 1) * (16 * CT), w_pe)
                    if not first(it, 2):
                        wake(pe, scanned, it - 1, w_pe)
                for t in range(CT):
                    last = pe.transpose(pT[b][:, t * P:(t + 1) * P], src[:, b, t, :], g["ident"][:, :])
                last.then_inc(turned, 1)
                if weight is not None:
                    wake(pe, copied, it + 1, w_pe)
                    pe.matmul(pM[:, :], weight[:, :], xT[:, :], start=True, stop=True).then_inc(prod, 1)
                wake(pe, scanned, it + 1, w_pe)
                if not first(it, 1):
                    wake(pe, rows_ready, it, w_pe)
                for t in range(CT):
                    last = pe.transpose(pB[:, t * H:(t + 1) * H], run[:, b, t * P:(t + 1) * P], g["ident"][0:H, 0:H])
                last.then_inc(back, 1)

        @block.scalar
        def _(act):
            if rows_to is not None:
                act.activation(lone[:, :], bias[0:1, :], ACT.Relu).then_inc(lone_ready, 1)
                act.wait_ge(lone_ready, 1)
                act.dma_start(rows_to[ROWS:ROWS + 1, :], lone[:, :]).then_inc(lone_sent, 16)
                act.wait_ge(lone_sent, 16)
            for it, b, k in steps(act):
                if weight is not None:
                    act.wait_ge(turned, it + 1)
                    if not first(it, 1):
                        act.wait_ge(prod, it)
                    act.activation(xT[:, :], pT[b][:, :], ACT.Copy).then_inc(copied, 1)
                if rows_to is not None:
                    act.wait_ge(rows_ready, it + 1)
                    act.dma_start(rows_to[bass.ds(it * CW, CW), :].rearrange("(p t) h -> p t h", t=CT),
                                  rows[:, b, :, :]).then_inc(sent[b], 16)
            if rows_to is not None:
                for b in range(2):
                    act.wait_ge(sent[b], per_row * STEPS // 2)

        @block.vector
        def _(dve):
            def scale(it, b, k):
                wake(dve, got[b], (k + 1) * (16 * CT), w_dve)
                if not first(it, 2):
                    wake(dve, turned, it - 1, w_dve)
                norm = g["norm_src"][:, bass.ds(it * CT, CT)]
                dve.tensor_tensor(scaled[:, b, :, :], got_rows[:, b, :, :], over_tiles(norm, H, CT), ALU.mult).then_inc(scaled_up, 1)

            link = Chain(dve, s_dve, 0 if weight is None else 2 if relu else 1)
            for it, b, k in steps(dve):
                link.start(it)
                if weight is not None:
                    scale(it, b, k)
                    wake(dve, prod, it + 1, w_dve)
                else:
                    wake(dve, turned, it + 1, w_dve)
                wake(dve, loaded[b], (k + 1) * 16, w_dve)
                if not first(it, 1):
                    wake(dve, scanned, it, w_dve)
                if not first(it, 2):
                    wake(dve, back, it - 1, w_dve)
                dve.tensor_tensor_scan(run[:, b, :], keep[:, b, :], (pM if weight is not None else pT[b])[:, :],
                                       0.0 if first(it, 1) else run[:, 1 - b, CW - 1:CW], ALU.mult, ALU.add).then_inc(scanned, 1)
                wake(dve, back, it + 1, w_dve)
                sums = tiled(pB[:, :], CT)
                if weight is not None:
                    norm = g["norm_dst"][:, bass.ds(it * CT, CT)]
                    link(dve.tensor_tensor(normed[:, :, :], sums, over_tiles(norm, H, CT), ALU.mult))
                    if relu:
                        link(dve.tensor_tensor(biased[:, :, :], normed[:, :, :], over_rows(bias, P, CT), ALU.add))
                if not first(it, 2):
                    wake(dve, sent[b], k * per_row, w_dve)
                if weight is None:
                    dve.tensor_copy(rows[:, b, :, :], sums).then_inc(rows_ready, 1)
                elif relu:
                    dve.tensor_scalar(rows[:, b, :, :], biased[:, :, :], 0.0, None, ALU.max).then_inc(rows_ready, 1)
                else:
                    dve.tensor_tensor(rows[:, b, :, :], normed[:, :, :], over_rows(bias, P, CT), ALU.add).then_inc(rows_ready, 1)


def scatter_rows_of_nodes(nc, g):
    with ExitStack() as ctx:
        sb, ps, sem = scope(nc, ctx)
        ix = sb("ix", [P, 2, CT], I32)
        val = sb("val", [P, 2, CT], I32)
        staged, woke = sem("staged"), sem("pool_woke")
        sent = [sem("rows_sent_even"), sem("rows_sent_odd")]
        block = ctx.enter_context(nc.Block())

        @block.gpsimd
        def _(pool):
            for it, b, k in steps(pool):
                if not first(it, 2):
                    wake(pool, sent[b], k * (16 * CT), woke)
                pool.tensor_copy(val[:, b, :], g["slot_row"][:, bass.ds(it * CT, CT)])
                pool.tensor_copy(ix[:, b, :], g["scat_dst"][:, bass.ds(it * CT, CT)]).then_inc(staged, 1)
                wake(pool, staged, it + 1, woke)
                scatter_rows(pool, g["edge_row"], lambda t: val[:, b, t:t + 1], ix, b, sent[b])
            for b in range(2):
                pool.wait_ge(sent[b], 16 * CT * STEPS // 2)


def dense(nc, g, kind, x, agg, out):
    mlp, attend = kind == "mlp", kind == "attend"
    update = mlp or attend
    with ExitStack() as ctx:
        sb, ps, sem = scope(nc, ctx)
        xa = sb("xa", [NP, 2, G, 2 * H] if update else [NP, 2, 2, DW])
        z = sb("z", [NP, 2, DW])
        sq = sb("sq", [NP, DW])
        yw = 2 * H if mlp else H
        y = sb("y", [NP, 2, G, yw])
        SUM, SQUARES, MEAN, VAR, RSTD = range(5)
        st = sb("stats", [NP, 5, 2, G])
        minus_half, s_half = sb("minus_half", [NP, 2, G]), sem("exponent_ready")
        load = [sem("loaded_even"), sem("loaded_odd")]
        store = [sem("stored_even"), sem("stored_odd")]
        z_ready, zsq, y_ready, s_a, s_b, s_p, var_ready, rstd_ready = (sem(n) for n in (
            "z_ready", "z_squared", "y_ready", "dve_step_h", "dve_step_z", "pool_step", "variance_ready", "rstd_ready"))
        w_pe, w_pool, w_dve = sem("pe_woke"), sem("pool_woke"), sem("dve_woke")
        if update:
            h = sb("h", [NP, 2, DW])
            hsq = sb("hsq", [NP, DW])
            d = sb("d", [NP, 2, DW])
            xb = sb("xb", [NP, DW])
            u = sb("u", [NP, DW])
            xh = sb("xh", [NP, DW])
            rb = sb("rb", [P, H])
            cT = [sb(f"cT{q}", [P, QW]) for q in range(2)]
            pT = [ps(f"pT{q}", [P, 512]) for q in range(2)]
            turned, cat, outp, h_ready, hsqd, d_ready, xb_ready, s_rb = (sem(n) for n in (
                "turned", "turned_copied", "rows_out", "h_ready", "h_squared", "d_ready", "biased_x_ready", "bias_ready"))
            if mlp:
                hT = [sb(f"hT{q}", [H + 1, QW]) for q in range(2)]
                pH = [ps(f"pH{q}", [H, 512]) for q in range(2)]
                pO = [ps("pO", [NP, DW])]
                pS = ps("pS", [NP, DW])
                hid, act_h, silu, ones = sem("hidden_summed"), sem("hidden_ready"), sem("silu_ready"), sem("ones_ready")
            else:
                pO = [ps(f"pO{q}", [NP, DW]) for q in range(2)]
        block = ctx.enter_context(nc.Block())
        gq = G // QN
        LOADS = 16 if update else 32

        @block.sync
        def _(sp):
            def put(it, b, k):
                sp.wait_ge(y_ready, it + 1)
                sp.dma_start(rows_of(out)[:, bass.ds(it * (G * yw), G * yw)], y[:, b, :, :].rearrange("p n h -> p (n h)")).then_inc(store[b], 16)

            for it, b, k in steps(sp):
                if not first(it, 2):
                    if update:
                        sp.wait_ge(h_ready, it - 1)
                        sp.wait_ge(xb_ready, it - 1)
                    else:
                        sp.wait_ge(z_ready, it - 1)
                if update:
                    sp.dma_start(xa[:, b, :, :].rearrange("p n h -> p (n h)"), rows_of(x)[:, bass.ds(it * (2 * DW), 2 * DW)]).then_inc(load[b], 16)
                else:
                    sp.dma_start(xa[:, b, 0, :], rows_of(x)[:, bass.ds(it * DW, DW)]).then_inc(load[b], 16)
                    sp.dma_start(xa[:, b, 1, :], rows_of(agg)[:, bass.ds(it * DW, DW)]).then_inc(load[b], 16)
                if not first(it, 2):
                    put(it - 2, b, k - 1)
            for it in (STEPS - 2, STEPS - 1):
                put(it, it % 2, it // 2)
            for b in range(2):
                sp.wait_ge(store[b], 16 * STEPS // 2)

        if update:
            @block.tensor
            def _(pe):
                def turn(it, b, q):
                    if q < 2 and not first(it, 1):
                        wake(pe, cat, it * QN + (q - 1), w_pe)
                    elif q >= 2:
                        wake(pe, cat, it * QN + (q - 1), w_pe)
                    for j in range(gq):
                        last = pe.transpose(pT[q % 2][:, j * NP:(j + 1) * NP], xa[:, b, q * gq + j, :], g["ident"][0:NP, 0:NP])
                    last.then_inc(turned, 1)

                def hidden(it, q):
                    wake(pe, cat, it * QN + (q + 1), w_pe)
                    if not (first(it, 1) and q < 2):
                        wake(pe, act_h, it * QN + (q - 1), w_pe)
                    pe.matmul(pH[q % 2][:, 0:QW], g["w_upd1"][:, :], cT[q % 2][:, :], start=True, stop=True).then_inc(hid, 1)

                def project(it, b, q):
                    if mlp:
                        wake(pe, act_h, it * QN + (q + 1), w_pe)
                        if q == 0 and not first(it, 1):
                            wake(pe, silu, it, w_pe)
                        left, right, o = hT[q % 2], g["w_upd2"], pO[0]
                    else:
                        wake(pe, cat, it * QN + (q + 1), w_pe)
                        if q == 0 and not first(it, 2):
                            wake(pe, h_ready, it - 1, w_pe)
                        left, right, o = cT[q % 2], g["w_out"], pO[b]
                    for j in range(gq):
                        c = (q * gq + j) * H
                        last = pe.matmul(o[:, c:c + H], left[:, j * NP:(j + 1) * NP], right[:, :], start=True, stop=True)
                    last.then_inc(outp, 1)

                if mlp:
                    pe.wait_ge(ones, 1)
                for it, b, k in steps(pe):
                    wake(pe, load[b], (k + 1) * LOADS, w_pe)
                    turn(it, b, 0)
                    turn(it, b, 1)
                    if mlp:
                        hidden(it, 0)
                        turn(it, b, 2)
                        hidden(it, 1)
                        project(it, b, 0)
                        turn(it, b, 3)
                        hidden(it, 2)
                        project(it, b, 1)
                        hidden(it, 3)
                    else:
                        project(it, b, 0)
                        turn(it, b, 2)
                        project(it, b, 1)
                        turn(it, b, 3)
                    project(it, b, 2)
                    project(it, b, 3)

        @block.scalar
        def _(act):
            def copy(it, q):
                act.wait_ge(turned, it * QN + (q + 1))
                if not (first(it, 1) and q < 2):
                    act.wait_ge(hid if mlp else outp, it * QN + (q - 1))
                act.activation(cT[q % 2][:, :], pT[q % 2][:, 0:QW], ACT.Copy).then_inc(cat, 1)

            def rectify(it, q):
                act.wait_ge(hid, it * QN + (q + 1))
                if not (first(it, 1) and q < 2):
                    act.wait_ge(outp, it * QN + (q - 1))
                act.activation(hT[q % 2][0:H, :], pH[q % 2][:, 0:QW], ACT.Relu, bias=g["b_upd1"][:, 0:1]).then_inc(act_h, 1)

            def square_z(it, b):
                act.wait_ge(z_ready, it + 1)
                if not (update or first(it, 1)):
                    act.wait_ge(var_ready, it)
                elif update and not first(it, 1):
                    act.wait_ge(var_ready, it + 1)
                act.activation(sq[:, :], z[:, b, :], ACT.Square).then_inc(zsq, 1)

            for it, b, k in steps(act):
                if update:
                    copy(it, 0)
                    copy(it, 1)
                    if mlp:
                        rectify(it, 0)
                        copy(it, 2)
                        rectify(it, 1)
                        copy(it, 3)
                        rectify(it, 2)
                        rectify(it, 3)
                        act.wait_ge(outp, it * QN + QN)
                        if not first(it, 1):
                            act.wait_ge(h_ready, it)
                        act.activation(pS[:, :], pO[0][:, :], ACT.Silu).then_inc(silu, 1)
                    else:
                        copy(it, 2)
                        copy(it, 3)
                    if not first(it, 1):
                        square_z(it - 1, 1 - b)
                    act.wait_ge(h_ready, it + 1)
                    if not first(it, 1):
                        act.wait_ge(var_ready, it)
                    act.activation(hsq[:, :], h[:, b, :], ACT.Square).then_inc(hsqd, 1)
                else:
                    square_z(it, b)
            if update:
                square_z(STEPS - 1, 1)

        @block.gpsimd
        def _(pool):
            link = Chain(pool, s_p, 2 if attend else 1)
            pool.memset(minus_half[:, :, :], -0.5).then_inc(s_half, 1)
            pool.wait_ge(s_half, 1)

            def inverse_root(it, which):
                wake(pool, var_ready, it + 1, w_pool)
                pool.tensor_tensor(st[:, RSTD, which, :], st[:, VAR, which, :], minus_half[:, which, :], ALU.pow).then_inc(rstd_ready, 1)

            for it, b, k in steps(pool):
                if update:
                    X = xa[:, b, :, 0:H]
                else:
                    X, A = tiled(xa[:, b, 0, :], G), tiled(xa[:, b, 1, :], G)
                Z = tiled(z[:, b, :], G)
                wake(pool, load[b], (k + 1) * LOADS, w_pool)
                if not update:
                    if not first(it, 2):
                        wake(pool, y_ready, it - 1, w_pool)
                    pool.tensor_tensor(Z, X, A, ALU.add).then_inc(z_ready, 1)
                    if not first(it, 1):
                        inverse_root(it - 1, slice(1 - b, 2 - b))
                    continue
                link.start(it)
                if not first(it, 1):
                    wake(pool, z_ready, it, w_pool)
                pool.tensor_tensor(tiled(xb[:, :], G), X, over_rows(g["r_b" if mlp else "r_beta"], NP, G), ALU.add).then_inc(xb_ready, 1)
                left = xb
                if attend:
                    wake(pool, h_ready, it + 1, w_pool)
                    wake(pool, xb_ready, it + 1, w_pool)
                    link(pool.tensor_tensor(xh[:, :], xb[:, :], h[:, b, :], ALU.add))
                    left = xh
                inverse_root(it, slice(0, 2))
                wake(pool, d_ready, it + 1, w_pool)
                if attend:
                    link(pool.tensor_tensor(tiled(u[:, :], G), tiled(d[:, b, :], G), over_rows(g["r_gamma"], NP, G), ALU.mult))
                else:
                    link(pool.tensor_tensor(tiled(u[:, :], G), tiled(d[:, b, :], G), over_rows(g["r_g"], NP, G), ALU.mult))
                    wake(pool, xb_ready, it + 1, w_pool)
                if not first(it, 2):
                    wake(pool, y_ready, it - 1, w_pool)
                pool.tensor_tensor(z[:, b, :], u[:, :], left[:, :], ALU.add).then_inc(z_ready, 1)
            if update:
                inverse_root(STEPS, slice(0, 2))
            else:
                inverse_root(STEPS - 1, slice(1, 2))

        @block.vector
        def _(dve):
            la, lb = Chain(dve, s_a, 5), Chain(dve, s_b, 2)
            if mlp:
                dve.memset(y[:, :, :, H:2 * H], 0.0)
                for q in range(2):
                    last = dve.memset(hT[q][H:H + 1, :], 1.0)
                last.then_inc(ones, 1)
            if update:
                dve.memset(st[:, :, :, :], 0.0).then_inc(s_rb, 1)
                dve.wait_ge(s_rb, 1)
            if attend:
                dve.tensor_tensor(rb[:, :], g["r_bf"][:, :], g["r_bo"][:, :], ALU.add).then_inc(s_rb, 1)
                dve.wait_ge(s_rb, 2)

            def row_sum(link, kind, which, rows):
                link(dve.tensor_reduce(st[:, kind, which, :], rows, AX.X, ALU.add))

            def variance(link, which):
                mean, var = st[:, MEAN, which, :], st[:, VAR, which, :]
                link(dve.tensor_scalar(mean, st[:, SUM, which, :], 1.0 / H, None, ALU.mult))
                link(dve.tensor_tensor(var, mean, mean, ALU.mult))
                link(dve.scalar_tensor_tensor(var, st[:, SQUARES, which, :], 1.0 / H, var, ALU.mult, ALU.subtract))
                dve.tensor_scalar(var, var, 0.0, EPS, ALU.max, ALU.add).then_inc(var_ready, 1)

            def normalise(which, src, dst, done):
                for j in range(G):
                    last = dve.tensor_scalar(dst[:, j, 0:H], src[:, j * H:(j + 1) * H],
                                             st[:, MEAN, which, j:j + 1], st[:, RSTD, which, j:j + 1], ALU.subtract, ALU.mult)
                last.then_inc(done, 1)

            def h_sum(it, b, k):
                if mlp:
                    wake(dve, silu, it + 1, w_dve)
                    wake(dve, load[b], (k + 1) * LOADS, w_dve)
                    dve.tensor_tensor(tiled(h[:, b, :], G), tiled(pS[:, :], G), xa[:, b, :, 0:H], ALU.add).then_inc(h_ready, 1)
                else:
                    wake(dve, outp, it * QN + QN, w_dve)
                    if not first(it, 2):
                        wake(dve, z_ready, it - 1, w_dve)
                    dve.tensor_tensor(tiled(h[:, b, :], G), tiled(pO[b][:, :], G), over_rows(rb, NP, G), ALU.add).then_inc(h_ready, 1)
                wake(dve, h_ready, it + 1, w_dve)
                row_sum(la, SUM, 0, tiled(h[:, b, :], G))

            def z_sum(it, b, which):
                wake(dve, z_ready, it + 1, w_dve)
                row_sum(lb, SUM, which, tiled(z[:, b, :], G))

            def z_squares(it, link, which):
                wake(dve, zsq, it + 1, w_dve)
                row_sum(link, SQUARES, which, tiled(sq[:, :], G))

            def z_norm(it, b, k, which):
                if not first(it, 2):
                    wake(dve, store[b], k * 16, w_dve)
                normalise(which, z[:, b, :], y[:, b, :, :], y_ready)

            if update:
                for it, b, k in steps(dve):
                    la.start(it)
                    h_sum(it, b, k)
                    if not first(it, 1):
                        lb.start(it - 1)
                        z_sum(it - 1, 1 - b, 1)
                    wake(dve, hsqd, it + 1, w_dve)
                    row_sum(la, SQUARES, 0, tiled(hsq[:, :], G))
                    if not first(it, 1):
                        z_squares(it - 1, lb, 1)
                    variance(la, slice(0, 2))
                    if not first(it, 2):
                        wake(dve, z_ready, it - 1, w_dve)
                    wake(dve, rstd_ready, it + 1, w_dve)
                    normalise(0, h[:, b, :], tiled(d[:, b, :], G), d_ready)
                    if not first(it, 1):
                        z_norm(it - 1, 1 - b, k - 1 if b == 0 else k, 1)
                la.start(STEPS)
                lb.start(STEPS - 1)
                z_sum(STEPS - 1, 1, 1)
                z_squares(STEPS - 1, lb, 1)
                variance(la, slice(0, 2))
                wake(dve, rstd_ready, STEPS + 1, w_dve)
                z_norm(STEPS - 1, 1, STEPS // 2 - 1, 1)
            else:
                for it, b, k in steps(dve):
                    la.start(it)
                    wake(dve, z_ready, it + 1, w_dve)
                    row_sum(la, SUM, b, tiled(z[:, b, :], G))
                    if not first(it, 1):
                        wake(dve, rstd_ready, it, w_dve)
                        z_norm(it - 1, 1 - b, k - 1 if b == 0 else k, 1 - b)
                    z_squares(it, la, b)
                    variance(la, slice(b, b + 1))
                wake(dve, rstd_ready, STEPS, w_dve)
                z_norm(STEPS - 1, 1, STEPS // 2 - 1, 1)


def program(nc, inputs, out):
    g = {"in": inputs}
    with ExitStack() as ctx:
        sb, ps, sem = scope(nc, ctx)
        for name, shape in (("ident", [P, P]), ("w_msg1", [2 * H, H]), ("w_msg1e", [ED, H]), ("w_msg2", [H, H]),
                            ("w_upd1", [2 * H, H]), ("w_upd2", [H + 1, H]), ("w_out", [2 * H, H]), ("w_conv0", [H, H]),
                            ("w_conv1", [H, H]), ("w_conv2", [H, H]), ("wq", [P, H]), ("wk", [P, H]), ("wv", [P, H]),
                            ("head_sum", [H, P]), ("norm_src", [P, TILES]), ("norm_dst", [P, TILES])):
            g[name] = sb(name, shape)
        for name in ("b_msg1", "b_msg2", "b_upd1", "b_q", "b_k", "b_v"):
            g[name] = sb(name, [H, 1])
        for name in ("r_g", "r_b", "r_gamma", "r_beta", "r_bf", "r_bo", "r_c0", "r_c1", "r_c2"):
            g[name] = sb(name, [P, H])
        for name in ("edge_id", "scat_dst", "dst_id", "edge_id2", "scat_src", "slot_row", "scat_dst_agg", "dst_x", "src_x"):
            g[name] = sb(name, [P, TILES], I32)
        g["record"] = sb("record_of_slot", [P, TILES, ED + 1], I32)
        g["src_row"] = sb("src_row", [P, TILES, 1], I32)
        g["dst_id2"] = sb("dst_id2", [P, TILES, 1], I32)
        dram = lambda name, shape, dt=F32: nc.dram_tensor(name, shape, dt, kind="Internal").ap()
        g["words"] = dram("sort_words", (2, SLOTS + 8), I32)
        g["keep"] = dram("keep", (2, SLOTS + 8))
        g["records"] = dram("records", (E, ED + 1), I32)
        g["edge_row"] = dram("edge_row", (N, 1), I32)
        for name in ("A2", "A3", "X2", "X3"):
            g[name] = dram(name, (N, H))
        for name in ("XA0", "XA1"):
            g[name] = dram(name, (N, 2 * H))
        for name in ("H1", "H2"):
            g[name] = dram(name, (ROWS + 1, H))

        load_constants(nc, g)
        sort_edges(nc, g)
        gather_pass(nc, g, g["records"], ED + 1, g["edge_id"], g["record"], I32, fill=(("A2", None), ("A3", "r_c2")))
        messages(nc, g)
        dense(nc, g, "mlp", g["XA0"], None, g["XA1"])
        attention(nc, g)
        dense(nc, g, "attend", g["XA1"], None, g["X2"])
        gather_pass(nc, g, inputs["dst"], 1, g["edge_id2"], g["dst_id2"], I32)
        spread(nc, g, g["X2"], g["dst_id2"][:, :, 0], 1, scatter_to=g["A2"], scatter_ix=g["scat_src"])
        dense(nc, g, "add", g["X2"], g["A2"], g["X3"])
        scatter_rows_of_nodes(nc, g)
        gather_pass(nc, g, g["edge_row"], 1, g["record"][:, :, ED], g["src_row"], I32)
        spread(nc, g, g["X3"], g["record"][:, :, ED], 0, g["w_conv0"], g["r_c0"], relu=True, rows_to=g["H1"])
        spread(nc, g, g["H1"], g["src_row"][:, :, 0], 0, g["w_conv1"], g["r_c1"], relu=True, rows_to=g["H2"])
        spread(nc, g, g["H2"], g["src_row"][:, :, 0], 0, g["w_conv2"], g["r_c2"], scatter_to=g["A3"], scatter_ix=g["scat_dst"])
        dense(nc, g, "add", g["X3"], g["A3"], out)


def kernel(**inputs):
    import numpy as np
    import concourse.bacc as bacc
    from concourse.bass_utils import run_bass_kernel_spmd as run

    nc = bacc.Bacc("TRN2", target_bir_lowering=False, num_devices=1)
    slot = np.arange(SLOTS).reshape(P, SW)
    bit = lambda k: 1.0 - 2.0 * ((slot >> k) & 1)
    signs = np.stack([bit(k) * (bit(k - 1) if k > 1 else 1.0) for k in range(1, LOGS + 1)], 1)
    head = np.arange(H) // HD
    head_sum = (head[:, None] == head[None, :]) / float(np.sqrt(H))
    arrays = {n: np.asarray(a) for n, a in inputs.items()}
    for n in ("src", "dst"):
        arrays[n] = arrays[n].reshape(E, 1)
    arrays["x_norm"] = np.concatenate([arrays["x"], arrays.pop("node_vec").reshape(N, 1)], axis=1)
    arrays["signs"] = signs.reshape(P, LOGS * SW).astype(np.float32)
    arrays["eye"] = np.eye(P, dtype=np.float32)
    arrays["head_sum"] = np.concatenate([head_sum, head_sum], axis=1).astype(np.float32)
    aps = {n: nc.dram_tensor("in_" + n, a.shape, mybir.dt.from_np(a.dtype), kind="ExternalInput").ap() for n, a in arrays.items()}
    out = nc.dram_tensor("out", (N, H), F32, kind="ExternalOutput").ap()
    program(nc, aps, out)
    r = run(nc, [{"in_" + n: a for n, a in arrays.items()}], core_ids=[0])
    return r.results[0]["out"]
```

```python
import concourse.bass as bass
from concourse import mybir
from contextlib import ExitStack
import itertools

F32 = mybir.dt.float32
I32 = mybir.dt.int32
BF16 = mybir.dt.bfloat16
ALU = mybir.AluOpType
ACT = mybir.ActivationFunctionType
AX = mybir.AxisListType

N = 100000
E = 25000
H = 64
ED = 32
HEADS = 4
HD = H // HEADS
EPS = 1e-5
P = 128

SW = 256
SLOTS = P * SW
LOGS = 15
LOGW = 8
IDB = 15
HALF = N // 2
PADKEY = 115000
FAR = float(1 << 20)

SORT_STEPS = 28

CT = 4
STEPS = 50
TILES = STEPS * CT
CW = CT * P
ROWS = STEPS * CW

W = H + 2
XC = slice(2, 2 + H)
AC = slice(W, W + H)
CATC = slice(2, 2 + 2 * H)
RC = W + H

NP = 125
NPP = N // NP
G = NPP // STEPS
DW = G * H
QN = 4
QW = (G // QN) * NP


def steps(eng, peeled=2):
    for it in range(peeled):
        yield it, it % 2, it // 2
    with eng.Fori(0, (STEPS - peeled) // 2) as i:
        yield i * 2 + peeled, 0, i + peeled // 2
        yield i * 2 + (peeled + 1), 1, i + peeled // 2


def wake(eng, sem, value, woke):
    eng.wait_ge(sem, value)
    eng.sem_inc(woke, 1)


class Chain:

    def __init__(self, eng, sem, links=0):
        self.eng, self.sem, self.links, self.step, self.n = eng, sem, links, 0, 0

    def start(self, step):
        assert self.n in (0, self.links), (self.n, self.links)
        self.step, self.n = step, 0

    def __call__(self, ins):
        self.n += 1
        ins.then_inc(self.sem, 1)
        self.eng.wait_ge(self.sem, self.step * self.links + self.n)


SCOPES = itertools.count()


def scope(nc, ctx):
    n = next(SCOPES)
    used = []

    def sem(name):
        used.append(nc.alloc_semaphore(f"{name}_{n}"))
        return used[-1]

    def clear():
        if used:
            nc.clear_and_free_semaphores(used)
            nc.all_engine_barrier()

    ctx.callback(clear)
    sb = lambda name, shape, dt=F32: ctx.enter_context(nc.sbuf_tensor(f"{name}_{n}", shape, dt))
    ps = lambda name, shape: ctx.enter_context(nc.psum_tensor(f"{name}_{n}", shape, F32))
    return sb, ps, sem


def rows_of(table):
    return table.rearrange("(p n) h -> p (n h)", p=NP)


def halves(table):
    return table.rearrange("n (two h) -> (n two) h", two=2)


def over_tiles(col, width, n):
    return col.unsqueeze(2).to_broadcast([col.shape[0], n, width])


def over_rows(vec, parts, n):
    return vec[0:parts, :].unsqueeze(1).to_broadcast([parts, n, H])


def tiled(ap, n):
    return ap.rearrange("p (n h) -> p n h", n=n)


def load_constants(nc, g):
    with ExitStack() as ctx:
        sb, ps, sem = scope(nc, ctx)
        loaded = sem("constants_loaded")
        zeroed = sem("weights_zeroed")
        block = ctx.enter_context(nc.Block())
        a = g["in"]
        plain = [("ident", "eye", P, H * 2), ("signs", "signs", P, LOGS * SW)]

        @block.vector
        def _(dve):
            dve.memset(g["wk"][:, :], 0.0)
            dve.memset(g["wv"][:, :], 0.0)
            dve.memset(g["wq"][:, :], 0.0).then_inc(zeroed, 1)

        @block.sync
        def _(sp):
            n = [0]

            def load(dst, src):
                n[0] += 16
                sp.dma_start(dst, src).then_inc(loaded, 16)

            load(g["ident"][:, :], a["eye"])
            load(g["w_msg1"][:, :], a["L0_gnn_msg_w1"][0:2 * H, :])
            load(g["w_msg1e"][:, :], a["L0_gnn_msg_w1"][2 * H:2 * H + ED, :])
            load(g["w_msg2"][:, :], a["L0_gnn_msg_w2"])
            load(g["w_upd1"][:, :], a["L0_gnn_upd_w1"])
            load(g["w_upd2"][0:H, :], a["L0_gnn_upd_w2"])
            load(g["w_upd2"][H:H + 1, :], a["L0_gnn_upd_b2"].rearrange("(a h) -> a h", a=1))
            load(g["w_out"][0:H, :], a["L1_gnn_Wf"])
            load(g["w_out"][H:2 * H, :], a["L1_gnn_Wo"])
            for k in range(3):
                load(g[f"w_conv{k}"][:, :], a[f"L3_gnn_W{k}"])
            load(g["head_sum"][:, :], a["head_sum"])
            for col, name in (("b_msg1", "L0_gnn_msg_b1"), ("b_msg2", "L0_gnn_msg_b2"), ("b_upd1", "L0_gnn_upd_b1"),
                              ("b_q", "L1_gnn_bq"), ("b_k", "L1_gnn_bk"), ("b_v", "L1_gnn_bv")):
                load(g[col][:, :], a[name].rearrange("(h a) -> h a", a=1))
            for row, name in (("r_g", "L0_gnn_ln_g"), ("r_b", "L0_gnn_ln_b"), ("r_gamma", "L1_gnn_gamma"),
                              ("r_beta", "L1_gnn_beta"), ("r_bf", "L1_gnn_bf"), ("r_bo", "L1_gnn_bo"),
                              ("r_c0", "L3_gnn_b0"), ("r_c1", "L3_gnn_b1"), ("r_c2", "L3_gnn_b2")):
                load(g[row][:, :], a[name].partition_broadcast(P))
            sp.wait_ge(zeroed, 1)
            load(g["wk"][0:H, :], a["L1_gnn_Wk"])
            load(g["wv"][0:H, :], a["L1_gnn_Wv"])
            load(g["wq"][H:2 * H, :], a["L1_gnn_Wq"])
            sp.wait_ge(loaded, n[0])


class XTables:

    def __init__(self, nc, g, sb, sem, begin, end):
        self.g, self.begin, self.end = g, begin, end
        self.x_in = sb("x_in", [NP, 2, DW])
        self.pair = sb("pair", [NP, 2, G, 2 * W])
        self.blanked, self.copied, self.woke, self.act_woke = sem("pair_blank"), sem("x_copied"), sem("x_load_woke"), sem("x_copy_woke")
        self.loaded = [sem("x_loaded_even"), sem("x_loaded_odd")]
        self.stored = [sem("pair_stored_even"), sem("pair_stored_odd")]

    def steps(self, eng):
        assert (self.end - self.begin) % 2 == 0
        for n in range(2):
            yield self.begin + n, n, n, 0
        with eng.Fori(1, (self.end - self.begin) // 2) as i:
            for b in range(2):
                yield i * 2 + (self.begin + b), i * 2 + b, b, i

    def blank(self, eng):
        pair = self.pair
        eng.memset(pair[:, :, :, 0:2], 0.0)
        eng.memset(pair[:, :, :, AC], 0.0)
        eng.memset(pair[:, :, :, RC:RC + 1], float(ROWS))
        eng.memset(pair[:, :, :, RC + 1:2 * W], 0.0).then_inc(self.blanked, 1)

    def load(self, eng):
        for it, n, b, k in self.steps(eng):
            if not first(n, 2):
                wake(eng, self.copied, n - 1, self.woke)
            eng.dma_start(self.x_in[:, b, :], rows_of(self.g["in"]["x"])[:, bass.ds(it * DW, DW)]).then_inc(self.loaded[b], 16)

    def build(self, act):
        act.wait_ge(self.blanked, 1)
        for it, n, b, k in self.steps(act):
            wake(act, self.loaded[b], (k + 1) * 16, self.act_woke)
            if not first(n, 2):
                wake(act, self.stored[b], k * 16, self.act_woke)
            act.activation(self.pair[:, b, :, XC], tiled(self.x_in[:, b, :], G), ACT.Copy).then_inc(self.copied, 1)
            act.wait_ge(self.copied, n + 1)
            act.dma_start(rows_of(self.g["XA0"])[:, bass.ds(it * (2 * G * W), 2 * G * W)],
                          self.pair[:, b, :, :].rearrange("p n h -> p (n h)")).then_inc(self.stored[b], 16)
        for b in range(2):
            act.wait_ge(self.stored[b], 8 * (self.end - self.begin))


def sort_edges(nc, g):
    with ExitStack() as ctx:
        sb, ps, sem = scope(nc, ctx)
        keys = sb("keys", [P, 2, SW], I32)
        ids = sb("ids", [P, 2, SW], I32)
        tmp = sb("tmp", [P, 2, SW], I32)
        tmp2 = sb("tmp2", [P, 2, SW], I32)
        tmp3 = sb("tmp3", [P, 2, SW], I32)
        nxt = sb("nxt", [P, 2, SW], I32)
        same = sb("same", [P, 2, SW])
        flt = sb("flt", [P, 2, 3, SW])
        bufs = (sb("bufA", [P, 2 * SW]), sb("bufB", [P, 2 * SW]))
        signs = sb("signs", [P, LOGS, SW])
        zero1 = sb("zero1", [1, 8], I32)
        EPP = E // NP
        record = sb("record", [NP, EPP, ED + 1], I32)
        srcs = sb("srcs", [NP, EPP], I32)
        tables = XTables(nc, g, sb, sem, 0, SORT_STEPS)
        ident = g["ident"]
        pT = ps("pT", [P, 2 * SW])
        pU = [ps(f"pU{n}", [P, SW]) for n in range(5)]
        s_pad, s_keys, s_ids, s_const = sem("keys_padded"), sem("keys_loaded"), sem("ids_ready"), sem("signs_loaded")
        s_dve, s_turn, s_turned, s_words = sem("dve_step"), sem("turn_ready"), sem("turned"), sem("words_stored")
        s_zero, s_next, s_same, s_keep = sem("zero_ready"), sem("next_loaded"), sem("same_ready"), sem("keep_stored")
        s_flt, s_cols, s_wr, s_out = sem("floats_ready"), sem("columns_turned"), sem("words_ready"), sem("columns_kept")
        s_rec, s_recs, s_joined = sem("record_loaded"), sem("record_stored"), sem("record_joined")
        block = ctx.enter_context(nc.Block())
        OUTS = (("edge_id", 0, 0), ("scat_dst", 0, 1), ("dst_id", 0, 2), ("edge_id2", 1, 0), ("scat_src", 1, 1))

        @block.sync
        def _(sp):
            sp.wait_ge(s_pad, 1)
            full = E // SW
            for q, name in enumerate(("dst", "src")):
                k = g["in"][name]
                sp.dma_start(keys[0:full, q, :], k[0:full * SW, :].rearrange("(p f) a -> p (f a)", f=SW)).then_inc(s_keys, 16)
                sp.dma_start(keys[full:full + 1, q, 0:E - full * SW],
                             k[full * SW:E, :].rearrange("(p f) a -> p (f a)", p=1)).then_inc(s_keys, 16)
            sp.dma_start(signs[:, :, :], g["in"]["signs"].rearrange("p (k f) -> p k f", k=LOGS)).then_inc(s_const, 16)
            sp.dma_start(record[:, :, 0:ED], g["in"]["edge_attr_32"].bitcast(I32).rearrange("(p e) f -> p e f", p=NP)).then_inc(s_rec, 16)
            sp.dma_start(srcs[:, :], g["in"]["src"].rearrange("(p e) a -> p (e a)", p=NP)).then_inc(s_rec, 16)
            sp.wait_ge(s_zero, 1)
            for q in range(2):
                sp.dma_start(g["words"][q:q + 1, SLOTS:SLOTS + 8], zero1[0:1, :]).then_inc(s_words, 16)
                sp.dma_start(g["keep"][q:q + 1, 0:1], zero1[0:1, 0:1].bitcast(F32)).then_inc(s_keep, 16)
            sp.wait_ge(s_joined, 1)
            sp.dma_start(g["records"].rearrange("(p e) f -> p (e f)", p=NP), record[:, :, :].rearrange("p e f -> p (e f)")).then_inc(s_recs, 16)
            sp.wait_ge(s_wr, 1)
            for q in range(2):
                sp.dma_start(g["words"][q, 0:SLOTS].rearrange("(p f) -> p f", f=SW),
                             bufs[0][:, q * SW:(q + 1) * SW].bitcast(I32)).then_inc(s_words, 16)
            sp.wait_ge(s_words, 64)
            for q in range(2):
                sp.dma_start(nxt[:, q, :], g["words"][q, 1:SLOTS + 1].rearrange("(p f) -> p f", f=SW)).then_inc(s_next, 16)
            sp.wait_ge(s_same, 1)
            for q in range(2):
                sp.dma_start(g["keep"][q, 1:SLOTS + 1].rearrange("(p f) -> p f", f=SW), same[:, q, :]).then_inc(s_keep, 16)
            sp.wait_ge(s_recs, 16)
            sp.wait_ge(s_keep, 64)

        @block.scalar
        def _(act):
            tables.build(act)

        @block.gpsimd
        def _(pool):
            tables.blank(pool)
            for q in range(2):
                pool.iota(ids[:, q, :], pattern=[[1, SW]], base=0, channel_multiplier=SW).then_inc(s_ids, 1)
            pool.iota(g["slot_row"][:, :].rearrange("p (c t) -> p c t", t=CT), pattern=[[CW, STEPS], [1, CT]], base=0, channel_multiplier=CT)
            pool.wait_ge(s_rec, 32)
            pool.tensor_copy(record[:, :, ED:ED + 1], srcs[:, :].unsqueeze(2)).then_inc(s_joined, 1)
            tables.load(pool)

        TURNS, at = [], 0
        for k in range(1, LOGS + 1):
            at += 1
            if k > LOGW:
                TURNS.append(at % 2)
                at += 1 + k - LOGW
                TURNS.append(at % 2)
                at += 1
            at += min(k, LOGW)

        @block.tensor
        def _(pe):
            for n in range(2 * (LOGS - LOGW)):
                pe.wait_ge(s_turn, n + 1)
                src = bufs[TURNS[n]]
                for b in range(4):
                    last = pe.transpose(pT[:, b * P:(b + 1) * P], src[:, b * P:(b + 1) * P], ident[:, :])
                last.then_inc(s_turned, 1)
            pe.wait_ge(s_flt, 1)
            for n, (_, q, a) in enumerate(OUTS):
                for b in range(2):
                    last = pe.transpose(pU[n][:, b * P:(b + 1) * P], flt[:, q, a, b * P:(b + 1) * P], ident[:, :])
            last.then_inc(s_cols, 1)

        @block.vector
        def _(dve):
            link = Chain(dve, s_dve)
            dve.memset(keys[:, :, :], PADKEY).then_inc(s_pad, 1)
            dve.memset(zero1[:, :], 0).then_inc(s_zero, 1)
            dve.wait_ge(s_keys, 64)
            link(dve.tensor_scalar(tmp[:, :, :], keys[:, :, :], HALF, None, ALU.is_lt))
            link(dve.tensor_scalar(tmp2[:, :, :], tmp[:, :, :], HALF, 256 - HALF, ALU.mult, ALU.add))
            link(dve.tensor_tensor(tmp3[:, :, :], keys[:, :, :], tmp2[:, :, :], ALU.add))
            link(dve.tensor_scalar(tmp3[:, :, :], tmp3[:, :, :], IDB, None, ALU.logical_shift_left))
            link(dve.tensor_scalar(tmp[:, :, :], tmp[:, :, :], 31, None, ALU.logical_shift_left))
            link(dve.tensor_tensor(tmp[:, :, :], tmp[:, :, :], tmp3[:, :, :], ALU.bitwise_or))
            dve.wait_ge(s_ids, 2)
            link(dve.tensor_tensor(bufs[0][:, :].bitcast(I32).rearrange("p (q f) -> p q f", q=2), tmp[:, :, :], ids[:, :, :], ALU.bitwise_or))
            dve.wait_ge(s_const, 16)
            at = turns = 0

            def exchange(src, dst, stride):
                v = src[:, :].rearrange("p (b two s) -> p b two s", two=2, s=stride)
                o = dst[:, :].rearrange("p (b two s) -> p b two s", two=2, s=stride)
                dve.tensor_tensor(o[:, :, 0, :], v[:, :, 0, :], v[:, :, 1, :], ALU.min)
                link(dve.tensor_tensor(o[:, :, 1, :], v[:, :, 0, :], v[:, :, 1, :], ALU.max))

            for k in range(1, LOGS + 1):
                s = signs[:, k - 1, :].unsqueeze(1).to_broadcast([P, 2, SW])
                link(dve.tensor_tensor(bufs[1 - at][:, :].rearrange("p (q f) -> p q f", q=2),
                                       bufs[at][:, :].rearrange("p (q f) -> p q f", q=2), s, ALU.mult))
                at = 1 - at
                if k > LOGW:
                    dve.sem_inc(s_turn, 1)
                    turns += 1
                    dve.wait_ge(s_turned, turns)
                    link(dve.tensor_copy(bufs[1 - at][:, :], pT[:, :]))
                    at = 1 - at
                    for b in range(k - 1, LOGW - 1, -1):
                        exchange(bufs[at], bufs[1 - at], 1 << (b - LOGW))
                        at = 1 - at
                    dve.sem_inc(s_turn, 1)
                    turns += 1
                    dve.wait_ge(s_turned, turns)
                    link(dve.tensor_copy(bufs[1 - at][:, :], pT[:, :]))
                    at = 1 - at
                for b in range(min(k, LOGW) - 1, -1, -1):
                    exchange(bufs[at], bufs[1 - at], 1 << b)
                    at = 1 - at
            if at:
                link(dve.tensor_copy(bufs[0][:, :], bufs[1][:, :]))
            dve.sem_inc(s_wr, 1)
            w = bufs[0][:, :].bitcast(I32).rearrange("p (q f) -> p q f", q=2)
            link(dve.tensor_scalar(tmp[:, :, :], w, 31, None, ALU.logical_shift_right))
            link(dve.tensor_scalar(tmp2[:, :, :], tmp[:, :, :], -HALF, HALF - 256, ALU.mult, ALU.add))
            link(dve.tensor_scalar(tmp3[:, :, :], w, IDB, 0xFFFF, ALU.logical_shift_right, ALU.bitwise_and))
            link(dve.tensor_tensor(keys[:, :, :], tmp2[:, :, :], tmp3[:, :, :], ALU.add))
            link(dve.tensor_scalar(tmp[:, :, :], w, (1 << IDB) - 1, None, ALU.bitwise_and))
            link(dve.tensor_scalar(flt[:, :, 0, :], tmp[:, :, :], E - 1, None, ALU.min))
            link(dve.tensor_scalar(flt[:, :, 2, :], keys[:, :, :], N - 1, None, ALU.min))
            link(dve.tensor_scalar(tmp3[:, :, :], w, IDB, 0x1FFFF, ALU.logical_shift_right, ALU.bitwise_and))
            dve.wait_ge(s_next, 32)
            link(dve.tensor_scalar(nxt[:, :, :], nxt[:, :, :], IDB, 0x1FFFF, ALU.logical_shift_right, ALU.bitwise_and))
            link(dve.tensor_tensor(same[:, :, :], nxt[:, :, :], tmp3[:, :, :], ALU.is_equal))
            dve.sem_inc(s_same, 1)
            link(dve.scalar_tensor_tensor(flt[:, :, 1, :], same[:, :, :], FAR, keys[:, :, :], ALU.mult, ALU.add))
            dve.sem_inc(s_flt, 1)
            dve.wait_ge(s_cols, 1)
            for n, (name, _, _) in enumerate(OUTS):
                dve.tensor_copy(g[name][:, :].rearrange("p (t b) -> p t b", b=2),
                                pU[n][:, :].rearrange("p (b t) -> p t b", b=2)[:, 0:TILES // 2, :]).then_inc(s_out, 1)
            dve.wait_ge(s_out, len(OUTS))
            dve.tensor_scalar(g["scat_dst_agg"][:, :], g["scat_dst"][:, :], 2.0, 1.0, ALU.mult, ALU.add)
            dve.tensor_scalar(g["dst_x"][:, :], g["dst_id"][:, :], 2.0, None, ALU.mult)


def stage(pool, ix, slot, index, it, ready, woke):
    pool.tensor_copy(ix[:, slot, :], index[:, bass.ds(it * CT, CT)]).then_inc(ready, 1)


def gather_rows(pool, dst, table, ix, slot, sem):
    for t in range(CT):
        pool.indirect_dma_start(dst(t), None, table, bass.IndirectOffsetOnAxis(ix[:, slot, t:t + 1], 0)).then_inc(sem, 16)


def scatter_rows(pool, table, src, ix, slot, sem):
    for t in range(CT):
        pool.indirect_dma_start(table, bass.IndirectOffsetOnAxis(ix[:, slot, t:t + 1], 0), src(t), None,
                                bounds_check=table.shape[0] - 1, oob_is_err=False).then_inc(sem, 16)


def fetch_records(nc, g):
    with ExitStack() as ctx:
        sb, ps, sem = scope(nc, ctx)
        buf = sb("gathered", [P, 2, CT, ED + 1], I32)
        ix = sb("index", [P, 2, CT], I32)
        tables = XTables(nc, g, sb, sem, SORT_STEPS, STEPS)
        got = [sem("rows_gathered_even"), sem("rows_gathered_odd")]
        ix_ready, w_pool, w_dve, kept = sem("index_staged"), sem("pool_woke"), sem("dve_woke"), sem("rows_kept")
        block = ctx.enter_context(nc.Block())

        @block.gpsimd
        def _(pool):
            for it, b, k in steps(pool):
                if not first(it, 2):
                    wake(pool, kept, it - 1, w_pool)
                stage(pool, ix, b, g["edge_id"], it, ix_ready, w_pool)
                wake(pool, ix_ready, it + 1, w_pool)
                gather_rows(pool, lambda t: buf[:, b, t, :], g["records"], ix, b, got[b])

        @block.vector
        def _(dve):
            tables.blank(dve)
            for it, b, k in steps(dve):
                wake(dve, got[b], (k + 1) * (16 * CT), w_dve)
                dve.tensor_copy(g["record"][:, bass.ds(it * CT, CT), :], buf[:, b, :, :]).then_inc(kept, 1)

        @block.sync
        def _(sp):
            tables.load(sp)

        @block.scalar
        def _(act):
            tables.build(act)


def first(it, n):
    return isinstance(it, int) and it < n


def scatter_steps(pool, gather, scatter):
    for it, b, k in steps(pool, 4):
        gather(it, b, k)
        if not first(it, 2):
            scatter(it - 2, b, k - 1)
    for it in (STEPS - 2, STEPS - 1):
        scatter(it, it % 2, it // 2)


def load_keep(sp, g, row, parts, keep, loaded, used, dma=None):
    for it, b, k in steps(sp):
        if not first(it, 2):
            sp.wait_ge(used, it - 1)
        sp.dma_start(keep[:, b, :], g["keep"][row, bass.ds(it * CW, CW)].partition_broadcast(parts)).then_inc(loaded[b], 16)
        if dma:
            dma(it, b, k)


def messages(nc, g):
    with ExitStack() as ctx:
        sb, ps, sem = scope(nc, ctx)
        ends = sb("ends", [P, 2, CT, 2, H + 1])
        pair = sb("pair", [P, CT, 2 * H])
        ea = sb("edge_features", [P, 2, CT, ED], I32)
        tile = sb("fill_tile", [NP, 2, DW])
        ix = sb("ix", [P, 3, 2, CT], I32)
        catT = sb("catT", [P, CW])
        eaT = sb("eaT", [ED, CW])
        hT = sb("hT", [H, CW])
        mT = sb("mT", [H, CW])
        keep = sb("keep_row", [H, 2, CW])
        run = sb("running", [H, 2, CW])
        rows = sb("sum_rows", [P, 2, CT, W])
        pT = [ps("pT0", [P, CW]), ps("pT1", [P, CW])]
        pE = ps("pE", [ED, CW])
        pH = ps("pH", [H, CW])
        pM = ps("pM", [H, CW])
        pB = ps("pB", [P, CT * H])
        got = [sem("ends_gathered_even"), sem("ends_gathered_odd")]
        sent = [sem("sums_scattered_even"), sem("sums_scattered_odd")]
        loaded = [sem("keep_loaded_even"), sem("keep_loaded_odd")]
        ix_ready, turned, cat, eat, hid, act_h, msg, act_m = (sem(n) for n in (
            "index_staged", "ends_turned", "cat_copied", "features_copied", "hidden_summed", "hidden_ready", "message_summed", "message_ready"))
        scanned, back, rows_ready, norms, ea_ready = (sem(n) for n in (
            "scanned", "sums_turned_back", "sum_rows_ready", "norms_kept", "features_staged"))
        w_pool, w_pe, w_dve = sem("pool_woke"), sem("pe_woke"), sem("dve_woke")
        paired, tiles_ready, filled = sem("ends_paired"), sem("fill_ready"), sem("filled")
        block = ctx.enter_context(nc.Block())
        src_ix = g["record"][:, :, ED:ED + 1]

        @block.gpsimd
        def _(pool):
            def gather(it, b, k):
                if not first(it, 2):
                    wake(pool, paired, it - 1, w_pool)
                    wake(pool, norms, it - 1, w_pool)
                pool.tensor_copy(ix[:, 0, b, :].unsqueeze(2), src_ix[:, bass.ds(it * CT, CT), :]).then_inc(ix_ready, 1)
                pool.tensor_copy(ix[:, 1, b, :], g["dst_id"][:, bass.ds(it * CT, CT)]).then_inc(ix_ready, 1)
                wake(pool, ix_ready, staged(it, 0), w_pool)
                gather_rows(pool, lambda t: ends[:, b, t, 0, :], g["in"]["x_norm"], ix[:, 0], b, got[b])
                gather_rows(pool, lambda t: ends[:, b, t, 1, :], g["in"]["x_norm"], ix[:, 1], b, got[b])

            def staged(it, scatter):
                if scatter:
                    return 2 * STEPS + it + 1 if isinstance(it, int) and it >= STEPS - 2 else it * 3 + 7
                return 2 * it + 2 if first(it, 2) else it * 3

            def scatter(it, b, k):
                if not first(it, 2):
                    wake(pool, sent[b], k * (16 * CT), w_pool)
                pool.tensor_copy(ix[:, 2, b, :], g["scat_dst_agg"][:, bass.ds(it * CT, CT)]).then_inc(ix_ready, 1)
                wake(pool, ix_ready, staged(it, 1), w_pool)
                wake(pool, rows_ready, it + 1, w_pool)
                scatter_rows(pool, halves(g["XA0"]), lambda t: rows[:, b, t, :], ix[:, 2], b, sent[b])

            scatter_steps(pool, gather, scatter)
            for b in range(2):
                pool.wait_ge(sent[b], 16 * CT * STEPS // 2)

        @block.sync
        def _(sp):
            def fill(it, b, k):
                for n, name in enumerate(("A2", "A3")):
                    sp.dma_start(rows_of(g[name])[:, bass.ds(it * DW, DW)], tile[:, n, :]).then_inc(filled, 16)

            sp.wait_ge(tiles_ready, 1)
            load_keep(sp, g, 0, H, keep, loaded, scanned, fill)
            sp.wait_ge(filled, 16 * 2 * STEPS)
            for b in range(2):
                sp.wait_ge(loaded[b], 16 * STEPS // 2)

        @block.tensor
        def _(pe):
            for it, b, k in steps(pe):
                wake(pe, paired, it + 1, w_pe)
                wake(pe, ea_ready, it + 1, w_pe)
                for t in range(CT):
                    pe.transpose(pT[b][:, t * P:(t + 1) * P], pair[:, t, :], g["ident"][:, :])
                for t in range(CT):
                    last = pe.transpose(pE[:, t * P:(t + 1) * P], ea[:, b, t, :].bitcast(F32), g["ident"][:, :])
                last.then_inc(turned, 1)
                wake(pe, cat, it + 1, w_pe)
                pe.matmul(pH[:, :], g["w_msg1"][:, :], catT[:, :], start=True, stop=False)
                wake(pe, eat, it + 1, w_pe)
                pe.matmul(pH[:, :], g["w_msg1e"][:, :], eaT[:, :], start=False, stop=True).then_inc(hid, 1)
                wake(pe, act_h, it + 1, w_pe)
                pe.matmul(pM[:, :], g["w_msg2"][:, :], hT[:, :], start=True, stop=True).then_inc(msg, 1)
                wake(pe, scanned, it + 1, w_pe)
                if not first(it, 1):
                    wake(pe, rows_ready, it, w_pe)
                for t in range(CT):
                    last = pe.transpose(pB[:, t * H:(t + 1) * H], run[:, b, t * P:(t + 1) * P], g["ident"][0:H, 0:H])
                last.then_inc(back, 1)

        @block.scalar
        def _(act):
            for it, b, k in steps(act):
                act.wait_ge(got[b], (k + 1) * (16 * 2 * CT))
                if not first(it, 1):
                    act.wait_ge(turned, it)
                act.activation(pair[:, :, :].rearrange("p t (e h) -> p t e h", e=2), ends[:, b, :, :, 0:H], ACT.Copy).then_inc(paired, 1)
                act.wait_ge(turned, it + 1)
                if not first(it, 1):
                    act.wait_ge(hid, it)
                act.activation(catT[:, :], pT[b][:, :], ACT.Copy).then_inc(cat, 1)
                act.wait_ge(hid, it + 1)
                if not first(it, 1):
                    act.wait_ge(msg, it)
                act.activation(hT[:, :], pH[:, :], ACT.Relu, bias=g["b_msg1"][:, 0:1]).then_inc(act_h, 1)
                act.wait_ge(msg, it + 1)
                if not first(it, 1):
                    act.wait_ge(scanned, it)
                act.activation(mT[:, :], pM[:, :], ACT.Identity, bias=g["b_msg2"][:, 0:1]).then_inc(act_m, 1)

        @block.vector
        def _(dve):
            dve.memset(rows[:, :, :, H:W], 0.0)
            dve.memset(tile[:, 0, :], 0.0)
            dve.tensor_copy(tiled(tile[:, 1, :], G), over_rows(g["r_c2"], NP, G)).then_inc(tiles_ready, 1)
            dve.tensor_scalar(g["src_x"][:, :], g["record"][:, :, ED], 2.0, None, ALU.mult)
            for it, b, k in steps(dve):
                if not first(it, 2):
                    wake(dve, turned, it - 1, w_dve)
                dve.tensor_copy(ea[:, b, :, :], g["record"][:, bass.ds(it * CT, CT), 0:ED]).then_inc(ea_ready, 1)
                wake(dve, got[b], (k + 1) * (16 * 2 * CT), w_dve)
                dve.tensor_copy(g["norm_src"][:, bass.ds(it * CT, CT)], ends[:, b, :, 0, H])
                dve.tensor_copy(g["norm_dst"][:, bass.ds(it * CT, CT)], ends[:, b, :, 1, H]).then_inc(norms, 1)
                wake(dve, turned, it + 1, w_dve)
                if not first(it, 1):
                    wake(dve, hid, it, w_dve)
                dve.tensor_copy(eaT[:, :], pE[:, :]).then_inc(eat, 1)
                wake(dve, act_m, it + 1, w_dve)
                wake(dve, loaded[b], (k + 1) * 16, w_dve)
                if not first(it, 1):
                    wake(dve, scanned, it, w_dve)
                if not first(it, 2):
                    wake(dve, back, it - 1, w_dve)
                dve.tensor_tensor_scan(run[:, b, :], keep[:, b, :], mT[:, :],
                                       0.0 if first(it, 1) else run[:, 1 - b, CW - 1:CW], ALU.mult, ALU.add).then_inc(scanned, 1)
                wake(dve, back, it + 1, w_dve)
                if not first(it, 2):
                    wake(dve, sent[b], k * (16 * CT), w_dve)
                dve.tensor_copy(rows[:, b, :, H], g["slot_row"][:, bass.ds(it * CT, CT)])
                dve.tensor_copy(rows[:, b, :, 0:H], tiled(pB[:, :], CT)).then_inc(rows_ready, 1)


def attention(nc, g):
    with ExitStack() as ctx:
        sb, ps, sem = scope(nc, ctx)
        ends = sb("ends", [P, 2, CT, 2, W])
        pair = sb("pair", [P, CT, 2 * H])
        ix = sb("ix", [P, 3, 2, CT], I32)
        catT = sb("catT", [P, CW])
        qT = sb("qT", [H, CW])
        prod = sb("prod", [H, CW])
        clip = sb("clip", [P, CW])
        e_low = sb("e_low", [H, CW])
        mz = sb("mz", [P, CW])
        keep = sb("keep_row", [P, 2, CW])
        run = sb("running", [P, 2, CW])
        z1 = sb("z1", [P, CT, H])
        rz = sb("rz", [P, CT, H])
        rows = sb("sum_rows", [P, 2, CT, W])
        pT = [ps("pT0", [P, CW]), ps("pT1", [P, CW])]
        pQ, pK, pV = ps("pQ", [H, CW]), ps("pK", [H, CW]), ps("pV", [H, CW])
        pS = ps("pS", [P, CW])
        pB = ps("pB", [P, CT * P])
        got = [sem("ends_gathered_even"), sem("ends_gathered_odd")]
        sent = [sem("sums_scattered_even"), sem("sums_scattered_odd")]
        loaded = [sem("keep_loaded_even"), sem("keep_loaded_odd")]
        ix_ready, turned, cat, qkv, q_ready, prod_ready, score, clipped, exped, weighed = (sem(n) for n in (
            "index_staged", "ends_turned", "cat_copied", "qkv_ready", "q_biased", "prod_ready", "score_summed", "score_clipped",
            "exp_ready", "values_weighed"))
        paired, kept = sem("ends_paired"), sem("src_rows_kept")
        scanned, back, rows_ready, s_dve = (sem(n) for n in ("scanned", "sums_turned_back", "sum_rows_ready", "dve_step"))
        w_pool, w_pe, w_dve = sem("pool_woke"), sem("pe_woke"), sem("dve_woke")
        block = ctx.enter_context(nc.Block())

        @block.gpsimd
        def _(pool):
            def staged(it, scatter):
                if scatter:
                    return 2 * STEPS + it + 1 if isinstance(it, int) and it >= STEPS - 2 else it * 3 + 7
                return 2 * it + 2 if first(it, 2) else it * 3

            def gather(it, b, k):
                if not first(it, 2):
                    wake(pool, paired, it - 1, w_pool)
                    wake(pool, kept, it - 1, w_pool)
                pool.tensor_copy(ix[:, 0, b, :], g["src_x"][:, bass.ds(it * CT, CT)]).then_inc(ix_ready, 1)
                pool.tensor_copy(ix[:, 1, b, :], g["dst_x"][:, bass.ds(it * CT, CT)]).then_inc(ix_ready, 1)
                wake(pool, ix_ready, staged(it, 0), w_pool)
                gather_rows(pool, lambda t: ends[:, b, t, 0, :], halves(g["XA1"]), ix[:, 0], b, got[b])
                gather_rows(pool, lambda t: ends[:, b, t, 1, :], halves(g["XA1"]), ix[:, 1], b, got[b])

            def scatter(it, b, k):
                if not first(it, 2):
                    wake(pool, sent[b], k * (16 * CT), w_pool)
                pool.tensor_copy(ix[:, 2, b, :], g["scat_dst_agg"][:, bass.ds(it * CT, CT)]).then_inc(ix_ready, 1)
                wake(pool, ix_ready, staged(it, 1), w_pool)
                wake(pool, rows_ready, it + 1, w_pool)
                scatter_rows(pool, halves(g["XA1"]), lambda t: rows[:, b, t, :], ix[:, 2], b, sent[b])

            scatter_steps(pool, gather, scatter)
            for b in range(2):
                pool.wait_ge(sent[b], 16 * CT * STEPS // 2)

        @block.sync
        def _(sp):
            load_keep(sp, g, 0, P, keep, loaded, scanned)
            for b in range(2):
                sp.wait_ge(loaded[b], 16 * STEPS // 2)

        @block.tensor
        def _(pe):
            for it, b, k in steps(pe):
                wake(pe, paired, it + 1, w_pe)
                for t in range(CT):
                    last = pe.transpose(pT[b][:, t * P:(t + 1) * P], pair[:, t, :], g["ident"][:, :])
                last.then_inc(turned, 1)
                wake(pe, cat, it + 1, w_pe)
                if not first(it, 1):
                    wake(pe, weighed, it, w_pe)
                pe.matmul(pQ[:, :], g["wq"][:, :], catT[:, :], start=True, stop=True).then_inc(qkv, 1)
                pe.matmul(pK[:, :], g["wk"][:, :], catT[:, :], start=True, stop=True).then_inc(qkv, 1)
                pe.matmul(pV[:, :], g["wv"][:, :], catT[:, :], start=True, stop=True).then_inc(qkv, 1)
                wake(pe, prod_ready, it + 1, w_pe)
                pe.matmul(pS[:, :], g["head_sum"][:, :], prod[:, :], start=True, stop=True).then_inc(score, 1)
                wake(pe, scanned, it + 1, w_pe)
                if not first(it, 1):
                    wake(pe, rows_ready, it, w_pe)
                for t in range(CT):
                    last = pe.transpose(pB[:, t * P:(t + 1) * P], run[:, b, t * P:(t + 1) * P], g["ident"][:, :])
                last.then_inc(back, 1)

        @block.scalar
        def _(act):
            for it, b, k in steps(act):
                act.wait_ge(got[b], (k + 1) * (16 * 2 * CT))
                if not first(it, 1):
                    act.wait_ge(turned, it)
                act.activation(pair[:, :, :].rearrange("p t (e h) -> p t e h", e=2), ends[:, b, :, :, XC], ACT.Copy).then_inc(paired, 1)
                act.wait_ge(turned, it + 1)
                if not first(it, 1):
                    act.wait_ge(qkv, it * 3)
                act.activation(catT[:, :], pT[b][:, :], ACT.Copy).then_inc(cat, 1)
                act.wait_ge(qkv, it * 3 + 1)
                if not first(it, 1):
                    act.wait_ge(prod_ready, it)
                act.activation(qT[:, :], pQ[:, :], ACT.Identity, bias=g["b_q"][:, 0:1]).then_inc(q_ready, 1)
                act.wait_ge(clipped, it + 1)
                if not first(it, 1):
                    act.wait_ge(scanned, it)
                act.activation(e_low[:, :], clip[0:H, :], ACT.Exp)
                act.activation(mz[H:P, :], clip[H:P, :], ACT.Exp).then_inc(exped, 1)

        @block.vector
        def _(dve):
            link = Chain(dve, s_dve, 2)
            dve.memset(rows[:, :, :, H:W], 0.0)
            for it, b, k in steps(dve):
                link.start(it)
                wake(dve, got[b], (k + 1) * (16 * 2 * CT), w_dve)
                dve.tensor_copy(g["src_row"][:, bass.ds(it * CT, CT)], ends[:, b, :, 0, 0]).then_inc(kept, 1)
                wake(dve, q_ready, it + 1, w_dve)
                wake(dve, qkv, it * 3 + 2, w_dve)
                if not first(it, 1):
                    wake(dve, score, it, w_dve)
                dve.scalar_tensor_tensor(prod[:, :], pK[:, :], g["b_k"][:, 0:1], qT[:, :], ALU.add, ALU.mult).then_inc(prod_ready, 1)
                wake(dve, score, it + 1, w_dve)
                if not first(it, 1):
                    wake(dve, exped, it, w_dve)
                dve.tensor_scalar(clip[:, :], pS[:, :], 5.0, -5.0, ALU.min, ALU.max).then_inc(clipped, 1)
                wake(dve, exped, it + 1, w_dve)
                wake(dve, qkv, it * 3 + 3, w_dve)
                dve.scalar_tensor_tensor(mz[0:H, :], pV[:, :], g["b_v"][:, 0:1], e_low[:, :], ALU.add, ALU.mult).then_inc(weighed, 1)
                wake(dve, weighed, it + 1, w_dve)
                wake(dve, loaded[b], (k + 1) * 16, w_dve)
                if not first(it, 1):
                    wake(dve, scanned, it, w_dve)
                if not first(it, 2):
                    wake(dve, back, it - 1, w_dve)
                dve.tensor_tensor_scan(run[:, b, :], keep[:, b, :], mz[:, :],
                                       0.0 if first(it, 1) else run[:, 1 - b, CW - 1:CW], ALU.mult, ALU.add).then_inc(scanned, 1)
                wake(dve, back, it + 1, w_dve)
                sums = pB[:, :].rearrange("p (t c) -> p t c", t=CT)
                link(dve.tensor_scalar(z1[:, :, :], sums[:, :, H:P], 1.0, None, ALU.add))
                link(dve.reciprocal(rz[:, :, :], z1[:, :, :]))
                if not first(it, 2):
                    wake(dve, sent[b], k * (16 * CT), w_dve)
                dve.tensor_tensor(rows[:, b, :, 0:H], sums[:, :, 0:H], rz[:, :, :], ALU.mult).then_inc(rows_ready, 1)


def lagged(eng):
    yield from steps(eng, 4)
    for it in (STEPS, STEPS + 1):
        yield it, it % 2, it // 2


def behind(it, b, k, lag):
    j = it - lag
    if isinstance(j, int) and not 0 <= j < STEPS:
        return None
    return (j, b, k - 1) if lag == 2 else (j, 1 - b, k - 1 if b == 0 else k) if lag == 1 else (j, b, k)


def spread(nc, g, table, index, keep_row, weight=None, bias=None, relu=False, scatter_to=None, scatter_ix=None, rows_to=None):
    with ExitStack() as ctx:
        sb, ps, sem = scope(nc, ctx)
        got_rows = sb("got_rows", [P, 2, CT, H])
        scaled = sb("scaled", [P, 2, CT, H])
        ix = sb("ix", [P, 2, 2, CT], I32)
        xT = sb("xT", [H, 2, CW])
        keep = sb("keep_row", [H, 2, CW])
        run = sb("running", [H, 2, CW])
        normed = sb("normed", [P, CT, H])
        biased = sb("biased", [P, CT, H])
        lone = sb("lone_row", [1, H])
        rows = sb("sum_rows", [P, 2, CT, H])
        pT = [ps("pT0", [H, CW]), ps("pT1", [H, CW])]
        pM = [ps("pM0", [H, CW]), ps("pM1", [H, CW])]
        pB = [ps("pB0", [P, CT * H]), ps("pB1", [P, CT * H])]
        got = [sem("rows_gathered_even"), sem("rows_gathered_odd")]
        sent = [sem("sums_out_even"), sem("sums_out_odd")]
        loaded = [sem("keep_loaded_even"), sem("keep_loaded_odd")]
        ix_ready, turned, copied, prod, scaled_up = (sem(n) for n in ("index_staged", "rows_turned", "turned_copied", "product_ready", "rows_scaled"))
        scanned, back, rows_ready, s_dve = (sem(n) for n in ("scanned", "sums_turned_back", "sum_rows_ready", "dve_step"))
        w_pool, w_pe, w_dve = sem("pool_woke"), sem("pe_woke"), sem("dve_woke")
        lone_ready, lone_sent = sem("lone_row_ready"), sem("lone_row_stored")
        block = ctx.enter_context(nc.Block())
        per_row = 16 * CT if scatter_to is not None else 16

        @block.gpsimd
        def _(pool):
            both = 2 if scatter_to is not None else 1

            def gather(it, b, k):
                if not first(it, 2):
                    wake(pool, scaled_up if weight is not None else turned, it - 1, w_pool)
                pool.tensor_copy(ix[:, 0, b, :], index[:, bass.ds(it * CT, CT)]).then_inc(ix_ready, 1)
                wake(pool, ix_ready, it * 2 - 1 if both == 2 and not first(it, 2) else it + 1, w_pool)
                gather_rows(pool, lambda t: got_rows[:, b, t, :], table, ix[:, 0], b, got[b])

            def scatter(it, b, k):
                if not first(it, 2):
                    wake(pool, sent[b], k * (16 * CT), w_pool)
                pool.tensor_copy(ix[:, 1, b, :], scatter_ix[:, bass.ds(it * CT, CT)]).then_inc(ix_ready, 1)
                wake(pool, ix_ready, STEPS + it + 1 if isinstance(it, int) and it >= STEPS - 2 else it * 2 + 4, w_pool)
                wake(pool, rows_ready, it + 1, w_pool)
                scatter_rows(pool, scatter_to, lambda t: rows[:, b, t, :], ix[:, 1], b, sent[b])

            if scatter_to is not None:
                scatter_steps(pool, gather, scatter)
                for b in range(2):
                    pool.wait_ge(sent[b], per_row * STEPS // 2)
            else:
                for it, b, k in steps(pool):
                    gather(it, b, k)

        @block.sync
        def _(sp):
            load_keep(sp, g, keep_row, H, keep, loaded, scanned)
            for b in range(2):
                sp.wait_ge(loaded[b], 16 * STEPS // 2)

        @block.tensor
        def _(pe):
            src = scaled if weight is not None else got_rows

            def turn(it, b, k):
                if weight is not None:
                    wake(pe, scaled_up, it + 1, w_pe)
                else:
                    wake(pe, got[b], (k + 1) * (16 * CT), w_pe)
                    if not first(it, 2):
                        wake(pe, scanned, it - 1, w_pe)
                for t in range(CT):
                    last = pe.transpose(pT[b][:, t * P:(t + 1) * P], src[:, b, t, :], g["ident"][:, :])
                last.then_inc(turned, 1)
                if weight is not None:
                    wake(pe, copied, it + 1, w_pe)
                    if not first(it, 2):
                        wake(pe, scanned, it - 1, w_pe)
                    pe.matmul(pM[b][:, :], weight[:, :], xT[:, b, :], start=True, stop=True).then_inc(prod, 1)

            def turn_back(it, b, k):
                wake(pe, scanned, it + 1, w_pe)
                if not first(it, 2):
                    wake(pe, rows_ready, it - 1, w_pe)
                for t in range(CT):
                    last = pe.transpose(pB[b][:, t * H:(t + 1) * H], run[:, b, t * P:(t + 1) * P], g["ident"][0:H, 0:H])
                last.then_inc(back, 1)

            for now in lagged(pe):
                for stage_of, lag in ((turn, 0), (turn_back, 1)):
                    if behind(*now, lag):
                        stage_of(*behind(*now, lag))

        @block.scalar
        def _(act):
            def copy(it, b, k):
                act.wait_ge(turned, it + 1)
                if not first(it, 2):
                    act.wait_ge(prod, it - 1)
                act.activation(xT[:, b, :], pT[b][:, :], ACT.Copy).then_inc(copied, 1)

            def put(it, b, k):
                act.wait_ge(rows_ready, it + 1)
                act.dma_start(rows_to[bass.ds(it * CW, CW), :].rearrange("(p t) h -> p t h", t=CT),
                              rows[:, b, :, :]).then_inc(sent[b], 16)

            if rows_to is not None:
                act.activation(lone[:, :], bias[0:1, :], ACT.Relu).then_inc(lone_ready, 1)
                act.wait_ge(lone_ready, 1)
                act.dma_start(rows_to[ROWS:ROWS + 1, :], lone[:, :]).then_inc(lone_sent, 16)
                act.wait_ge(lone_sent, 16)
            for now in lagged(act):
                if weight is not None and behind(*now, 0):
                    copy(*behind(*now, 0))
                if rows_to is not None and behind(*now, 2):
                    put(*behind(*now, 2))
            if rows_to is not None:
                for b in range(2):
                    act.wait_ge(sent[b], per_row * STEPS // 2)

        @block.vector
        def _(dve):
            def scale(it, b, k):
                wake(dve, got[b], (k + 1) * (16 * CT), w_dve)
                if not first(it, 2):
                    wake(dve, turned, it - 1, w_dve)
                norm = g["norm_src"][:, bass.ds(it * CT, CT)]
                dve.tensor_tensor(scaled[:, b, :, :], got_rows[:, b, :, :], over_tiles(norm, H, CT), ALU.mult).then_inc(scaled_up, 1)

            def scan(it, b, k):
                wake(dve, prod if weight is not None else turned, it + 1, w_dve)
                wake(dve, loaded[b], (k + 1) * 16, w_dve)
                if not first(it, 1):
                    wake(dve, scanned, it, w_dve)
                if not first(it, 2):
                    wake(dve, back, it - 1, w_dve)
                dve.tensor_tensor_scan(run[:, b, :], keep[:, b, :], (pM if weight is not None else pT)[b][:, :],
                                       0.0 if first(it, 1) else run[:, 1 - b, CW - 1:CW], ALU.mult, ALU.add).then_inc(scanned, 1)

            link = Chain(dve, s_dve, 0 if weight is None else 2 if relu else 1)

            def take_rows(it, b, k):
                link.start(it)
                wake(dve, back, it + 1, w_dve)
                sums = tiled(pB[b][:, :], CT)
                if weight is not None:
                    norm = g["norm_dst"][:, bass.ds(it * CT, CT)]
                    link(dve.tensor_tensor(normed[:, :, :], sums, over_tiles(norm, H, CT), ALU.mult))
                    if relu:
                        link(dve.tensor_tensor(biased[:, :, :], normed[:, :, :], over_rows(bias, P, CT), ALU.add))
                if not first(it, 2):
                    wake(dve, sent[b], k * per_row, w_dve)
                if weight is None:
                    dve.tensor_copy(rows[:, b, :, :], sums).then_inc(rows_ready, 1)
                elif relu:
                    dve.tensor_scalar(rows[:, b, :, :], biased[:, :, :], 0.0, None, ALU.max).then_inc(rows_ready, 1)
                else:
                    dve.tensor_tensor(rows[:, b, :, :], normed[:, :, :], over_rows(bias, P, CT), ALU.add).then_inc(rows_ready, 1)

            for now in lagged(dve):
                if behind(*now, 2):
                    take_rows(*behind(*now, 2))
                if behind(*now, 1):
                    scan(*behind(*now, 1))
                if weight is not None and behind(*now, 0):
                    scale(*behind(*now, 0))


def dense(nc, g, kind, x, agg, out, gather=None):
    mlp, attend = kind == "mlp", kind == "attend"
    BP = (0, 32, 64)
    XB = 4
    PEELED = 6
    update = mlp or attend
    with ExitStack() as ctx:
        sb, ps, sem = scope(nc, ctx)
        xa = sb("xa", [NP, XB, G, 2 * W] if update else [NP, XB, 2, DW])
        z = sb("z", [NP, 2, DW])
        zsq = sb("zsq", [NP, DW])
        yw = 2 * W if mlp else H
        YC = XC if mlp else slice(0, H)
        y = sb("y", [NP, 2, G, yw])
        slot_rows = sb("slot_rows", [NP, XB, G])
        SUM, SQUARES, MEANSQ, NEGHALF, ROOT, TMP, INVERSE, THREE_HALVES = range(8)
        st = sb("stats", [NP, 8, 2, G])
        which = slice(0, 2) if update else slice(1, 2)
        MEAN, RSTD = 0, 1
        pst = ps("pst", [NP, 2, 2, 128])
        load = [sem(f"loaded{n}") for n in range(XB)]
        store = [sem("stored_even"), sem("stored_odd")]
        z_ready, z_squared, z_used, y_ready, s_set, s_dve, s_finish, s_pool, var_ready, root_ready = (sem(n) for n in (
            "z_ready", "z_squared", "z_used", "y_ready", "constants_ready", "dve_step", "dve_finish_step", "pool_step", "variance_ready", "root_ready"))
        w_pe, w_pool, w_dve, w_sp = sem("pe_woke"), sem("pool_woke"), sem("dve_woke"), sem("sp_woke")
        if update:
            hsq = sb("hsq", [NP, DW])
            d = sb("d", [NP, 2, DW])
            xb = sb("xb", [NP, 2, DW])
            u = sb("u", [NP, DW])
            cT = [sb(f"cT{q}", [P, QW]) for q in range(2)]
            pT = [ps(f"pT{q}", [P, 512]) for q in range(2)]
            turned, cat, outp, hsqd, d_ready, xb_ready = (sem(n) for n in (
                "turned", "turned_copied", "rows_out", "h_squared", "d_ready", "biased_x_ready"))
            if mlp:
                h = sb("h", [NP, 2, DW])
                hT = [sb(f"hT{q}", [H + 1, QW]) for q in range(2)]
                pH = [ps(f"pH{q}", [H, 512]) for q in range(2)]
                pO = ps("pO", [NP, DW])
                pS = ps("pS", [NP, DW // 2])
                hid, act_h, silu, h_ready = sem("hidden_summed"), sem("hidden_ready"), sem("silu_ready"), sem("h_half_ready")
            else:
                xh = sb("xh", [NP, 2, DW])
                pO = [ps(f"pO{q}", [NP, DW]) for q in range(2)]
                wc = sb("w_centred", [2 * H, H])
                w_mean = sb("w_mean", [2 * H, 1])
                bias = sb("bias_centred", [P, H])
                bias_mean = sb("bias_mean", [P, 1])
                part = sb("bias_part", [P, 3, H], BF16)
                bias3 = sb("bias_parts", [BP[-1] + 1, 8, H], BF16)
                ones3 = sb("ones", [BP[-1] + 1, NP], BF16)
                rstd = sb("rstd_h", [NP, G])
                xh_ready = sem("xh_ready")
        if gather:
            table, index, keep_in = gather
            fetched = sb("fetched", [P, 2, CT], I32)
            ix = sb("index", [P, 2, CT], I32)
            got = [sem("fetched_even"), sem("fetched_odd")]
            ix_ready, kept = sem("index_staged"), sem("fetched_kept")
        block = ctx.enter_context(nc.Block())
        gq = G // QN
        LOADS = 16 if update else 32

        def dense_steps(eng):
            for it in range(PEELED):
                yield it, it % 2, it // 2, it % XB, it // XB
            with eng.Fori(0, (STEPS - PEELED) // XB) as i:
                for n in range(PEELED, PEELED + XB):
                    yield i * XB + n, n % 2, i * (XB // 2) + n // 2, n % XB, i + n // XB

        def phases(eng):
            yield from dense_steps(eng)
            for it in (STEPS, STEPS + 1):
                yield it, it % 2, it // 2, it % XB, it // XB

        def tail(it):
            return isinstance(it, int) and it >= STEPS

        @block.sync
        def _(sp):
            for it, b, k, xbuf, xk in dense_steps(sp):
                if not first(it, XB):
                    if update:
                        wake(sp, turned, (it - (XB - 1)) * QN, w_sp)
                        wake(sp, xb_ready, it - (XB - 1), w_sp)
                        if mlp:
                            wake(sp, h_ready, (it - (XB - 1)) * 2, w_sp)
                    else:
                        wake(sp, z_ready, it - (XB - 1), w_sp)
                if update:
                    sp.dma_start(xa[:, xbuf, :, :].rearrange("p n h -> p (n h)"), rows_of(x)[:, bass.ds(it * (2 * G * W), 2 * G * W)]).then_inc(load[xbuf], 16)
                else:
                    sp.dma_start(xa[:, xbuf, 0, :], rows_of(x)[:, bass.ds(it * DW, DW)]).then_inc(load[xbuf], 16)
                    sp.dma_start(xa[:, xbuf, 1, :], rows_of(agg)[:, bass.ds(it * DW, DW)]).then_inc(load[xbuf], 16)

        if update:
            @block.tensor
            def _(pe):
                def turn(it, xbuf, q):
                    if not (first(it, 1) and q < 2):
                        wake(pe, cat, it * QN + (q - 1), w_pe)
                    for j in range(gq):
                        last = pe.transpose(pT[q % 2][:, j * NP:(j + 1) * NP], xa[:, xbuf, q * gq + j, CATC], g["ident"][0:NP, 0:NP])
                    last.then_inc(turned, 1)

                def hidden(it, q):
                    wake(pe, cat, it * QN + (q + 1), w_pe)
                    if not (first(it, 1) and q < 2):
                        wake(pe, act_h, it * QN + (q - 1), w_pe)
                    pe.matmul(pH[q % 2][:, 0:QW], g["w_upd1"][:, :], cT[q % 2][:, :], start=True, stop=True).then_inc(hid, 1)

                def biases(it, b):
                    if not first(it, 2):
                        wake(pe, xh_ready, it - 1, w_pe)
                    for half in range(2):
                        pe.matmul(pO[b][:, half * 512:(half + 1) * 512], ones3[:, :], bias3[:, :, :].rearrange("p n h -> p (n h)"), start=True, stop=False)

                def project(it, b, q):
                    if mlp:
                        wake(pe, act_h, it * QN + (q + 1), w_pe)
                        if q % 2 == 0 and not first(it, 1):
                            wake(pe, silu, it * 2 + (q // 2 - 1), w_pe)
                        left, right, o = hT[q % 2], g["w_upd2"], pO
                    else:
                        wake(pe, cat, it * QN + (q + 1), w_pe)
                        left, right, o = cT[q % 2], wc, pO[b]
                    for j in range(gq):
                        c = (q * gq + j) * H
                        last = pe.matmul(o[:, c:c + H], left[:, j * NP:(j + 1) * NP], right[:, :], start=mlp, stop=mlp or (q * gq + j) % 8 == 7)
                    last.then_inc(outp, 1)

                pe.wait_ge(s_set, 1)
                for it, b, k, xbuf, xk in dense_steps(pe):
                    if attend:
                        biases(it, b)
                    wake(pe, load[xbuf], (xk + 1) * LOADS, w_pe)
                    turn(it, xbuf, 0)
                    turn(it, xbuf, 1)
                    if mlp:
                        hidden(it, 0)
                        turn(it, xbuf, 2)
                        hidden(it, 1)
                        project(it, b, 0)
                        turn(it, xbuf, 3)
                        hidden(it, 2)
                        project(it, b, 1)
                        hidden(it, 3)
                    else:
                        project(it, b, 0)
                        turn(it, xbuf, 2)
                        project(it, b, 1)
                        turn(it, xbuf, 3)
                    project(it, b, 2)
                    project(it, b, 3)

        @block.scalar
        def _(act):
            def copy(it, q):
                act.wait_ge(turned, it * QN + (q + 1))
                if not (first(it, 1) and q < 2):
                    act.wait_ge(hid if mlp else outp, it * QN + (q - 1))
                act.activation(cT[q % 2][:, :], pT[q % 2][:, 0:QW], ACT.Copy).then_inc(cat, 1)

            def rectify(it, q):
                act.wait_ge(hid, it * QN + (q + 1))
                if not (first(it, 1) and q < 2):
                    act.wait_ge(outp, it * QN + (q - 1))
                act.activation(hT[q % 2][0:H, :], pH[q % 2][:, 0:QW], ACT.Relu, bias=g["b_upd1"][:, 0:1]).then_inc(act_h, 1)

            def weigh(it, half):
                act.wait_ge(outp, it * QN + (2 * half + 2))
                if not (first(it, 1) and half == 0):
                    act.wait_ge(h_ready, it * 2 + half)
                act.activation(pS[:, :], pO[:, half * 512:(half + 1) * 512], ACT.Silu).then_inc(silu, 1)

            def root(it):
                act.wait_ge(var_ready, it + 1)
                act.activation(st[:, ROOT, which, :], st[:, NEGHALF, which, :], ACT.Sqrt, scale=-2.0).then_inc(root_ready, 1)

            def put(it, b):
                act.wait_ge(y_ready, it + 1)
                act.dma_start(rows_of(out)[:, bass.ds(it * (G * yw), G * yw)], y[:, b, :, :].rearrange("p n h -> p (n h)")).then_inc(store[b], 16)

            if mlp:
                act.wait_ge(s_set, 1)
            def squares(it, b):
                if not first(it, 1):
                    act.wait_ge(var_ready, it)
                if not first(it, 2):
                    act.wait_ge(z_ready, it - 1)
                    act.activation(zsq[:, :], z[:, b, :], ACT.Square).then_inc(z_squared, 1)
                if update and not tail(it):
                    if mlp:
                        act.wait_ge(h_ready, it * 2 + 2)
                    else:
                        act.wait_ge(outp, it * QN + QN)
                    act.activation(hsq[:, :], h[:, b, :] if mlp else pO[b][:, :], ACT.Square).then_inc(hsqd, 1)

            def keep_fetched(it, b, k):
                act.wait_ge(got[b], (k + 1) * (16 * CT))
                act.activation(keep_in[:, bass.ds(it * CT, CT)], fetched[:, b, :], ACT.Copy).then_inc(kept, 1)

            for it, b, k, xbuf, xk in phases(act):
                if mlp:
                    if not tail(it):
                        copy(it, 0)
                        copy(it, 1)
                    if not first(it, 1):
                        squares(it - 1, 1 - b)
                    if not tail(it):
                        rectify(it, 0)
                        copy(it, 2)
                        rectify(it, 1)
                        copy(it, 3)
                        weigh(it, 0)
                        rectify(it, 2)
                        rectify(it, 3)
                    if not first(it, 4):
                        put(it - 4, b)
                    if not tail(it):
                        weigh(it, 1)
                    continue
                if update and not tail(it):
                    copy(it, 0)
                    copy(it, 1)
                if not first(it, 1):
                    root(it - 1)
                if update and not tail(it):
                    copy(it, 2)
                    copy(it, 3)
                squares(it, b)
                if gather and not first(it, 2):
                    keep_fetched(it - 2, b, k - 1)
                if not first(it, 3):
                    put(it - 3, 1 - b)
            if mlp:
                squares(STEPS + 1, 1)
                put(STEPS - 2, 0)
            if not mlp:
                root(STEPS + 1)
            put(STEPS - 1, 1)
            for b in range(2):
                act.wait_ge(store[b], 16 * STEPS // 2)

        @block.gpsimd
        def _(pool):
            link = Chain(pool, s_pool, 12 if mlp else 1 if attend else 0)
            tail_link = Chain(pool, sem("pool_tail_step"))

            def inverse_root(it, link):
                wake(pool, var_ready, it + 1, w_pool)
                r, t = st[:, ROOT, :, :], st[:, TMP, :, :]
                for n in range(3):
                    link(pool.tensor_tensor(t, r, r, ALU.mult))
                    link(pool.tensor_tensor(t, t, st[:, NEGHALF, :, :], ALU.mult))
                    link(pool.tensor_tensor(t, t, st[:, THREE_HALVES, :, :], ALU.add))
                    last = pool.tensor_tensor(r, r, t, ALU.mult)
                    if n < 2:
                        link(last)
                last.then_inc(root_ready, 1)

            for it, b, k, xbuf, xk in phases(pool):
                if tail(it):
                    if mlp:
                        inverse_root(it, tail_link)
                    continue
                link.start(it)
                if not update:
                    wake(pool, load[xbuf], (xk + 1) * LOADS, w_pool)
                    if not first(it, 2):
                        wake(pool, z_used, it - 1, w_pool)
                    pool.tensor_tensor(z[:, b, :], xa[:, xbuf, 0, :], xa[:, xbuf, 1, :], ALU.add).then_inc(z_ready, 1)
                    continue
                if mlp:
                    inverse_root(it, link)
                wake(pool, load[xbuf], (xk + 1) * LOADS, w_pool)
                if not first(it, 2):
                    wake(pool, z_ready if mlp else xh_ready, it - 1, w_pool)
                pool.tensor_tensor(tiled(xb[:, b, :], G), xa[:, xbuf, :, XC],
                                   over_rows(g["r_b" if mlp else "r_beta"], NP, G), ALU.add).then_inc(xb_ready, 1)
                wake(pool, d_ready, it + 1, w_pool)
                if not first(it, 1):
                    wake(pool, z_ready, it, w_pool)
                link(pool.tensor_tensor(tiled(u[:, :], G), tiled(d[:, b, :], G),
                                        over_rows(g["r_g" if mlp else "r_gamma"], NP, G), ALU.mult))
                if mlp:
                    wake(pool, xb_ready, it + 1, w_pool)
                else:
                    wake(pool, xh_ready, it + 1, w_pool)
                if not first(it, 2):
                    wake(pool, z_used, it - 1, w_pool)
                pool.tensor_tensor(z[:, b, :], u[:, :], (xb if mlp else xh)[:, b, :], ALU.add).then_inc(z_ready, 1)
                if gather:
                    if not first(it, 2):
                        wake(pool, kept, it - 1, w_pool)
                    stage(pool, ix, b, index, it, ix_ready, w_pool)
                    wake(pool, ix_ready, it + 1, w_pool)
                    gather_rows(pool, lambda t: fetched[:, b, t:t + 1], table, ix, b, got[b])

        @block.vector
        def _(dve):
            if mlp:
                dve.memset(y[:, :, :, 1:2], 0.0)
                dve.memset(y[:, :, :, W:2 * W], 0.0)
                dve.memset(hT[0][H:H + 1, :], 1.0)
                dve.memset(hT[1][H:H + 1, :], 1.0)
            setup = Chain(dve, sem("setup_step"))
            setup(dve.memset(st[:, :, :, :], 0.0))
            setup(dve.memset(st[:, THREE_HALVES, :, :], 1.5))
            if attend:
                setup(dve.tensor_reduce(w_mean[:, :], g["w_out"][:, :], AX.X, ALU.add))
                setup(dve.tensor_scalar(w_mean[:, :], w_mean[:, :], 1.0 / H, None, ALU.mult))
                setup(dve.tensor_scalar(wc[:, :], g["w_out"][:, :], w_mean[:, 0:1], None, ALU.subtract))
                setup(dve.tensor_tensor(bias[:, :], g["r_bf"][:, :], g["r_bo"][:, :], ALU.add))
                setup(dve.tensor_reduce(bias_mean[:, :], bias[:, :], AX.X, ALU.add))
                setup(dve.tensor_scalar(bias_mean[:, :], bias_mean[:, :], 1.0 / H, None, ALU.mult))
                setup(dve.tensor_scalar(bias[:, :], bias[:, :], bias_mean[:, 0:1], None, ALU.subtract))
                setup(dve.memset(bias3[:, :, :], 0.0))
                setup(dve.memset(ones3[:, :], 0.0))
                for n, row in enumerate(BP):
                    setup(dve.tensor_copy(part[:, n, :], bias[:, :]))
                    setup(dve.tensor_copy(bias3[row:row + 1, :, :], part[row:row + 1, n:n + 1, :].to_broadcast([1, 8, H])))
                    setup(dve.memset(ones3[row:row + 1, :], 1.0))
                    if n < 2:
                        setup(dve.tensor_tensor(bias[:, :], bias[:, :], part[:, n, :], ALU.subtract))
            dve.sem_inc(s_set, 1)
            link = Chain(dve, s_dve, 5 if mlp else 3)
            finish_link = Chain(dve, s_finish, 1 if mlp else 4)

            def row_stat(kind, which, rows):
                return dve.tensor_reduce(st[:, kind, which, :], tiled(rows, G), AX.X, ALU.add)

            def by(kind, which):
                return over_tiles(pst[:, kind, which, 0:G], H, G)

            def variance():
                s, m, v = st[:, SUM, which, :], st[:, MEANSQ, which, :], st[:, NEGHALF, which, :]
                dve.tensor_scalar(pst[:, MEAN, which, 0:G], s, 1.0 / H, None, ALU.mult)
                link(dve.scalar_tensor_tensor(m, s, 0.5 / (H * H), s, ALU.mult, ALU.mult))
                link(dve.scalar_tensor_tensor(v, st[:, SQUARES, which, :], -0.5 / H, m, ALU.mult, ALU.add))
                if mlp:
                    link(dve.tensor_scalar(v, v, 0.0, -EPS / 2, ALU.min, ALU.add))
                    shifted = st[:, TMP, which, :].bitcast(I32)
                    link(dve.tensor_scalar(shifted, v.bitcast(I32), 1, 2, ALU.logical_shift_left, ALU.logical_shift_right))
                    dve.tensor_scalar(st[:, ROOT, which, :].bitcast(I32), shifted, -1.0, float(0x5F3759DF - (1 << 22)), ALU.mult, ALU.add).then_inc(var_ready, 1)
                else:
                    dve.tensor_scalar(v, v, 0.0, -EPS / 2, ALU.min, ALU.add).then_inc(var_ready, 1)

            def finish(it, b):
                finish_link.start(it)
                wake(dve, root_ready, it + 1, w_dve)
                h_too = update and not tail(it)
                if mlp:
                    finish_link(dve.tensor_copy(pst[:, RSTD, which, 0:G], st[:, ROOT, which, :]))
                    if h_too:
                        dve.tensor_tensor(tiled(d[:, b, :], G), tiled(d[:, b, :], G), by(RSTD, 0), ALU.mult).then_inc(d_ready, 1)
                else:
                    r, t = st[:, INVERSE, which, :], st[:, TMP, which, :]
                    finish_link(dve.reciprocal(r, st[:, ROOT, which, :]))
                    finish_link(dve.tensor_tensor(t, r, r, ALU.mult))
                    finish_link(dve.tensor_tensor(t, t, st[:, NEGHALF, which, :], ALU.mult))
                    if h_too:
                        dve.scalar_tensor_tensor(rstd[:, :], st[:, TMP, 0, :], 1.5, st[:, INVERSE, 0, :], ALU.add, ALU.mult)
                    finish_link(dve.scalar_tensor_tensor(pst[:, RSTD, 1, 0:G], st[:, TMP, 1, :], 1.5, st[:, INVERSE, 1, :], ALU.add, ALU.mult))
                    if h_too:
                        if not first(it, 2):
                            wake(dve, z_ready, it - 1, w_dve)
                        dve.tensor_tensor(tiled(d[:, b, :], G), tiled(pO[b][:, :], G), over_tiles(rstd[:, :], H, G), ALU.mult).then_inc(d_ready, 1)
                        wake(dve, xb_ready, it + 1, w_dve)
                        dve.tensor_tensor(xh[:, b, :], pO[b][:, :], xb[:, b, :], ALU.add).then_inc(xh_ready, 1)
                if not first(it, 2):
                    dve.tensor_tensor(y[:, b, :, YC], y[:, b, :, YC], by(RSTD, 1), ALU.mult).then_inc(y_ready, 1)

            for it, b, k, xbuf, xk in phases(dve):
                link.start(it)
                h_too = update and not tail(it)
                z_too = not first(it, 2)
                if h_too and mlp:
                    wake(dve, load[xbuf], (xk + 1) * LOADS, w_dve)
                    dve.tensor_copy(slot_rows[:, xbuf, :], xa[:, xbuf, :, RC])
                    for half in range(2):
                        n = slice(half * (G // 2), (half + 1) * (G // 2))
                        wake(dve, silu, it * 2 + (half + 1), w_dve)
                        dve.tensor_tensor(tiled(h[:, b, :], G)[:, n, :], tiled(pS[:, :], G // 2), xa[:, xbuf, n, XC], ALU.add).then_inc(h_ready, 1)
                if not first(it, 1):
                    finish(it - 1, 1 - b)
                if z_too:
                    wake(dve, z_ready, it - 1, w_dve)
                    last = row_stat(SUM, 1, z[:, b, :])
                if h_too and mlp:
                    wake(dve, h_ready, it * 2 + 2, w_dve)
                    last = row_stat(SUM, 0, h[:, b, :])
                if z_too:
                    wake(dve, z_squared, it - 1, w_dve)
                    last = row_stat(SQUARES, 1, zsq[:, :])
                if h_too:
                    wake(dve, hsqd, it + 1, w_dve)
                    last = row_stat(SQUARES, 0, hsq[:, :])
                if not h_too and not z_too:
                    last = dve.memset(st[:, SUM, 1, :], 0.0)
                link(last)
                variance()
                if z_too:
                    if not first(it, 4):
                        wake(dve, store[b], (k - 1) * 16, w_dve)
                    if mlp:
                        dve.tensor_copy(y[:, b, :, 0], slot_rows[:, (xbuf + 2) % XB, :])
                    dve.tensor_tensor(y[:, b, :, YC], tiled(z[:, b, :], G), by(MEAN, 1), ALU.subtract).then_inc(z_used, 1)
                if h_too and mlp:
                    if not first(it, 2):
                        wake(dve, z_ready, it - 1, w_dve)
                    dve.tensor_tensor(tiled(d[:, b, :], G), tiled(h[:, b, :], G), by(MEAN, 0), ALU.subtract)
            finish(STEPS + 1, 1)


def program(nc, inputs, out):
    g = {"in": inputs}
    with ExitStack() as ctx:
        sb, ps, sem = scope(nc, ctx)
        for name, shape in (("ident", [P, P]), ("w_msg1", [2 * H, H]), ("w_msg1e", [ED, H]), ("w_msg2", [H, H]),
                            ("w_upd1", [2 * H, H]), ("w_upd2", [H + 1, H]), ("w_out", [2 * H, H]), ("w_conv0", [H, H]),
                            ("w_conv1", [H, H]), ("w_conv2", [H, H]), ("wq", [P, H]), ("wk", [P, H]), ("wv", [P, H]),
                            ("head_sum", [H, P]), ("norm_src", [P, TILES]), ("norm_dst", [P, TILES])):
            g[name] = sb(name, shape)
        for name in ("b_msg1", "b_msg2", "b_upd1", "b_q", "b_k", "b_v"):
            g[name] = sb(name, [H, 1])
        for name in ("r_g", "r_b", "r_gamma", "r_beta", "r_bf", "r_bo", "r_c0", "r_c1", "r_c2"):
            g[name] = sb(name, [P, H])
        for name in ("edge_id", "scat_dst", "dst_id", "edge_id2", "scat_src", "slot_row", "scat_dst_agg", "dst_x", "src_x"):
            g[name] = sb(name, [P, TILES], I32)
        g["record"] = sb("record_of_slot", [P, TILES, ED + 1], I32)
        g["src_row"] = sb("src_row", [P, TILES], I32)
        g["dst_id2"] = sb("dst_id2", [P, TILES], I32)
        dram = lambda name, shape, dt=F32: nc.dram_tensor(name, shape, dt, kind="Internal").ap()
        g["words"] = dram("sort_words", (2, SLOTS + 8), I32)
        g["keep"] = dram("keep", (2, SLOTS + 8))
        g["records"] = dram("records", (E, ED + 1), I32)
        for name in ("A2", "A3", "X2", "X3"):
            g[name] = dram(name, (N, H))
        for name in ("XA0", "XA1"):
            g[name] = dram(name, (N, 2 * W))
        for name in ("H1", "H2"):
            g[name] = dram(name, (ROWS + 1, H))

        load_constants(nc, g)
        sort_edges(nc, g)
        fetch_records(nc, g)
        messages(nc, g)
        dense(nc, g, "mlp", g["XA0"], None, g["XA1"])
        attention(nc, g)
        dense(nc, g, "attend", g["XA1"], None, g["X2"], gather=(inputs["dst"], g["edge_id2"], g["dst_id2"]))
        spread(nc, g, g["X2"], g["dst_id2"], 1, scatter_to=g["A2"], scatter_ix=g["scat_src"])
        dense(nc, g, "add", g["X2"], g["A2"], g["X3"])
        spread(nc, g, g["X3"], g["record"][:, :, ED], 0, g["w_conv0"], g["r_c0"], relu=True, rows_to=g["H1"])
        spread(nc, g, g["H1"], g["src_row"], 0, g["w_conv1"], g["r_c1"], relu=True, rows_to=g["H2"])
        spread(nc, g, g["H2"], g["src_row"], 0, g["w_conv2"], g["r_c2"], scatter_to=g["A3"], scatter_ix=g["scat_dst"])
        dense(nc, g, "add", g["X3"], g["A3"], out)


def kernel(**inputs):
    import numpy as np
    import concourse.bacc as bacc
    from concourse.bass_utils import run_bass_kernel_spmd as run

    nc = bacc.Bacc("TRN2", target_bir_lowering=False, num_devices=1)
    slot = np.arange(SLOTS).reshape(P, SW)
    bit = lambda k: 1.0 - 2.0 * ((slot >> k) & 1)
    signs = np.stack([bit(k) * (bit(k - 1) if k > 1 else 1.0) for k in range(1, LOGS + 1)], 1)
    head = np.arange(H) // HD
    head_sum = (head[:, None] == head[None, :]) / float(np.sqrt(H))
    arrays = {n: np.asarray(a) for n, a in inputs.items()}
    for n in ("src", "dst"):
        arrays[n] = arrays[n].reshape(E, 1)
    arrays["x_norm"] = np.concatenate([arrays["x"], arrays.pop("node_vec").reshape(N, 1)], axis=1)
    arrays["signs"] = signs.reshape(P, LOGS * SW).astype(np.float32)
    arrays["eye"] = np.eye(P, dtype=np.float32)
    arrays["head_sum"] = np.concatenate([head_sum, head_sum], axis=1).astype(np.float32)
    aps = {n: nc.dram_tensor("in_" + n, a.shape, mybir.dt.from_np(a.dtype), kind="ExternalInput").ap() for n, a in arrays.items()}
    out = nc.dram_tensor("out", (N, H), F32, kind="ExternalOutput").ap()
    program(nc, aps, out)
    r = run(nc, [{"in_" + n: a for n, a in arrays.items()}], core_ids=[0])
    return r.results[0]["out"]
```

```python
import concourse.bass as bass
from concourse import mybir
from contextlib import ExitStack
import itertools

F32 = mybir.dt.float32
I32 = mybir.dt.int32
BF16 = mybir.dt.bfloat16
ALU = mybir.AluOpType
ACT = mybir.ActivationFunctionType
AX = mybir.AxisListType

N = 100000
E = 25000
H = 64
ED = 32
HEADS = 4
HD = H // HEADS
EPS = 1e-5
P = 128

SW = 256
SLOTS = P * SW
LOGS = 15
LOGW = 8
IDB = 15
HALF = N // 2
PADKEY = 115000
FAR = float(1 << 20)

SORT_STEPS = 22

CT = 4
STEPS = 50
TILES = STEPS * CT
CW = CT * P
CHUNKS = -(-E // CW)
assert CHUNKS in (STEPS - 1, STEPS)
COLS = max(TILES, (CHUNKS + 2) * CT)
ROWS = CHUNKS * CW

W = H + 2
XC = slice(2, 2 + H)
AC = slice(W, W + H)
CATC = slice(2, 2 + 2 * H)
RC = W + H

NP = 125
NPP = N // NP
G = NPP // STEPS
DW = G * H
QN = 4
QW = (G // QN) * NP


def steps(eng, peeled=2):
    peeled += (CHUNKS - peeled) % 2
    for it in range(peeled):
        yield it, it % 2, it // 2
    with eng.Fori(0, (CHUNKS - peeled) // 2) as i:
        for n in (peeled, peeled + 1):
            yield i * 2 + n, n % 2, i + n // 2


def times(b, count=CHUNKS):
    return (count + 1 - b) // 2


def wake(eng, sem, value, woke):
    eng.wait_ge(sem, value)
    eng.sem_inc(woke, 1)


class Chain:

    def __init__(self, eng, sem, links=0):
        self.eng, self.sem, self.links, self.step, self.n = eng, sem, links, 0, 0

    def start(self, step):
        assert self.n in (0, self.links), (self.n, self.links)
        self.step, self.n = step, 0

    def __call__(self, ins):
        self.n += 1
        ins.then_inc(self.sem, 1)
        self.eng.wait_ge(self.sem, self.step * self.links + self.n)


SCOPES = itertools.count()


def scope(nc, ctx):
    n = next(SCOPES)
    used = []

    def sem(name):
        used.append(nc.alloc_semaphore(f"{name}_{n}"))
        return used[-1]

    def clear():
        if used:
            nc.clear_and_free_semaphores(used)
            nc.all_engine_barrier()

    ctx.callback(clear)
    sb = lambda name, shape, dt=F32: ctx.enter_context(nc.sbuf_tensor(f"{name}_{n}", shape, dt))
    ps = lambda name, shape: ctx.enter_context(nc.psum_tensor(f"{name}_{n}", shape, F32))
    return sb, ps, sem


def rows_of(table):
    return table.rearrange("(p n) h -> p (n h)", p=NP)


def halves(table):
    return table.rearrange("n (two h) -> (n two) h", two=2)


def over_tiles(col, width, n):
    return col.unsqueeze(2).to_broadcast([col.shape[0], n, width])


def over_rows(vec, parts, n):
    return vec[0:parts, :].unsqueeze(1).to_broadcast([parts, n, H])


def tiled(ap, n):
    return ap.rearrange("p (n h) -> p n h", n=n)


class Constants:

    def __init__(self, g, sem):
        self.g, self.n = g, 0
        self.loaded, self.ident_loaded, self.zeroed = sem("constants_loaded"), sem("identity_loaded"), sem("weights_zeroed")

    def zero(self, eng):
        g = self.g
        for name in ("edge_id", "dst_id", "dst_x", "src_x", "dst_id2", "src_row"):
            eng.memset(g[name][:, CHUNKS * CT:COLS], 0)
        eng.memset(g["record"][:, CHUNKS * CT:COLS, :], 0)
        eng.memset(g["wk"][:, :], 0.0)
        eng.memset(g["wv"][:, :], 0.0)
        eng.memset(g["wq"][:, :], 0.0).then_inc(self.zeroed, 1)

    def load(self, eng):
        g, a = self.g, self.g["in"]

        def load(dst, src):
            self.n += 16
            eng.dma_start(dst, src).then_inc(self.loaded, 16)

        eng.dma_start(g["ident"][:, :], a["eye"]).then_inc(self.ident_loaded, 16)
        load(g["w_msg1"][:, :], a["L0_gnn_msg_w1"][0:2 * H, :])
        load(g["w_msg1e"][:, :], a["L0_gnn_msg_w1"][2 * H:2 * H + ED, :])
        load(g["w_msg2"][:, :], a["L0_gnn_msg_w2"])
        load(g["w_upd1"][:, :], a["L0_gnn_upd_w1"])
        load(g["w_upd2"][0:H, :], a["L0_gnn_upd_w2"])
        load(g["w_upd2"][H:H + 1, :], a["L0_gnn_upd_b2"].rearrange("(a h) -> a h", a=1))
        load(g["w_out"][0:H, :], a["L1_gnn_Wf"])
        load(g["w_out"][H:2 * H, :], a["L1_gnn_Wo"])
        for k in range(3):
            load(g[f"w_conv{k}"][:, :], a[f"L3_gnn_W{k}"])
        load(g["head_sum"][:, :], a["head_sum"])
        for col, name in (("b_msg1", "L0_gnn_msg_b1"), ("b_msg2", "L0_gnn_msg_b2"), ("b_upd1", "L0_gnn_upd_b1"),
                          ("b_q", "L1_gnn_bq"), ("b_k", "L1_gnn_bk"), ("b_v", "L1_gnn_bv")):
            load(g[col][:, :], a[name].rearrange("(h a) -> h a", a=1))
        for row, name in (("r_g", "L0_gnn_ln_g"), ("r_b", "L0_gnn_ln_b"), ("r_gamma", "L1_gnn_gamma"),
                          ("r_beta", "L1_gnn_beta"), ("r_bf", "L1_gnn_bf"), ("r_bo", "L1_gnn_bo"),
                          ("r_c0", "L3_gnn_b0"), ("r_c1", "L3_gnn_b1"), ("r_c2", "L3_gnn_b2")):
            load(g[row][:, :], a[name].partition_broadcast(P))
        eng.wait_ge(self.zeroed, 1)
        load(g["wk"][0:H, :], a["L1_gnn_Wk"])
        load(g["wv"][0:H, :], a["L1_gnn_Wv"])
        load(g["wq"][H:2 * H, :], a["L1_gnn_Wq"])

    def wait(self, eng):
        eng.wait_ge(self.loaded, self.n)


class XTables:

    def __init__(self, nc, g, sb, sem, begin, end):
        self.g, self.begin, self.end = g, begin, end
        self.x_in = sb("x_in", [NP, 2, DW])
        self.pair = sb("pair", [NP, 2, G, 2 * W])
        self.blanked, self.copied, self.woke, self.act_woke = sem("pair_blank"), sem("x_copied"), sem("x_load_woke"), sem("x_copy_woke")
        self.loaded = [sem("x_loaded_even"), sem("x_loaded_odd")]
        self.stored = [sem("pair_stored_even"), sem("pair_stored_odd")]

    def steps(self, eng):
        assert (self.end - self.begin) % 2 == 0
        for n in range(2):
            yield self.begin + n, n, n, 0
        with eng.Fori(1, (self.end - self.begin) // 2) as i:
            for b in range(2):
                yield i * 2 + (self.begin + b), i * 2 + b, b, i

    def blank(self, eng):
        pair = self.pair
        eng.memset(pair[:, :, :, 0:2], 0.0)
        eng.memset(pair[:, :, :, AC], 0.0)
        eng.memset(pair[:, :, :, RC:RC + 1], float(ROWS))
        eng.memset(pair[:, :, :, RC + 1:2 * W], 0.0).then_inc(self.blanked, 1)

    def load(self, eng):
        for it, n, b, k in self.steps(eng):
            if not first(n, 2):
                wake(eng, self.copied, n - 1, self.woke)
            eng.dma_start(self.x_in[:, b, :], rows_of(self.g["in"]["x"])[:, bass.ds(it * DW, DW)]).then_inc(self.loaded[b], 16)

    def build(self, act):
        act.wait_ge(self.blanked, 1)
        for it, n, b, k in self.steps(act):
            wake(act, self.loaded[b], (k + 1) * 16, self.act_woke)
            if not first(n, 2):
                wake(act, self.stored[b], k * 16, self.act_woke)
            act.activation(self.pair[:, b, :, XC], tiled(self.x_in[:, b, :], G), ACT.Copy).then_inc(self.copied, 1)
            act.wait_ge(self.copied, n + 1)
            act.dma_start(rows_of(self.g["XA0"])[:, bass.ds(it * (2 * G * W), 2 * G * W)],
                          self.pair[:, b, :, :].rearrange("p n h -> p (n h)")).then_inc(self.stored[b], 16)
        for b in range(2):
            act.wait_ge(self.stored[b], 8 * (self.end - self.begin))


def sort_edges(nc, g):
    with ExitStack() as ctx:
        sb, ps, sem = scope(nc, ctx)
        keys = sb("keys", [P, 2, SW], I32)
        ids = sb("ids", [P, 2, SW], I32)
        tmp = sb("tmp", [P, 2, SW], I32)
        tmp2 = sb("tmp2", [P, 2, SW], I32)
        tmp3 = sb("tmp3", [P, 2, SW], I32)
        nxt = sb("nxt", [P, 2, SW], I32)
        same = sb("same", [P, 2, SW])
        flt = sb("flt", [P, 2, 3, SW])
        bufs = (sb("bufA", [P, 2 * SW]), sb("bufB", [P, 2 * SW]))
        signs = sb("signs", [P, LOGS, SW])
        zero1 = sb("zero1", [1, 8], I32)
        EPP = E // NP
        record = sb("record", [NP, EPP, ED + 1], I32)
        srcs = sb("srcs", [NP, EPP], I32)
        tables = XTables(nc, g, sb, sem, 0, SORT_STEPS)
        constants = Constants(g, sem)
        ident = g["ident"]
        pT = ps("pT", [P, 2 * SW])
        pU = [ps(f"pU{n}", [P, SW]) for n in range(5)]
        s_pad, s_keys, s_ids, s_const = sem("keys_padded"), sem("keys_loaded"), sem("ids_ready"), sem("signs_loaded")
        s_dve, s_turn, s_turned, s_words = sem("dve_step"), sem("turn_ready"), sem("turned"), sem("words_stored")
        s_zero, s_next, s_same, s_keep = sem("zero_ready"), sem("next_loaded"), sem("same_ready"), sem("keep_stored")
        s_flt, s_cols, s_wr, s_out = sem("floats_ready"), sem("columns_turned"), sem("words_ready"), sem("columns_kept")
        s_rec, s_recs, s_joined = sem("record_loaded"), sem("record_stored"), sem("record_joined")
        block = ctx.enter_context(nc.Block())
        OUTS = (("edge_id", 0, 0), ("scat_dst", 0, 1), ("dst_id", 0, 2), ("edge_id2", 1, 0), ("scat_src", 1, 1))

        @block.sync
        def _(sp):
            sp.wait_ge(s_pad, 1)
            full = E // SW
            for q, name in enumerate(("dst", "src")):
                k = g["in"][name]
                sp.dma_start(keys[0:full, q, :], k[0:full * SW, :].rearrange("(p f) a -> p (f a)", f=SW)).then_inc(s_keys, 16)
                sp.dma_start(keys[full:full + 1, q, 0:E - full * SW],
                             k[full * SW:E, :].rearrange("(p f) a -> p (f a)", p=1)).then_inc(s_keys, 16)
            sp.dma_start(signs[:, :, :], g["in"]["signs"].rearrange("p (k f) -> p k f", k=LOGS)).then_inc(s_const, 16)
            sp.dma_start(record[:, :, 0:ED], g["in"]["edge_attr_32"].bitcast(I32).rearrange("(p e) f -> p e f", p=NP)).then_inc(s_rec, 16)
            sp.dma_start(srcs[:, :], g["in"]["src"].rearrange("(p e) a -> p (e a)", p=NP)).then_inc(s_rec, 16)
            sp.wait_ge(s_zero, 1)
            for q in range(2):
                sp.dma_start(g["words"][q:q + 1, SLOTS:SLOTS + 8], zero1[0:1, :]).then_inc(s_words, 16)
                sp.dma_start(g["keep"][q:q + 1, 0:1], zero1[0:1, 0:1].bitcast(F32)).then_inc(s_keep, 16)
            sp.wait_ge(s_joined, 1)
            sp.dma_start(g["records"].rearrange("(p e) f -> p (e f)", p=NP), record[:, :, :].rearrange("p e f -> p (e f)")).then_inc(s_recs, 16)
            sp.wait_ge(s_wr, 1)
            for q in range(2):
                sp.dma_start(g["words"][q, 0:SLOTS].rearrange("(p f) -> p f", f=SW),
                             bufs[0][:, q * SW:(q + 1) * SW].bitcast(I32)).then_inc(s_words, 16)
            sp.wait_ge(s_words, 64)
            for q in range(2):
                sp.dma_start(nxt[:, q, :], g["words"][q, 1:SLOTS + 1].rearrange("(p f) -> p f", f=SW)).then_inc(s_next, 16)
            sp.wait_ge(s_same, 1)
            for q in range(2):
                sp.dma_start(g["keep"][q, 1:SLOTS + 1].rearrange("(p f) -> p f", f=SW), same[:, q, :]).then_inc(s_keep, 16)
            sp.wait_ge(s_recs, 16)
            sp.wait_ge(s_keep, 64)

        @block.scalar
        def _(act):
            constants.load(act)
            tables.build(act)
            constants.wait(act)

        @block.gpsimd
        def _(pool):
            tables.blank(pool)
            for q in range(2):
                pool.iota(ids[:, q, :], pattern=[[1, SW]], base=0, channel_multiplier=SW).then_inc(s_ids, 1)
            pool.iota(g["slot_row"][:, 0:TILES].rearrange("p (c t) -> p c t", t=CT), pattern=[[CW, STEPS], [1, CT]], base=0, channel_multiplier=CT)
            pool.wait_ge(s_rec, 32)
            pool.tensor_copy(record[:, :, ED:ED + 1], srcs[:, :].unsqueeze(2)).then_inc(s_joined, 1)
            tables.load(pool)

        TURNS, at = [], 0
        for k in range(1, LOGS + 1):
            at += 1
            if k > LOGW:
                TURNS.append(at % 2)
                at += 1 + k - LOGW
                TURNS.append(at % 2)
                at += 1
            at += min(k, LOGW)

        @block.tensor
        def _(pe):
            pe.wait_ge(constants.ident_loaded, 16)
            for n in range(2 * (LOGS - LOGW)):
                pe.wait_ge(s_turn, n + 1)
                src = bufs[TURNS[n]]
                for b in range(4):
                    last = pe.transpose(pT[:, b * P:(b + 1) * P], src[:, b * P:(b + 1) * P], ident[:, :])
                last.then_inc(s_turned, 1)
            pe.wait_ge(s_flt, 1)
            for n, (_, q, a) in enumerate(OUTS):
                for b in range(2):
                    last = pe.transpose(pU[n][:, b * P:(b + 1) * P], flt[:, q, a, b * P:(b + 1) * P], ident[:, :])
            last.then_inc(s_cols, 1)

        @block.vector
        def _(dve):
            link = Chain(dve, s_dve)
            dve.memset(keys[:, :, :], PADKEY).then_inc(s_pad, 1)
            dve.memset(zero1[:, :], 0).then_inc(s_zero, 1)
            constants.zero(dve)
            dve.wait_ge(s_keys, 64)
            link(dve.tensor_scalar(tmp[:, :, :], keys[:, :, :], HALF, None, ALU.is_lt))
            link(dve.tensor_scalar(tmp2[:, :, :], tmp[:, :, :], HALF, 256 - HALF, ALU.mult, ALU.add))
            link(dve.tensor_tensor(tmp3[:, :, :], keys[:, :, :], tmp2[:, :, :], ALU.add))
            link(dve.tensor_scalar(tmp3[:, :, :], tmp3[:, :, :], IDB, None, ALU.logical_shift_left))
            link(dve.tensor_scalar(tmp[:, :, :], tmp[:, :, :], 31, None, ALU.logical_shift_left))
            link(dve.tensor_tensor(tmp[:, :, :], tmp[:, :, :], tmp3[:, :, :], ALU.bitwise_or))
            dve.wait_ge(s_ids, 2)
            link(dve.tensor_tensor(bufs[0][:, :].bitcast(I32).rearrange("p (q f) -> p q f", q=2), tmp[:, :, :], ids[:, :, :], ALU.bitwise_or))
            dve.wait_ge(s_const, 16)
            at = turns = 0

            def exchange(src, dst, stride):
                v = src[:, :].rearrange("p (b two s) -> p b two s", two=2, s=stride)
                o = dst[:, :].rearrange("p (b two s) -> p b two s", two=2, s=stride)
                dve.tensor_tensor(o[:, :, 0, :], v[:, :, 0, :], v[:, :, 1, :], ALU.min)
                link(dve.tensor_tensor(o[:, :, 1, :], v[:, :, 0, :], v[:, :, 1, :], ALU.max))

            for k in range(1, LOGS + 1):
                s = signs[:, k - 1, :].unsqueeze(1).to_broadcast([P, 2, SW])
                link(dve.tensor_tensor(bufs[1 - at][:, :].rearrange("p (q f) -> p q f", q=2),
                                       bufs[at][:, :].rearrange("p (q f) -> p q f", q=2), s, ALU.mult))
                at = 1 - at
                if k > LOGW:
                    dve.sem_inc(s_turn, 1)
                    turns += 1
                    dve.wait_ge(s_turned, turns)
                    link(dve.tensor_copy(bufs[1 - at][:, :], pT[:, :]))
                    at = 1 - at
                    for b in range(k - 1, LOGW - 1, -1):
                        exchange(bufs[at], bufs[1 - at], 1 << (b - LOGW))
                        at = 1 - at
                    dve.sem_inc(s_turn, 1)
                    turns += 1
                    dve.wait_ge(s_turned, turns)
                    link(dve.tensor_copy(bufs[1 - at][:, :], pT[:, :]))
                    at = 1 - at
                for b in range(min(k, LOGW) - 1, -1, -1):
                    exchange(bufs[at], bufs[1 - at], 1 << b)
                    at = 1 - at
            if at:
                link(dve.tensor_copy(bufs[0][:, :], bufs[1][:, :]))
            dve.sem_inc(s_wr, 1)
            w = bufs[0][:, :].bitcast(I32).rearrange("p (q f) -> p q f", q=2)
            link(dve.tensor_scalar(tmp[:, :, :], w, 31, None, ALU.logical_shift_right))
            link(dve.tensor_scalar(tmp2[:, :, :], tmp[:, :, :], -HALF, HALF - 256, ALU.mult, ALU.add))
            link(dve.tensor_scalar(tmp3[:, :, :], w, IDB, 0xFFFF, ALU.logical_shift_right, ALU.bitwise_and))
            link(dve.tensor_tensor(keys[:, :, :], tmp2[:, :, :], tmp3[:, :, :], ALU.add))
            link(dve.tensor_scalar(tmp[:, :, :], w, (1 << IDB) - 1, None, ALU.bitwise_and))
            link(dve.tensor_scalar(flt[:, :, 0, :], tmp[:, :, :], E - 1, None, ALU.min))
            link(dve.tensor_scalar(flt[:, :, 2, :], keys[:, :, :], N - 1, None, ALU.min))
            link(dve.tensor_scalar(tmp3[:, :, :], w, IDB, 0x1FFFF, ALU.logical_shift_right, ALU.bitwise_and))
            dve.wait_ge(s_next, 32)
            link(dve.tensor_scalar(nxt[:, :, :], nxt[:, :, :], IDB, 0x1FFFF, ALU.logical_shift_right, ALU.bitwise_and))
            link(dve.tensor_tensor(same[:, :, :], nxt[:, :, :], tmp3[:, :, :], ALU.is_equal))
            dve.sem_inc(s_same, 1)
            link(dve.scalar_tensor_tensor(flt[:, :, 1, :], same[:, :, :], FAR, keys[:, :, :], ALU.mult, ALU.add))
            dve.sem_inc(s_flt, 1)
            dve.wait_ge(s_cols, 1)
            for n, (name, _, _) in enumerate(OUTS):
                dve.tensor_copy(g[name][:, 0:TILES].rearrange("p (t b) -> p t b", b=2),
                                pU[n][:, :].rearrange("p (b t) -> p t b", b=2)[:, 0:TILES // 2, :]).then_inc(s_out, 1)
            dve.wait_ge(s_out, len(OUTS))
            dve.tensor_scalar(g["scat_dst_agg"][:, 0:TILES], g["scat_dst"][:, 0:TILES], 2.0, 1.0, ALU.mult, ALU.add)
            dve.tensor_scalar(g["dst_x"][:, 0:TILES], g["dst_id"][:, 0:TILES], 2.0, None, ALU.mult)


def stage(eng, ix, index, it):
    columns = index[:, bass.ds(it * CT, CT)]
    if eng.engine == mybir.EngineType.Activation:
        return eng.activation(ix, columns, ACT.Copy)
    return eng.tensor_copy(ix, columns)


def gather_rows(pool, dst, table, ix, slot, sem):
    for t in range(CT):
        pool.indirect_dma_start(dst(t), None, table, bass.IndirectOffsetOnAxis(ix[:, slot, t:t + 1], 0)).then_inc(sem, 16)


def scatter_rows(pool, table, src, ix, slot, sem):
    for t in range(CT):
        pool.indirect_dma_start(table, bass.IndirectOffsetOnAxis(ix[:, slot, t:t + 1], 0), src(t), None,
                                bounds_check=table.shape[0] - 1, oob_is_err=False).then_inc(sem, 16)


def fetch_records(nc, g):
    with ExitStack() as ctx:
        sb, ps, sem = scope(nc, ctx)
        buf = sb("gathered", [P, 2, CT, ED + 1], I32)
        ix = sb("index", [P, 2, CT], I32)
        tables = XTables(nc, g, sb, sem, SORT_STEPS, STEPS)
        got = [sem("rows_gathered_even"), sem("rows_gathered_odd")]
        ix_ready, w_pool, w_dve = sem("index_staged"), sem("pool_woke"), sem("dve_woke")
        block = ctx.enter_context(nc.Block())

        @block.gpsimd
        def _(pool):
            for it, b, k in steps(pool):
                wake(pool, ix_ready, it + 1, w_pool)
                gather_rows(pool, lambda t: buf[:, b, t, :], g["records"], ix, b, got[b])

        @block.vector
        def _(dve):
            tables.blank(dve)
            for n in range(2):
                stage(dve, ix[:, n, :], g["edge_id"], n).then_inc(ix_ready, 1)
            for it, b, k in steps(dve):
                wake(dve, got[b], (k + 1) * (16 * CT), w_dve)
                dve.tensor_copy(g["record"][:, bass.ds(it * CT, CT), :], buf[:, b, :, :])
                stage(dve, ix[:, b, :], g["edge_id"], it + 2).then_inc(ix_ready, 1)

        @block.sync
        def _(sp):
            tables.load(sp)

        @block.scalar
        def _(act):
            tables.build(act)


def first(it, n):
    return isinstance(it, int) and it < n


def scatter_steps(pool, gather, scatter):
    for it, b, k in steps(pool, 4):
        gather(it, b, k)
        if not first(it, 2):
            scatter(it - 2, b, k - 1)
    for it in (CHUNKS - 2, CHUNKS - 1):
        scatter(it, it % 2, it // 2)


def lagged(eng):
    yield from steps(eng, 4)
    for it in (CHUNKS, CHUNKS + 1):
        yield it, it % 2, it // 2


def behind(it, b, k, lag):
    j = it - lag
    if isinstance(j, int) and not 0 <= j < CHUNKS:
        return None
    return (j, b, k - 1) if lag == 2 else (j, 1 - b, k - 1 if b == 0 else k) if lag == 1 else (j, b, k)


def run_stages(eng, *order):
    for now in lagged(eng):
        for stage_of, lag in order:
            if behind(*now, lag):
                stage_of(*behind(*now, lag))


def load_keep(sp, g, row, parts, keep, loaded, used, dma=None):
    for it, b, k in steps(sp):
        if not first(it, 2):
            sp.wait_ge(used, it - 1)
        sp.dma_start(keep[:, b, :], g["keep"][row, bass.ds(it * CW, CW)].partition_broadcast(parts)).then_inc(loaded[b], 16)
        if dma:
            dma(it, b, k)


def messages(nc, g):
    with ExitStack() as ctx:
        sb, ps, sem = scope(nc, ctx)
        ends = sb("ends", [P, 2, CT, 2, H + 1])
        pair = sb("pair", [P, CT, 2 * H])
        ea = sb("edge_features", [P, 2, CT, ED], I32)
        tile = sb("fill_tile", [NP, 2, DW])
        ix = sb("ix", [P, 3, 2, CT], I32)
        catT = sb("catT", [P, CW])
        eaT = sb("eaT", [ED, CW])
        hT = sb("hT", [H, CW])
        mT = sb("mT", [H, CW])
        keep = sb("keep_row", [H, 2, CW])
        run = sb("running", [H, 2, CW])
        rows = sb("sum_rows", [P, 2, CT, W])
        pT = [ps("pT0", [P, CW]), ps("pT1", [P, CW])]
        pE = ps("pE", [ED, CW])
        pH = ps("pH", [H, CW])
        pM = ps("pM", [H, CW])
        pB = ps("pB", [P, CT * H])
        got = [sem("ends_gathered_even"), sem("ends_gathered_odd")]
        sent = [sem("sums_scattered_even"), sem("sums_scattered_odd")]
        loaded = [sem("keep_loaded_even"), sem("keep_loaded_odd")]
        ix_ready, turned, cat, eat, hid, act_h, msg, act_m = (sem(n) for n in (
            "index_staged", "ends_turned", "cat_copied", "features_copied", "hidden_summed", "hidden_ready", "message_summed", "message_ready"))
        scanned, back, rows_ready, norms, ea_ready = (sem(n) for n in (
            "scanned", "sums_turned_back", "sum_rows_ready", "norms_kept", "features_staged"))
        w_pool, w_pe, w_dve = sem("pool_woke"), sem("pe_woke"), sem("dve_woke")
        paired, tiles_ready, filled = sem("ends_paired"), sem("fill_ready"), sem("filled")
        block = ctx.enter_context(nc.Block())

        @block.gpsimd
        def _(pool):
            def gather(it, b, k):
                wake(pool, ix_ready, it + 1, w_pool)
                if not first(it, 2):
                    wake(pool, norms, it - 1, w_pool)
                gather_rows(pool, lambda t: ends[:, b, t, 0, :], g["in"]["x_norm"], ix[:, 0], b, got[b])
                gather_rows(pool, lambda t: ends[:, b, t, 1, :], g["in"]["x_norm"], ix[:, 1], b, got[b])

            def scatter(it, b, k):
                wake(pool, rows_ready, it + 1, w_pool)
                scatter_rows(pool, halves(g["XA0"]), lambda t: rows[:, b, t, :], ix[:, 2], b, sent[b])

            scatter_steps(pool, gather, scatter)
            for b in range(2):
                pool.wait_ge(sent[b], 16 * CT * times(b))

        @block.sync
        def _(sp):
            def fill(it, b, k):
                for n, name in enumerate(("A2", "A3")):
                    sp.dma_start(rows_of(g[name])[:, bass.ds(it * DW, DW)], tile[:, n, :]).then_inc(filled, 16)

            sp.wait_ge(tiles_ready, 1)
            load_keep(sp, g, 0, H, keep, loaded, scanned, fill)
            fill(STEPS - 1, 0, 0)
            sp.wait_ge(filled, 16 * 2 * STEPS)
            for b in range(2):
                sp.wait_ge(loaded[b], 16 * times(b))

        @block.tensor
        def _(pe):
            def turn(it, b, k):
                wake(pe, paired, it + 1, w_pe)
                wake(pe, ea_ready, it + 1, w_pe)
                for t in range(CT):
                    pe.transpose(pT[b][:, t * P:(t + 1) * P], pair[:, t, :], g["ident"][:, :])
                for t in range(CT):
                    last = pe.transpose(pE[:, t * P:(t + 1) * P], ea[:, b, t, :].bitcast(F32), g["ident"][:, :])
                last.then_inc(turned, 1)

            def hidden(it, b, k):
                wake(pe, cat, it + 1, w_pe)
                pe.matmul(pH[:, :], g["w_msg1"][:, :], catT[:, :], start=True, stop=False)
                wake(pe, eat, it + 1, w_pe)
                pe.matmul(pH[:, :], g["w_msg1e"][:, :], eaT[:, :], start=False, stop=True).then_inc(hid, 1)

            def message(it, b, k):
                wake(pe, act_h, it + 1, w_pe)
                pe.matmul(pM[:, :], g["w_msg2"][:, :], hT[:, :], start=True, stop=True).then_inc(msg, 1)

            def turn_back(it, b, k):
                wake(pe, scanned, it + 1, w_pe)
                if not first(it, 1):
                    wake(pe, rows_ready, it, w_pe)
                for t in range(CT):
                    last = pe.transpose(pB[:, t * H:(t + 1) * H], run[:, b, t * P:(t + 1) * P], g["ident"][0:H, 0:H])
                last.then_inc(back, 1)

            run_stages(pe, (message, 1), (turn, 0), (hidden, 0), (turn_back, 1))

        @block.scalar
        def _(act):
            def stage_ends(it, b):
                act.activation(ix[:, 0, b, :].unsqueeze(2), g["record"][:, bass.ds(it * CT, CT), ED:ED + 1], ACT.Copy)
                stage(act, ix[:, 1, b, :], g["dst_id"], it).then_inc(ix_ready, 1)

            def pair_ends(it, b, k):
                act.wait_ge(got[b], (k + 1) * (16 * 2 * CT))
                if not first(it, 1):
                    act.wait_ge(turned, it)
                act.activation(pair[:, :, :].rearrange("p t (e h) -> p t e h", e=2), ends[:, b, :, :, 0:H], ACT.Copy).then_inc(paired, 1)
                stage_ends(it + 2, b)

            def copy(it, b, k):
                act.wait_ge(turned, it + 1)
                if not first(it, 1):
                    act.wait_ge(hid, it)
                act.activation(catT[:, :], pT[b][:, :], ACT.Copy).then_inc(cat, 1)

            def rectify(it, b, k):
                act.wait_ge(hid, it + 1)
                if not first(it, 1):
                    act.wait_ge(msg, it)
                act.activation(hT[:, :], pH[:, :], ACT.Relu, bias=g["b_msg1"][:, 0:1]).then_inc(act_h, 1)

            def finish(it, b, k):
                act.wait_ge(msg, it + 1)
                if not first(it, 1):
                    act.wait_ge(scanned, it)
                act.activation(mT[:, :], pM[:, :], ACT.Identity, bias=g["b_msg2"][:, 0:1]).then_inc(act_m, 1)

            for n in range(2):
                stage_ends(n, n)
            run_stages(act, (finish, 1), (pair_ends, 0), (copy, 0), (rectify, 0))

        @block.vector
        def _(dve):
            dve.memset(rows[:, :, :, H:W], 0.0)
            dve.memset(tile[:, 0, :], 0.0)
            dve.tensor_copy(tiled(tile[:, 1, :], G), over_rows(g["r_c2"], NP, G)).then_inc(tiles_ready, 1)
            dve.tensor_scalar(g["src_x"][:, 0:CHUNKS * CT], g["record"][:, 0:CHUNKS * CT, ED], 2.0, None, ALU.mult)

            def stage_features(it, b, k):
                if not first(it, 2):
                    wake(dve, turned, it - 1, w_dve)
                dve.tensor_copy(ea[:, b, :, :], g["record"][:, bass.ds(it * CT, CT), 0:ED]).then_inc(ea_ready, 1)

            def keep_norms(it, b, k):
                wake(dve, got[b], (k + 1) * (16 * 2 * CT), w_dve)
                dve.tensor_copy(g["norm_src"][:, bass.ds(it * CT, CT)], ends[:, b, :, 0, H])
                dve.tensor_copy(g["norm_dst"][:, bass.ds(it * CT, CT)], ends[:, b, :, 1, H]).then_inc(norms, 1)

            def copy_features(it, b, k):
                wake(dve, turned, it + 1, w_dve)
                if not first(it, 1):
                    wake(dve, hid, it, w_dve)
                dve.tensor_copy(eaT[:, :], pE[:, :]).then_inc(eat, 1)

            def scan(it, b, k):
                wake(dve, act_m, it + 1, w_dve)
                wake(dve, loaded[b], (k + 1) * 16, w_dve)
                if not first(it, 1):
                    wake(dve, scanned, it, w_dve)
                if not first(it, 2):
                    wake(dve, back, it - 1, w_dve)
                dve.tensor_tensor_scan(run[:, b, :], keep[:, b, :], mT[:, :],
                                       0.0 if first(it, 1) else run[:, 1 - b, CW - 1:CW], ALU.mult, ALU.add).then_inc(scanned, 1)

            def take_rows(it, b, k):
                wake(dve, back, it + 1, w_dve)
                if not first(it, 2):
                    wake(dve, sent[b], k * (16 * CT), w_dve)
                stage(dve, ix[:, 2, b, :], g["scat_dst_agg"], it)
                dve.tensor_copy(rows[:, b, :, H], g["slot_row"][:, bass.ds(it * CT, CT)])
                dve.tensor_copy(rows[:, b, :, 0:H], tiled(pB[:, :], CT)).then_inc(rows_ready, 1)

            run_stages(dve, (stage_features, 0), (scan, 1), (keep_norms, 0), (copy_features, 0), (take_rows, 1))


def attention(nc, g):
    with ExitStack() as ctx:
        sb, ps, sem = scope(nc, ctx)
        ends = sb("ends", [P, 2, CT, 2, W])
        pair = sb("pair", [P, CT, 2 * H])
        ix = sb("ix", [P, 3, 2, CT], I32)
        catT = sb("catT", [P, CW])
        qT = sb("qT", [H, CW])
        prod = sb("prod", [H, CW])
        clip = sb("clip", [P, CW])
        e_low = sb("e_low", [H, CW])
        mz = sb("mz", [P, CW])
        keep = sb("keep_row", [P, 2, CW])
        run = sb("running", [P, 2, CW])
        z1 = sb("z1", [P, CT, H])
        rz = sb("rz", [P, CT, H])
        rows = sb("sum_rows", [P, 2, CT, W])
        pT = [ps("pT0", [P, CW]), ps("pT1", [P, CW])]
        pQ, pK, pV = ps("pQ", [H, CW]), ps("pK", [H, CW]), ps("pV", [H, CW])
        pS = ps("pS", [P, CW])
        pB = ps("pB", [P, CT * P])
        got = [sem("ends_gathered_even"), sem("ends_gathered_odd")]
        sent = [sem("sums_scattered_even"), sem("sums_scattered_odd")]
        loaded = [sem("keep_loaded_even"), sem("keep_loaded_odd")]
        ix_ready, turned, cat, qkv, q_ready, prod_ready, score, clipped, exped, weighed = (sem(n) for n in (
            "index_staged", "ends_turned", "cat_copied", "qkv_ready", "q_biased", "prod_ready", "score_summed", "score_clipped",
            "exp_ready", "values_weighed"))
        paired, kept = sem("ends_paired"), sem("src_rows_kept")
        scanned, back, rows_ready, s_dve = (sem(n) for n in ("scanned", "sums_turned_back", "sum_rows_ready", "dve_step"))
        w_pool, w_pe, w_dve = sem("pool_woke"), sem("pe_woke"), sem("dve_woke")
        block = ctx.enter_context(nc.Block())

        @block.gpsimd
        def _(pool):
            def gather(it, b, k):
                wake(pool, ix_ready, it + 1, w_pool)
                if not first(it, 2):
                    wake(pool, kept, it - 1, w_pool)
                gather_rows(pool, lambda t: ends[:, b, t, 0, :], halves(g["XA1"]), ix[:, 0], b, got[b])
                gather_rows(pool, lambda t: ends[:, b, t, 1, :], halves(g["XA1"]), ix[:, 1], b, got[b])

            def scatter(it, b, k):
                wake(pool, rows_ready, it + 1, w_pool)
                scatter_rows(pool, halves(g["XA1"]), lambda t: rows[:, b, t, :], ix[:, 2], b, sent[b])

            scatter_steps(pool, gather, scatter)
            for b in range(2):
                pool.wait_ge(sent[b], 16 * CT * times(b))

        @block.sync
        def _(sp):
            load_keep(sp, g, 0, P, keep, loaded, scanned)
            for b in range(2):
                sp.wait_ge(loaded[b], 16 * times(b))

        @block.tensor
        def _(pe):
            def turn(it, b, k):
                wake(pe, paired, it + 1, w_pe)
                for t in range(CT):
                    last = pe.transpose(pT[b][:, t * P:(t + 1) * P], pair[:, t, :], g["ident"][:, :])
                last.then_inc(turned, 1)

            def project(it, b, k):
                wake(pe, cat, it + 1, w_pe)
                pe.matmul(pQ[:, :], g["wq"][:, :], catT[:, :], start=True, stop=True).then_inc(qkv, 1)
                pe.matmul(pK[:, :], g["wk"][:, :], catT[:, :], start=True, stop=True).then_inc(qkv, 1)
                if not first(it, 1):
                    wake(pe, weighed, it, w_pe)
                pe.matmul(pV[:, :], g["wv"][:, :], catT[:, :], start=True, stop=True).then_inc(qkv, 1)

            def sum_heads(it, b, k):
                wake(pe, prod_ready, it + 1, w_pe)
                pe.matmul(pS[:, :], g["head_sum"][:, :], prod[:, :], start=True, stop=True).then_inc(score, 1)

            def turn_back(it, b, k):
                wake(pe, scanned, it + 1, w_pe)
                if not first(it, 1):
                    wake(pe, rows_ready, it, w_pe)
                for t in range(CT):
                    last = pe.transpose(pB[:, t * P:(t + 1) * P], run[:, b, t * P:(t + 1) * P], g["ident"][:, :])
                last.then_inc(back, 1)

            run_stages(pe, (sum_heads, 1), (turn, 0), (project, 0), (turn_back, 1))

        @block.scalar
        def _(act):
            def stage_ends(it, b):
                stage(act, ix[:, 0, b, :], g["src_x"], it)
                stage(act, ix[:, 1, b, :], g["dst_x"], it).then_inc(ix_ready, 1)

            def pair_ends(it, b, k):
                act.wait_ge(got[b], (k + 1) * (16 * 2 * CT))
                if not first(it, 1):
                    act.wait_ge(turned, it)
                act.activation(pair[:, :, :].rearrange("p t (e h) -> p t e h", e=2), ends[:, b, :, :, XC], ACT.Copy).then_inc(paired, 1)
                stage_ends(it + 2, b)

            def copy(it, b, k):
                act.wait_ge(turned, it + 1)
                if not first(it, 1):
                    act.wait_ge(qkv, it * 3)
                act.activation(catT[:, :], pT[b][:, :], ACT.Copy).then_inc(cat, 1)

            def bias_q(it, b, k):
                act.wait_ge(qkv, it * 3 + 1)
                if not first(it, 1):
                    act.wait_ge(prod_ready, it)
                act.activation(qT[:, :], pQ[:, :], ACT.Identity, bias=g["b_q"][:, 0:1]).then_inc(q_ready, 1)

            def exponentials(it, b, k):
                act.wait_ge(clipped, it + 1)
                if not first(it, 1):
                    act.wait_ge(scanned, it)
                act.activation(e_low[:, :], clip[0:H, :], ACT.Exp)
                act.activation(mz[H:P, :], clip[H:P, :], ACT.Exp).then_inc(exped, 1)

            for n in range(2):
                stage_ends(n, n)
            run_stages(act, (pair_ends, 0), (exponentials, 1), (copy, 0), (bias_q, 0))

        @block.vector
        def _(dve):
            link = Chain(dve, s_dve, 2)
            dve.memset(rows[:, :, :, H:W], 0.0)

            def keep_src_rows(it, b, k):
                wake(dve, got[b], (k + 1) * (16 * 2 * CT), w_dve)
                dve.tensor_copy(g["src_row"][:, bass.ds(it * CT, CT)], ends[:, b, :, 0, 0]).then_inc(kept, 1)

            def multiply(it, b, k):
                wake(dve, q_ready, it + 1, w_dve)
                wake(dve, qkv, it * 3 + 2, w_dve)
                if not first(it, 1):
                    wake(dve, score, it, w_dve)
                dve.scalar_tensor_tensor(prod[:, :], pK[:, :], g["b_k"][:, 0:1], qT[:, :], ALU.add, ALU.mult).then_inc(prod_ready, 1)

            def clip_scores(it, b, k):
                wake(dve, score, it + 1, w_dve)
                if not first(it, 1):
                    wake(dve, exped, it, w_dve)
                dve.tensor_scalar(clip[:, :], pS[:, :], 5.0, -5.0, ALU.min, ALU.max).then_inc(clipped, 1)

            def weigh(it, b, k):
                wake(dve, exped, it + 1, w_dve)
                wake(dve, qkv, it * 3 + 3, w_dve)
                dve.scalar_tensor_tensor(mz[0:H, :], pV[:, :], g["b_v"][:, 0:1], e_low[:, :], ALU.add, ALU.mult).then_inc(weighed, 1)

            def scan(it, b, k):
                wake(dve, weighed, it + 1, w_dve)
                wake(dve, loaded[b], (k + 1) * 16, w_dve)
                if not first(it, 1):
                    wake(dve, scanned, it, w_dve)
                if not first(it, 2):
                    wake(dve, back, it - 1, w_dve)
                dve.tensor_tensor_scan(run[:, b, :], keep[:, b, :], mz[:, :],
                                       0.0 if first(it, 1) else run[:, 1 - b, CW - 1:CW], ALU.mult, ALU.add).then_inc(scanned, 1)

            def take_rows(it, b, k):
                link.start(it)
                wake(dve, back, it + 1, w_dve)
                sums = pB[:, :].rearrange("p (t c) -> p t c", t=CT)
                link(dve.tensor_scalar(z1[:, :, :], sums[:, :, H:P], 1.0, None, ALU.add))
                link(dve.reciprocal(rz[:, :, :], z1[:, :, :]))
                if not first(it, 2):
                    wake(dve, sent[b], k * (16 * CT), w_dve)
                stage(dve, ix[:, 2, b, :], g["scat_dst_agg"], it)
                dve.tensor_tensor(rows[:, b, :, 0:H], sums[:, :, 0:H], rz[:, :, :], ALU.mult).then_inc(rows_ready, 1)

            run_stages(dve, (clip_scores, 1), (keep_src_rows, 0), (weigh, 1), (scan, 1), (multiply, 0), (take_rows, 1))


def spread(nc, g, table, index, keep_row, weight=None, bias=None, relu=False, scatter_to=None, scatter_ix=None, rows_to=None):
    with ExitStack() as ctx:
        sb, ps, sem = scope(nc, ctx)
        got_rows = sb("got_rows", [P, 2, CT, H])
        scaled = sb("scaled", [P, 2, CT, H])
        ix = sb("ix", [P, 2, 2, CT], I32)
        xT = sb("xT", [H, 2, CW])
        keep = sb("keep_row", [H, 2, CW])
        run = sb("running", [H, 2, CW])
        normed = sb("normed", [P, CT, H])
        biased = sb("biased", [P, CT, H])
        lone = sb("lone_row", [1, H])
        rows = sb("sum_rows", [P, 2, CT, H])
        pT = [ps("pT0", [H, CW]), ps("pT1", [H, CW])]
        pM = [ps("pM0", [H, CW]), ps("pM1", [H, CW])]
        pB = [ps("pB0", [P, CT * H]), ps("pB1", [P, CT * H])]
        got = [sem("rows_gathered_even"), sem("rows_gathered_odd")]
        sent = [sem("sums_out_even"), sem("sums_out_odd")]
        loaded = [sem("keep_loaded_even"), sem("keep_loaded_odd")]
        ix_ready, turned, copied, prod, scaled_up = (sem(n) for n in ("index_staged", "rows_turned", "turned_copied", "product_ready", "rows_scaled"))
        scanned, back, rows_ready, s_dve = (sem(n) for n in ("scanned", "sums_turned_back", "sum_rows_ready", "dve_step"))
        w_pool, w_pe, w_dve = sem("pool_woke"), sem("pe_woke"), sem("dve_woke")
        lone_ready, lone_sent = sem("lone_row_ready"), sem("lone_row_stored")
        block = ctx.enter_context(nc.Block())
        per_row = 16 * CT if scatter_to is not None else 16

        @block.gpsimd
        def _(pool):
            def gather(it, b, k):
                wake(pool, ix_ready, it + 1, w_pool)
                gather_rows(pool, lambda t: got_rows[:, b, t, :], table, ix[:, 0], b, got[b])

            def scatter(it, b, k):
                wake(pool, rows_ready, it + 1, w_pool)
                scatter_rows(pool, scatter_to, lambda t: rows[:, b, t, :], ix[:, 1], b, sent[b])

            if scatter_to is not None:
                scatter_steps(pool, gather, scatter)
                for b in range(2):
                    pool.wait_ge(sent[b], per_row * times(b))
            else:
                for it, b, k in steps(pool):
                    gather(it, b, k)

        @block.sync
        def _(sp):
            load_keep(sp, g, keep_row, H, keep, loaded, scanned)
            for b in range(2):
                sp.wait_ge(loaded[b], 16 * times(b))

        @block.tensor
        def _(pe):
            src = scaled if weight is not None else got_rows

            def turn(it, b, k):
                if weight is not None:
                    wake(pe, scaled_up, it + 1, w_pe)
                else:
                    wake(pe, got[b], (k + 1) * (16 * CT), w_pe)
                    if not first(it, 2):
                        wake(pe, scanned, it - 1, w_pe)
                for t in range(CT):
                    last = pe.transpose(pT[b][:, t * P:(t + 1) * P], src[:, b, t, :], g["ident"][:, :])
                last.then_inc(turned, 1)

            def multiply(it, b, k):
                if weight is not None:
                    wake(pe, copied, it + 1, w_pe)
                    if not first(it, 2):
                        wake(pe, scanned, it - 1, w_pe)
                    pe.matmul(pM[b][:, :], weight[:, :], xT[:, b, :], start=True, stop=True).then_inc(prod, 1)

            def turn_back(it, b, k):
                wake(pe, scanned, it + 1, w_pe)
                if not first(it, 2):
                    wake(pe, rows_ready, it - 1, w_pe)
                for t in range(CT):
                    last = pe.transpose(pB[b][:, t * H:(t + 1) * H], run[:, b, t * P:(t + 1) * P], g["ident"][0:H, 0:H])
                last.then_inc(back, 1)

            order = ((turn, 0), (multiply, 0), (turn_back, 1)) if scatter_to is not None else ((turn, 0), (turn_back, 2), (multiply, 0))
            run_stages(pe, *order)

        @block.scalar
        def _(act):
            def copy(it, b, k):
                act.wait_ge(turned, it + 1)
                if not first(it, 2):
                    act.wait_ge(prod, it - 1)
                act.activation(xT[:, b, :], pT[b][:, :], ACT.Copy).then_inc(copied, 1)

            def stage_next(it, b, k):
                act.wait_ge(turned, it + 1)
                stage(act, ix[:, 0, b, :], index, it + 2).then_inc(ix_ready, 1)

            def put(it, b, k):
                act.wait_ge(rows_ready, it + 1)
                act.dma_start(rows_to[bass.ds(it * CW, CW), :].rearrange("(p t) h -> p t h", t=CT),
                              rows[:, b, :, :]).then_inc(sent[b], 16)

            if rows_to is not None:
                act.activation(lone[:, :], bias[0:1, :], ACT.Relu).then_inc(lone_ready, 1)
                act.wait_ge(lone_ready, 1)
                act.dma_start(rows_to[ROWS:ROWS + 1, :], lone[:, :]).then_inc(lone_sent, 16)
                act.wait_ge(lone_sent, 16)
            if weight is None:
                for n in range(2):
                    stage(act, ix[:, 0, n, :], index, n).then_inc(ix_ready, 1)
            for now in lagged(act):
                if behind(*now, 0):
                    (stage_next if weight is None else copy)(*behind(*now, 0))
                if rows_to is not None and behind(*now, 2):
                    put(*behind(*now, 2))
            if rows_to is not None:
                for b in range(2):
                    act.wait_ge(sent[b], per_row * times(b))

        @block.vector
        def _(dve):
            def scale(it, b, k):
                if weight is None:
                    return
                wake(dve, got[b], (k + 1) * (16 * CT), w_dve)
                if not first(it, 2):
                    wake(dve, turned, it - 1, w_dve)
                norm = g["norm_src"][:, bass.ds(it * CT, CT)]
                dve.tensor_tensor(scaled[:, b, :, :], got_rows[:, b, :, :], over_tiles(norm, H, CT), ALU.mult).then_inc(scaled_up, 1)
                stage(dve, ix[:, 0, b, :], index, it + 2).then_inc(ix_ready, 1)

            def scan(it, b, k):
                wake(dve, prod if weight is not None else turned, it + 1, w_dve)
                wake(dve, loaded[b], (k + 1) * 16, w_dve)
                if not first(it, 1):
                    wake(dve, scanned, it, w_dve)
                if not first(it, 2):
                    wake(dve, back, it - 1, w_dve)
                dve.tensor_tensor_scan(run[:, b, :], keep[:, b, :], (pM if weight is not None else pT)[b][:, :],
                                       0.0 if first(it, 1) else run[:, 1 - b, CW - 1:CW], ALU.mult, ALU.add).then_inc(scanned, 1)

            link = Chain(dve, s_dve, 0 if weight is None else 2 if relu else 1)

            def take_rows(it, b, k):
                link.start(it)
                wake(dve, back, it + 1, w_dve)
                sums = tiled(pB[b][:, :], CT)
                if weight is not None:
                    norm = g["norm_dst"][:, bass.ds(it * CT, CT)]
                    link(dve.tensor_tensor(normed[:, :, :], sums, over_tiles(norm, H, CT), ALU.mult))
                    if relu:
                        link(dve.tensor_tensor(biased[:, :, :], normed[:, :, :], over_rows(bias, P, CT), ALU.add))
                if not first(it, 2):
                    wake(dve, sent[b], k * per_row, w_dve)
                if scatter_to is not None:
                    stage(dve, ix[:, 1, b, :], scatter_ix, it)
                if weight is None:
                    dve.tensor_copy(rows[:, b, :, :], sums).then_inc(rows_ready, 1)
                elif relu:
                    dve.tensor_scalar(rows[:, b, :, :], biased[:, :, :], 0.0, None, ALU.max).then_inc(rows_ready, 1)
                else:
                    dve.tensor_tensor(rows[:, b, :, :], normed[:, :, :], over_rows(bias, P, CT), ALU.add).then_inc(rows_ready, 1)

            order = ((take_rows, 2), (scan, 1), (scale, 0)) if scatter_to is not None else ((scale, 0), (take_rows, 2), (scan, 1))
            if weight is not None:
                for n in range(2):
                    stage(dve, ix[:, 0, n, :], index, n).then_inc(ix_ready, 1)
            run_stages(dve, *order)


def dense(nc, g, kind, x, agg, out, gather=None):
    mlp, attend = kind == "mlp", kind == "attend"
    BP = (0, 32, 64)
    XB = 4
    PEELED = 6
    POOL_NODES = 10 if attend else G
    update = mlp or attend
    with ExitStack() as ctx:
        sb, ps, sem = scope(nc, ctx)
        xa = sb("xa", [NP, XB, G, 2 * W] if update else [NP, XB, 2, DW])
        z = sb("z", [NP, 2, DW])
        zsq = sb("zsq", [NP, DW])
        yw = 2 * W if mlp else H
        YC = XC if mlp else slice(0, H)
        y = sb("y", [NP, 2, G, yw])
        slot_rows = sb("slot_rows", [NP, XB, G])
        SUM, SQUARES, MEANSQ, NEGHALF, ROOT, TMP, INVERSE, THREE_HALVES = range(8)
        st = sb("stats", [NP, 8, 2, G])
        which = slice(0, 2) if update else slice(1, 2)
        MEAN, RSTD = 0, 1
        pst = ps("pst", [NP, 2, 2, 128])
        load = [sem(f"loaded{n}") for n in range(XB)]
        store = [sem("stored_even"), sem("stored_odd")]
        z_ready, z_squared, z_used, y_ready, s_set, s_dve, s_finish, s_pool, var_ready, root_ready = (sem(n) for n in (
            "z_ready", "z_squared", "z_used", "y_ready", "constants_ready", "dve_step", "dve_finish_step", "pool_step", "variance_ready", "root_ready"))
        w_pe, w_pool, w_dve, w_sp, w_act = sem("pe_woke"), sem("pool_woke"), sem("dve_woke"), sem("sp_woke"), sem("act_woke")
        if update:
            hsq = sb("hsq", [NP, DW])
            d = sb("d", [NP, 2, DW])
            xb = sb("xb", [NP, 2, DW])
            u = sb("u", [NP, DW])
            cT = [sb(f"cT{q}", [P, QW]) for q in range(2)]
            pT = [ps(f"pT{q}", [P, 512]) for q in range(2)]
            turned, cat, outp, hsqd, d_ready, xb_ready = (sem(n) for n in (
                "turned", "turned_copied", "rows_out", "h_squared", "d_ready", "biased_x_ready"))
            if mlp:
                h = sb("h", [NP, 2, DW])
                hT = [sb(f"hT{q}", [H + 1, QW]) for q in range(2)]
                pH = [ps(f"pH{q}", [H, 512]) for q in range(2)]
                pO = ps("pO", [NP, DW])
                pS = ps("pS", [NP, DW // 2])
                hid, act_h, silu, h_ready = sem("hidden_summed"), sem("hidden_ready"), sem("silu_ready"), sem("h_half_ready")
            else:
                xh = sb("xh", [NP, 2, DW])
                pO = [ps(f"pO{q}", [NP, DW]) for q in range(2)]
                wc = sb("w_centred", [2 * H, H])
                w_mean = sb("w_mean", [2 * H, 1])
                bias = sb("bias_centred", [P, H])
                bias_mean = sb("bias_mean", [P, 1])
                part = sb("bias_part", [P, 3, H], BF16)
                bias3 = sb("bias_parts", [BP[-1] + 1, 8, H], BF16)
                ones3 = sb("ones", [BP[-1] + 1, NP], BF16)
                rstd = sb("rstd_h", [NP, G])
                xh_ready, u_ready, z_rest = sem("xh_ready"), sem("u_ready"), sem("z_rest_ready")
        else:
            rstd_z = sb("rstd_z", [NP, 2, G])
            rstd_ready = sem("rstd_ready")
        if gather:
            table, index, keep_in = gather
            fetched = sb("fetched", [P, 2, CT], I32)
            ix = sb("index", [P, 2, CT], I32)
            got = [sem("fetched_even"), sem("fetched_odd")]
            ix_ready = sem("index_staged")
        block = ctx.enter_context(nc.Block())
        gq = G // QN
        LOADS = 16 if update else 32

        def dense_steps(eng):
            for it in range(PEELED):
                yield it, it % 2, it // 2, it % XB, it // XB
            with eng.Fori(0, (STEPS - PEELED) // XB) as i:
                for n in range(PEELED, PEELED + XB):
                    yield i * XB + n, n % 2, i * (XB // 2) + n // 2, n % XB, i + n // XB

        def phases(eng):
            yield from dense_steps(eng)
            for it in (STEPS, STEPS + 1):
                yield it, it % 2, it // 2, it % XB, it // XB

        def tail(it):
            return isinstance(it, int) and it >= STEPS

        def put(eng, it, b, woke):
            wake(eng, y_ready, it + 1, woke)
            eng.dma_start(rows_of(out)[:, bass.ds(it * (G * yw), G * yw)], y[:, b, :, :].rearrange("p n h -> p (n h)")).then_inc(store[b], 16)

        @block.sync
        def _(sp):
            LATE = XB + 2
            for it, b, k, xbuf, xk in dense_steps(sp):
                if not first(it, XB):
                    if update:
                        wake(sp, turned, (it - (XB - 1)) * QN, w_sp)
                        wake(sp, xb_ready, it - (XB - 1), w_sp)
                        if mlp:
                            wake(sp, h_ready, (it - (XB - 1)) * 2, w_sp)
                    else:
                        wake(sp, z_ready, it - (XB - 1), w_sp)
                if update:
                    sp.dma_start(xa[:, xbuf, :, :].rearrange("p n h -> p (n h)"), rows_of(x)[:, bass.ds(it * (2 * G * W), 2 * G * W)]).then_inc(load[xbuf], 16)
                else:
                    sp.dma_start(xa[:, xbuf, 0, :], rows_of(x)[:, bass.ds(it * DW, DW)]).then_inc(load[xbuf], 16)
                    sp.dma_start(xa[:, xbuf, 1, :], rows_of(agg)[:, bass.ds(it * DW, DW)]).then_inc(load[xbuf], 16)
                    if not first(it, LATE):
                        put(sp, it - LATE, b, w_sp)
            if not update:
                for it in range(STEPS - LATE, STEPS):
                    put(sp, it, it % 2, w_sp)

        if update:
            @block.tensor
            def _(pe):
                def turn(it, xbuf, q):
                    if not (first(it, 1) and q < 2):
                        wake(pe, cat, it * QN + (q - 1), w_pe)
                    for j in range(gq):
                        last = pe.transpose(pT[q % 2][:, j * NP:(j + 1) * NP], xa[:, xbuf, q * gq + j, CATC], g["ident"][0:NP, 0:NP])
                    last.then_inc(turned, 1)

                def hidden(it, q):
                    wake(pe, cat, it * QN + (q + 1), w_pe)
                    if not (first(it, 1) and q < 2):
                        wake(pe, act_h, it * QN + (q - 1), w_pe)
                    pe.matmul(pH[q % 2][:, 0:QW], g["w_upd1"][:, :], cT[q % 2][:, :], start=True, stop=True).then_inc(hid, 1)

                def biases(it, b):
                    if not first(it, 2):
                        wake(pe, xh_ready, it - 1, w_pe)
                    for half in range(2):
                        pe.matmul(pO[b][:, half * 512:(half + 1) * 512], ones3[:, :], bias3[:, :, :].rearrange("p n h -> p (n h)"), start=True, stop=False)

                def project(it, b, q):
                    if mlp:
                        wake(pe, act_h, it * QN + (q + 1), w_pe)
                        if q % 2 == 0 and not first(it, 1):
                            wake(pe, silu, it * 2 + (q // 2 - 1), w_pe)
                        left, right, o = hT[q % 2], g["w_upd2"], pO
                    else:
                        wake(pe, cat, it * QN + (q + 1), w_pe)
                        left, right, o = cT[q % 2], wc, pO[b]
                    for j in range(gq):
                        c = (q * gq + j) * H
                        last = pe.matmul(o[:, c:c + H], left[:, j * NP:(j + 1) * NP], right[:, :], start=mlp, stop=mlp or (q * gq + j) % 8 == 7)
                    last.then_inc(outp, 1)

                pe.wait_ge(s_set, 1)
                for it, b, k, xbuf, xk in dense_steps(pe):
                    if attend:
                        biases(it, b)
                    wake(pe, load[xbuf], (xk + 1) * LOADS, w_pe)
                    turn(it, xbuf, 0)
                    turn(it, xbuf, 1)
                    if mlp:
                        hidden(it, 0)
                        turn(it, xbuf, 2)
                        hidden(it, 1)
                        project(it, b, 0)
                        turn(it, xbuf, 3)
                        hidden(it, 2)
                        project(it, b, 1)
                        hidden(it, 3)
                    else:
                        project(it, b, 0)
                        turn(it, xbuf, 2)
                        project(it, b, 1)
                        turn(it, xbuf, 3)
                    project(it, b, 2)
                    project(it, b, 3)

        @block.scalar
        def _(act):
            def copy(it, q):
                act.wait_ge(turned, it * QN + (q + 1))
                if not (first(it, 1) and q < 2):
                    act.wait_ge(hid if mlp else outp, it * QN + (q - 1))
                act.activation(cT[q % 2][:, :], pT[q % 2][:, 0:QW], ACT.Copy).then_inc(cat, 1)

            def rectify(it, q):
                act.wait_ge(hid, it * QN + (q + 1))
                if not (first(it, 1) and q < 2):
                    act.wait_ge(outp, it * QN + (q - 1))
                act.activation(hT[q % 2][0:H, :], pH[q % 2][:, 0:QW], ACT.Relu, bias=g["b_upd1"][:, 0:1]).then_inc(act_h, 1)

            def weigh(it, half):
                act.wait_ge(outp, it * QN + (2 * half + 2))
                if not (first(it, 1) and half == 0):
                    act.wait_ge(h_ready, it * 2 + half)
                act.activation(pS[:, :], pO[:, half * 512:(half + 1) * 512], ACT.Silu).then_inc(silu, 1)

            def root(it):
                act.wait_ge(var_ready, it + 1)
                act.activation(st[:, ROOT, which, :], st[:, NEGHALF, which, :], ACT.Sqrt, scale=-2.0).then_inc(root_ready, 1)

            def squares(it, b):
                if not first(it, 1):
                    act.wait_ge(var_ready, it)
                if not first(it, 2):
                    act.wait_ge(z_ready, it - 1)
                    if attend:
                        act.wait_ge(z_rest, it - 1)
                    act.activation(zsq[:, :], z[:, b, :], ACT.Square).then_inc(z_squared, 1)
                if update and not tail(it):
                    if mlp:
                        act.wait_ge(h_ready, it * 2 + 2)
                    else:
                        act.wait_ge(outp, it * QN + QN)
                    act.activation(hsq[:, :], h[:, b, :] if mlp else pO[b][:, :], ACT.Square).then_inc(hsqd, 1)

            def keep_fetched(it, b, k):
                act.wait_ge(got[b], (k + 1) * (16 * CT))
                act.activation(keep_in[:, bass.ds(it * CT, CT)], fetched[:, b, :], ACT.Copy)

            for it, b, k, xbuf, xk in phases(act):
                if mlp:
                    if not tail(it):
                        copy(it, 0)
                        copy(it, 1)
                    if not first(it, 1):
                        squares(it - 1, 1 - b)
                    if not tail(it):
                        rectify(it, 0)
                        copy(it, 2)
                        rectify(it, 1)
                        copy(it, 3)
                        weigh(it, 0)
                        rectify(it, 2)
                        rectify(it, 3)
                    if not first(it, 4):
                        put(act, it - 4, b, w_act)
                    if not tail(it):
                        weigh(it, 1)
                    continue
                if update and not tail(it):
                    copy(it, 0)
                    copy(it, 1)
                if not first(it, 1):
                    root(it - 1)
                if update and not tail(it):
                    copy(it, 2)
                    copy(it, 3)
                squares(it, b)
                if gather and not first(it, 2):
                    keep_fetched(it - 2, b, k - 1)
                if gather and not tail(it):
                    stage(act, ix[:, b, :], index, it).then_inc(ix_ready, 1)
                if attend and not first(it, 3):
                    put(act, it - 3, 1 - b, w_act)
            if mlp:
                squares(STEPS + 1, 1)
                put(act, STEPS - 2, 0, w_act)
            if not mlp:
                root(STEPS + 1)
            if update:
                put(act, STEPS - 1, 1, w_act)
            for b in range(2):
                act.wait_ge(store[b], 16 * STEPS // 2)

        @block.gpsimd
        def _(pool):
            link = Chain(pool, s_pool, 12 if mlp else 0)
            tail_link = Chain(pool, sem("pool_tail_step"))

            def inverse_root(it, link):
                wake(pool, var_ready, it + 1, w_pool)
                r, t = st[:, ROOT, :, :], st[:, TMP, :, :]
                for n in range(3):
                    link(pool.tensor_tensor(t, r, r, ALU.mult))
                    link(pool.tensor_tensor(t, t, st[:, NEGHALF, :, :], ALU.mult))
                    link(pool.tensor_tensor(t, t, st[:, THREE_HALVES, :, :], ALU.add))
                    last = pool.tensor_tensor(r, r, t, ALU.mult)
                    if n < 2:
                        link(last)
                last.then_inc(root_ready, 1)

            def scale_y(it, b):
                wake(pool, rstd_ready, it + 3, w_pool)
                pool.tensor_tensor(tiled_y(b), tiled_y(b), over_tiles(rstd_z[:, b, :], H, G), ALU.mult).then_inc(y_ready, 1)

            def tiled_y(b):
                return y[:, b, :, :]

            for it, b, k, xbuf, xk in phases(pool):
                if not update and not first(it, 3):
                    scale_y(it - 3, 1 - b)
                if tail(it):
                    if mlp:
                        inverse_root(it, tail_link)
                    continue
                link.start(it)
                if not update:
                    wake(pool, load[xbuf], (xk + 1) * LOADS, w_pool)
                    if not first(it, 2):
                        wake(pool, z_used, it - 1, w_pool)
                    pool.tensor_tensor(z[:, b, :], xa[:, xbuf, 0, :], xa[:, xbuf, 1, :], ALU.add).then_inc(z_ready, 1)
                    continue
                if mlp:
                    inverse_root(it, link)
                wake(pool, load[xbuf], (xk + 1) * LOADS, w_pool)
                if not first(it, 2):
                    wake(pool, z_ready if mlp else xh_ready, it - 1, w_pool)
                pool.tensor_tensor(tiled(xb[:, b, :], G), xa[:, xbuf, :, XC],
                                   over_rows(g["r_b" if mlp else "r_beta"], NP, G), ALU.add).then_inc(xb_ready, 1)
                wake(pool, d_ready, it + 1, w_pool)
                if not first(it, 1):
                    wake(pool, z_ready, it, w_pool)
                if attend and not first(it, 1):
                    wake(pool, z_rest, it, w_pool)
                scaled_d = pool.tensor_tensor(tiled(u[:, :], G), tiled(d[:, b, :], G),
                                              over_rows(g["r_g" if mlp else "r_gamma"], NP, G), ALU.mult)
                if mlp:
                    link(scaled_d)
                else:
                    scaled_d.then_inc(u_ready, 1)
                    wake(pool, u_ready, it + 1, w_pool)
                if mlp:
                    wake(pool, xb_ready, it + 1, w_pool)
                else:
                    wake(pool, xh_ready, it + 1, w_pool)
                if not first(it, 2):
                    wake(pool, z_used, it - 1, w_pool)
                n = slice(0, POOL_NODES * H)
                pool.tensor_tensor(z[:, b, n], u[:, n], (xb if mlp else xh)[:, b, n], ALU.add).then_inc(z_ready, 1)
                if gather:
                    wake(pool, ix_ready, it + 1, w_pool)
                    gather_rows(pool, lambda t: fetched[:, b, t:t + 1], table, ix, b, got[b])
            if not update:
                scale_y(STEPS - 1, 1)

        @block.vector
        def _(dve):
            if mlp:
                dve.memset(y[:, :, :, 1:2], 0.0)
                dve.memset(y[:, :, :, W:2 * W], 0.0)
                dve.memset(hT[0][H:H + 1, :], 1.0)
                dve.memset(hT[1][H:H + 1, :], 1.0)
            setup = Chain(dve, sem("setup_step"))
            setup(dve.memset(st[:, :, :, :], 0.0))
            setup(dve.memset(st[:, THREE_HALVES, :, :], 1.5))
            if attend:
                setup(dve.tensor_reduce(w_mean[:, :], g["w_out"][:, :], AX.X, ALU.add))
                setup(dve.tensor_scalar(w_mean[:, :], w_mean[:, :], 1.0 / H, None, ALU.mult))
                setup(dve.tensor_scalar(wc[:, :], g["w_out"][:, :], w_mean[:, 0:1], None, ALU.subtract))
                setup(dve.tensor_tensor(bias[:, :], g["r_bf"][:, :], g["r_bo"][:, :], ALU.add))
                setup(dve.tensor_reduce(bias_mean[:, :], bias[:, :], AX.X, ALU.add))
                setup(dve.tensor_scalar(bias_mean[:, :], bias_mean[:, :], 1.0 / H, None, ALU.mult))
                setup(dve.tensor_scalar(bias[:, :], bias[:, :], bias_mean[:, 0:1], None, ALU.subtract))
                setup(dve.memset(bias3[:, :, :], 0.0))
                setup(dve.memset(ones3[:, :], 0.0))
                for n, row in enumerate(BP):
                    setup(dve.tensor_copy(part[:, n, :], bias[:, :]))
                    setup(dve.tensor_copy(bias3[row:row + 1, :, :], part[row:row + 1, n:n + 1, :].to_broadcast([1, 8, H])))
                    setup(dve.memset(ones3[row:row + 1, :], 1.0))
                    if n < 2:
                        setup(dve.tensor_tensor(bias[:, :], bias[:, :], part[:, n, :], ALU.subtract))
            dve.sem_inc(s_set, 1)
            link = Chain(dve, s_dve, 5 if mlp else 3)
            finish_link = Chain(dve, s_finish, 1 if mlp else 4 if attend else 3)

            def row_stat(kind, which, rows):
                return dve.tensor_reduce(st[:, kind, which, :], tiled(rows, G), AX.X, ALU.add)

            def by(kind, which):
                return over_tiles(pst[:, kind, which, 0:G], H, G)

            def variance():
                s, m, v = st[:, SUM, which, :], st[:, MEANSQ, which, :], st[:, NEGHALF, which, :]
                dve.tensor_scalar(pst[:, MEAN, which, 0:G], s, 1.0 / H, None, ALU.mult)
                link(dve.scalar_tensor_tensor(m, s, 0.5 / (H * H), s, ALU.mult, ALU.mult))
                link(dve.scalar_tensor_tensor(v, st[:, SQUARES, which, :], -0.5 / H, m, ALU.mult, ALU.add))
                if mlp:
                    link(dve.tensor_scalar(v, v, 0.0, -EPS / 2, ALU.min, ALU.add))
                    shifted = st[:, TMP, which, :].bitcast(I32)
                    link(dve.tensor_scalar(shifted, v.bitcast(I32), 1, 2, ALU.logical_shift_left, ALU.logical_shift_right))
                    dve.tensor_scalar(st[:, ROOT, which, :].bitcast(I32), shifted, -1.0, float(0x5F3759DF - (1 << 22)), ALU.mult, ALU.add).then_inc(var_ready, 1)
                else:
                    dve.tensor_scalar(v, v, 0.0, -EPS / 2, ALU.min, ALU.add).then_inc(var_ready, 1)

            def finish(it, b):
                finish_link.start(it)
                wake(dve, root_ready, it + 1, w_dve)
                h_too = update and not tail(it)
                if mlp:
                    finish_link(dve.tensor_copy(pst[:, RSTD, which, 0:G], st[:, ROOT, which, :]))
                    if h_too:
                        dve.tensor_tensor(tiled(d[:, b, :], G), tiled(d[:, b, :], G), by(RSTD, 0), ALU.mult).then_inc(d_ready, 1)
                else:
                    r, t = st[:, INVERSE, which, :], st[:, TMP, which, :]
                    finish_link(dve.reciprocal(r, st[:, ROOT, which, :]))
                    finish_link(dve.tensor_tensor(t, r, r, ALU.mult))
                    finish_link(dve.tensor_tensor(t, t, st[:, NEGHALF, which, :], ALU.mult))
                    if h_too:
                        dve.scalar_tensor_tensor(rstd[:, :], st[:, TMP, 0, :], 1.5, st[:, INVERSE, 0, :], ALU.add, ALU.mult)
                    if not update:
                        if not first(it, 4):
                            wake(dve, y_ready, it - 3, w_dve)
                        dve.scalar_tensor_tensor(rstd_z[:, b, :], st[:, TMP, 1, :], 1.5, st[:, INVERSE, 1, :], ALU.add, ALU.mult).then_inc(rstd_ready, 1)
                        return
                    finish_link(dve.scalar_tensor_tensor(pst[:, RSTD, 1, 0:G], st[:, TMP, 1, :], 1.5, st[:, INVERSE, 1, :], ALU.add, ALU.mult))
                    if h_too:
                        if not first(it, 2):
                            wake(dve, z_ready, it - 1, w_dve)
                        dve.tensor_tensor(tiled(d[:, b, :], G), tiled(pO[b][:, :], G), over_tiles(rstd[:, :], H, G), ALU.mult).then_inc(d_ready, 1)
                        wake(dve, xb_ready, it + 1, w_dve)
                        dve.tensor_tensor(xh[:, b, :], pO[b][:, :], xb[:, b, :], ALU.add).then_inc(xh_ready, 1)
                if not first(it, 2):
                    dve.tensor_tensor(y[:, b, :, YC], y[:, b, :, YC], by(RSTD, 1), ALU.mult).then_inc(y_ready, 1)

            for it, b, k, xbuf, xk in phases(dve):
                link.start(it)
                h_too = update and not tail(it)
                z_too = not first(it, 2)
                if h_too and mlp:
                    wake(dve, load[xbuf], (xk + 1) * LOADS, w_dve)
                    dve.tensor_copy(slot_rows[:, xbuf, :], xa[:, xbuf, :, RC])
                    for half in range(2):
                        n = slice(half * (G // 2), (half + 1) * (G // 2))
                        wake(dve, silu, it * 2 + (half + 1), w_dve)
                        dve.tensor_tensor(tiled(h[:, b, :], G)[:, n, :], tiled(pS[:, :], G // 2), xa[:, xbuf, n, XC], ALU.add).then_inc(h_ready, 1)
                if not first(it, 1):
                    finish(it - 1, 1 - b)
                if z_too:
                    wake(dve, z_ready, it - 1, w_dve)
                    if attend:
                        wake(dve, z_rest, it - 1, w_dve)
                    last = row_stat(SUM, 1, z[:, b, :])
                if h_too and mlp:
                    wake(dve, h_ready, it * 2 + 2, w_dve)
                    last = row_stat(SUM, 0, h[:, b, :])
                if z_too:
                    wake(dve, z_squared, it - 1, w_dve)
                    last = row_stat(SQUARES, 1, zsq[:, :])
                if h_too:
                    wake(dve, hsqd, it + 1, w_dve)
                    last = row_stat(SQUARES, 0, hsq[:, :])
                if not h_too and not z_too:
                    last = dve.memset(st[:, SUM, 1, :], 0.0)
                link(last)
                variance()
                if z_too:
                    if not first(it, 4):
                        wake(dve, store[b], (k - 1) * 16, w_dve)
                    if mlp:
                        dve.tensor_copy(y[:, b, :, 0], slot_rows[:, (xbuf + 2) % XB, :])
                    dve.tensor_tensor(y[:, b, :, YC], tiled(z[:, b, :], G), by(MEAN, 1), ALU.subtract).then_inc(z_used, 1)
                if attend and not first(it, 1) and not (tail(it) and it > STEPS):
                    wake(dve, u_ready, it, w_dve)
                    wake(dve, xh_ready, it, w_dve)
                    if not first(it, 3):
                        wake(dve, z_used, it - 2, w_dve)
                    n = slice(POOL_NODES * H, DW)
                    dve.tensor_tensor(z[:, 1 - b, n], u[:, n], xh[:, 1 - b, n], ALU.add).then_inc(z_rest, 1)
                if h_too and mlp:
                    if not first(it, 2):
                        wake(dve, z_ready, it - 1, w_dve)
                    dve.tensor_tensor(tiled(d[:, b, :], G), tiled(h[:, b, :], G), by(MEAN, 0), ALU.subtract)
            finish(STEPS + 1, 1)


def program(nc, inputs, out):
    g = {"in": inputs}
    with ExitStack() as ctx:
        sb, ps, sem = scope(nc, ctx)
        for name, shape in (("ident", [P, P]), ("w_msg1", [2 * H, H]), ("w_msg1e", [ED, H]), ("w_msg2", [H, H]),
                            ("w_upd1", [2 * H, H]), ("w_upd2", [H + 1, H]), ("w_out", [2 * H, H]), ("w_conv0", [H, H]),
                            ("w_conv1", [H, H]), ("w_conv2", [H, H]), ("wq", [P, H]), ("wk", [P, H]), ("wv", [P, H]),
                            ("head_sum", [H, P]), ("norm_src", [P, TILES]), ("norm_dst", [P, TILES])):
            g[name] = sb(name, shape)
        for name in ("b_msg1", "b_msg2", "b_upd1", "b_q", "b_k", "b_v"):
            g[name] = sb(name, [H, 1])
        for name in ("r_g", "r_b", "r_gamma", "r_beta", "r_bf", "r_bo", "r_c0", "r_c1", "r_c2"):
            g[name] = sb(name, [P, H])
        for name in ("edge_id", "scat_dst", "dst_id", "edge_id2", "scat_src", "slot_row", "scat_dst_agg", "dst_x", "src_x"):
            g[name] = sb(name, [P, COLS], I32)
        g["record"] = sb("record_of_slot", [P, COLS, ED + 1], I32)
        g["src_row"] = sb("src_row", [P, COLS], I32)
        g["dst_id2"] = sb("dst_id2", [P, COLS], I32)
        dram = lambda name, shape, dt=F32: nc.dram_tensor(name, shape, dt, kind="Internal").ap()
        g["words"] = dram("sort_words", (2, SLOTS + 8), I32)
        g["keep"] = dram("keep", (2, SLOTS + 8))
        g["records"] = dram("records", (E, ED + 1), I32)
        for name in ("A2", "A3", "X2", "X3"):
            g[name] = dram(name, (N, H))
        for name in ("XA0", "XA1"):
            g[name] = dram(name, (N, 2 * W))
        for name in ("H1", "H2"):
            g[name] = dram(name, (ROWS + 1, H))

        sort_edges(nc, g)
        fetch_records(nc, g)
        messages(nc, g)
        dense(nc, g, "mlp", g["XA0"], None, g["XA1"])
        attention(nc, g)
        dense(nc, g, "attend", g["XA1"], None, g["X2"], gather=(inputs["dst"], g["edge_id2"], g["dst_id2"]))
        spread(nc, g, g["X2"], g["dst_id2"], 1, scatter_to=g["A2"], scatter_ix=g["scat_src"])
        dense(nc, g, "add", g["X2"], g["A2"], g["X3"])
        spread(nc, g, g["X3"], g["record"][:, :, ED], 0, g["w_conv0"], g["r_c0"], relu=True, rows_to=g["H1"])
        spread(nc, g, g["H1"], g["src_row"], 0, g["w_conv1"], g["r_c1"], relu=True, rows_to=g["H2"])
        spread(nc, g, g["H2"], g["src_row"], 0, g["w_conv2"], g["r_c2"], scatter_to=g["A3"], scatter_ix=g["scat_dst"])
        dense(nc, g, "add", g["X3"], g["A3"], out)


def kernel(**inputs):
    import numpy as np
    import concourse.bacc as bacc
    from concourse.bass_utils import run_bass_kernel_spmd as run

    nc = bacc.Bacc("TRN2", target_bir_lowering=False, num_devices=1)
    slot = np.arange(SLOTS).reshape(P, SW)
    bit = lambda k: 1.0 - 2.0 * ((slot >> k) & 1)
    signs = np.stack([bit(k) * (bit(k - 1) if k > 1 else 1.0) for k in range(1, LOGS + 1)], 1)
    head = np.arange(H) // HD
    head_sum = (head[:, None] == head[None, :]) / float(np.sqrt(H))
    arrays = {n: np.asarray(a) for n, a in inputs.items()}
    for n in ("src", "dst"):
        arrays[n] = arrays[n].reshape(E, 1)
    arrays["x_norm"] = np.concatenate([arrays["x"], arrays.pop("node_vec").reshape(N, 1)], axis=1)
    arrays["signs"] = signs.reshape(P, LOGS * SW).astype(np.float32)
    arrays["eye"] = np.eye(P, dtype=np.float32)
    arrays["head_sum"] = np.concatenate([head_sum, head_sum], axis=1).astype(np.float32)
    aps = {n: nc.dram_tensor("in_" + n, a.shape, mybir.dt.from_np(a.dtype), kind="ExternalInput").ap() for n, a in arrays.items()}
    out = nc.dram_tensor("out", (N, H), F32, kind="ExternalOutput").ap()
    program(nc, aps, out)
    r = run(nc, [{"in_" + n: a for n, a in arrays.items()}], core_ids=[0])
    return r.results[0]["out"]
```
